# Optimizing a Trainium2 kernel written in Bass

```python
import numpy as np
import jax
import jax.numpy as jnp

def _softmax(x, axis=-1):
    return jax.nn.softmax(x, axis=axis)

def _gelu(x):
    return jax.nn.gelu(x, approximate=True)

def _silu(x):
    return jax.nn.silu(x)

def _sigmoid(x):
    return jax.nn.sigmoid(x)

def _layernorm(x, axis=-1, eps=1e-05):
    m = jnp.mean(x, axis=axis, keepdims=True)
    v = jnp.var(x, axis=axis, keepdims=True)
    return (x - m) / jnp.sqrt(v + eps)

def _scatter_add(tgt, idx, src, axis=0):
    return tgt.at[idx].add(src)

def _segment_sum(src, seg, n):
    return jax.ops.segment_sum(src, seg, n)
kernel_name = 'mk_xattn_ffn_d4_seqx_r8_81bec6'

def setup_inputs(seed: int=0):
    np.random.seed(seed)
    _w = jnp.asarray

    def _rec_inputs():
        import jax
        import jax.numpy as jnp
        _rk = jax.random.key(seed)
        x = -0.0002928 + 1 * jax.random.normal(jax.random.fold_in(_rk, 1), (32, 128, 128), jnp.float32)
        _lenS = 128 - jax.random.randint(jax.random.fold_in(_rk, 7), (32,), 0, max(1, 128 // 4) + 1, jnp.int32)
        _lenS2 = 128 - jax.random.randint(jax.random.fold_in(_rk, 8), (32,), 0, max(1, 128 // 4) + 1, jnp.int32)
        _ctx_1024P = jax.random.normal(jax.random.fold_in(_rk, 11), (32, 16, 128), jnp.float32)
        _ctx_1024c = jax.random.dirichlet(jax.random.fold_in(_rk, 511), 0.3 * jnp.ones((16,), jnp.float32), (32, 128))
        _ctx_1024t = jnp.einsum('bsk,bkd->bsd', _ctx_1024c, _ctx_1024P)
        _ctx_1024t = _ctx_1024t * jax.lax.rsqrt(jnp.mean(jnp.square(_ctx_1024t)) + 1e-12) * 0.953939
        ctx_1024 = -1.39393e-06 + 0.999914 * (_ctx_1024t + 0.3 * jax.random.normal(jax.random.fold_in(_rk, 611), (32, 128, 128), jnp.float32))
        fside_Bx16_0 = 0.119436 + 0.907674 * jax.random.normal(jax.random.fold_in(_rk, 13), (32, 16), jnp.float32)
        _validS = jnp.arange(128)[None, :] < _lenS[:, None]
        _validS2 = jnp.arange(128)[None, :] < _lenS2[:, None]
        _causal = jnp.tril(jnp.ones((128, 128), dtype=bool))
        mask_BxS2_if0 = jnp.where(jnp.ones((32, 128), dtype=bool), 0, 1).astype(jnp.int32)
        return (x, ctx_1024, fside_Bx16_0, mask_BxS2_if0)
    x, ctx_1024, fside_Bx16_0, mask_BxS2_if0 = _rec_inputs()

    def _L0_xattn_setup():
        import jax, jax.numpy as jnp
        import numpy as np
        D_MODEL = 128
        N_HEAD = 16
        D_HEAD = D_MODEL // N_HEAD
        key = jax.random.key(seed)
        ks = jax.random.split(key, 11)
        B, S = (2, 256)
        scale = 1.0 / np.sqrt(D_MODEL)
        inp = {'q': jax.random.normal(ks[0], (B, S, D_MODEL), jnp.float32), 'k': jax.random.normal(ks[1], (B, S, D_MODEL), jnp.float32), 'v': jax.random.normal(ks[2], (B, S, D_MODEL), jnp.float32), 'w_q': jax.random.normal(ks[3], (D_MODEL, D_MODEL), jnp.float32) * scale, 'b_q': jnp.zeros((D_MODEL,), jnp.float32), 'w_k': jax.random.normal(ks[4], (D_MODEL, D_MODEL), jnp.float32) * scale, 'b_k': jnp.zeros((D_MODEL,), jnp.float32), 'w_v': jax.random.normal(ks[5], (D_MODEL, D_MODEL), jnp.float32) * scale, 'b_v': jnp.zeros((D_MODEL,), jnp.float32), 'w_out': jax.random.normal(ks[6], (D_MODEL, D_MODEL), jnp.float32) * scale, 'b_out': jnp.zeros((D_MODEL,), jnp.float32)}
        return inp
    _L0_xattn_all = _L0_xattn_setup()
    _L0_xattn_in = {k: v for k, v in _L0_xattn_all.items() if k in ('w_q', 'b_q', 'w_k', 'b_k', 'w_v', 'b_v', 'w_out', 'b_out')}
    del _L0_xattn_all

    def _L0_ffn_setup():
        import jax, jax.numpy as jnp
        import numpy as np
        B, N, D = (4, 256, 128)
        SPARSITY = 0.01
        key = jax.random.key(seed)
        k1, k2, k3 = jax.random.split(key, 3)
        x = jax.random.normal(k1, (B, N, D), dtype=jnp.float32)
        spatial = jax.random.normal(k2, (D, D), dtype=jnp.float32) * 0.02
        freq = jnp.fft.fft(spatial, axis=-1)
        k = int(D * SPARSITY)
        mag = jnp.abs(freq)
        kth = jax.lax.top_k(mag, k)[0][:, -1:]
        w_sparse = jnp.where(mag >= kth, freq, 0.0 + 0j)
        bias = jax.random.normal(k3, (D,), dtype=jnp.float32) * 0.01
        return {'x': x, 'w_freq_real': jnp.real(w_sparse).astype(jnp.float32), 'w_freq_imag': jnp.imag(w_sparse).astype(jnp.float32), 'bias': bias}
    _L0_ffn_all = _L0_ffn_setup()
    _L0_ffn_in = {k: v for k, v in _L0_ffn_all.items() if k in ('w_freq_real', 'w_freq_imag', 'bias')}
    del _L0_ffn_all

    def _L1_xattn_setup():
        import jax, jax.numpy as jnp
        import numpy as np
        import math
        B, M, D, H, NK = (4, 256, 128, 16, 5)
        HD = D // H

        def _gather_pad0(x, idx):
            Bx, Hx, W, hd = x.shape
            valid = (idx >= 0) & (idx < W)
            idxc = jnp.clip(idx, 0, W - 1).reshape(Bx, Hx, -1)
            g = jnp.take_along_axis(x, idxc[..., None], axis=2)
            g = g.reshape(idx.shape + (hd,))
            return g * valid[..., None].astype(x.dtype)
        key = jax.random.key(seed)
        ks = jax.random.split(key, 9)
        w = lambda k, shape: jax.random.normal(k, shape, jnp.float32) * 0.02
        return {'k': jax.random.normal(ks[0], (B, M, D), jnp.float32), 'v': jax.random.normal(ks[1], (B, M, D), jnp.float32), 'q': jax.random.normal(ks[2], (B, M, D), jnp.float32), 'mask': jnp.zeros((B, M), jnp.int32), 'Wk': w(ks[3], (D, D)), 'bk': jnp.zeros((D,), jnp.float32), 'Wv': w(ks[4], (D, D)), 'bv': jnp.zeros((D,), jnp.float32), 'Wq': w(ks[5], (D, D)), 'bq': jnp.zeros((D,), jnp.float32), 'Woff': w(ks[6], (H * NK, D)), 'boff': jnp.zeros((H * NK,), jnp.float32), 'Wo': w(ks[7], (D, D)), 'bo': jnp.zeros((D,), jnp.float32)}
    _L1_xattn_all = _L1_xattn_setup()
    _L1_xattn_in = {k: v for k, v in _L1_xattn_all.items() if k in ('Wk', 'bk', 'Wv', 'bv', 'Wq', 'bq', 'Woff', 'boff', 'Wo', 'bo')}
    del _L1_xattn_all

    def _L1_ffn_setup():
        import jax, jax.numpy as jnp
        import numpy as np
        B, T, D = (4, 512, 128)
        E = 8
        TOP_K = 2
        FFN = 384
        HALF = FFN // 2

        def _kaiming_uniform(key, shape, fan_in):
            bound = 1.0 / np.sqrt(fan_in)
            return jax.random.uniform(key, shape, jnp.float32, -bound, bound)
        key = jax.random.key(seed)
        ks = jax.random.split(key, 7)
        x = jax.random.normal(ks[0], (B, T, D), jnp.float32)
        gate_w = _kaiming_uniform(ks[1], (E, D), D) * 0.01
        w_up = _kaiming_uniform(ks[2], (E, FFN, D), D)
        w_down = _kaiming_uniform(ks[3], (E, D, HALF), HALF)
        sg_gate = _kaiming_uniform(ks[4], (HALF, D), D)
        sg_up = _kaiming_uniform(ks[5], (HALF, D), D)
        sg_down = _kaiming_uniform(ks[6], (D, HALF), HALF)
        return {'x': x, 'gate_w': gate_w, 'w_up': w_up, 'w_down': w_down, 'sg_gate': sg_gate, 'sg_up': sg_up, 'sg_down': sg_down}
    _L1_ffn_all = _L1_ffn_setup()
    _L1_ffn_in = {k: v for k, v in _L1_ffn_all.items() if k in ('gate_w', 'w_up', 'w_down', 'sg_gate', 'sg_up', 'sg_down')}
    del _L1_ffn_all

    def _L2_xattn_setup():
        import jax, jax.numpy as jnp
        import numpy as np
        DIM = 128
        HEADS = 16
        DIM_HEAD = 64
        INNER = HEADS * DIM_HEAD
        EPS = 1e-05

        def layernorm(x, w, b):
            mu = jnp.mean(x, axis=-1, keepdims=True)
            var = jnp.mean(jnp.square(x - mu), axis=-1, keepdims=True)
            return (x - mu) * jax.lax.rsqrt(var + EPS) * w + b
        key = jax.random.key(seed)
        ks = jax.random.split(key, 9)
        b, n1, n2 = (4, 512, 32)
        x = jax.random.normal(ks[0], (b, n1, DIM), dtype=jnp.float32)
        latents = jax.random.normal(ks[1], (b, n2, DIM), dtype=jnp.float32)
        shift = jax.random.normal(ks[2], (b, HEADS), dtype=jnp.float32)
        scale = jax.random.normal(ks[3], (b, HEADS), dtype=jnp.float32)
        s = 1.0 / np.sqrt(DIM)
        Wq = jax.random.normal(ks[4], (DIM, INNER), dtype=jnp.float32) * s
        Wkv = jax.random.normal(ks[5], (DIM, 2 * INNER), dtype=jnp.float32) * s
        Wout = jax.random.normal(ks[6], (INNER, DIM), dtype=jnp.float32) * (1.0 / np.sqrt(INNER))
        ln1_w = jnp.ones((DIM,), jnp.float32)
        ln1_b = jnp.zeros((DIM,), jnp.float32)
        ln2_w = jnp.ones((DIM,), jnp.float32)
        ln2_b = jnp.zeros((DIM,), jnp.float32)
        return {'x': x, 'latents': latents, 'shift': shift, 'scale': scale, 'ln1_w': ln1_w, 'ln1_b': ln1_b, 'ln2_w': ln2_w, 'ln2_b': ln2_b, 'Wq': Wq, 'Wkv': Wkv, 'Wout': Wout}
    _L2_xattn_all = _L2_xattn_setup()
    _L2_xattn_in = {k: v for k, v in _L2_xattn_all.items() if k in ('ln1_w', 'ln1_b', 'ln2_w', 'ln2_b', 'Wq', 'Wkv', 'Wout')}
    del _L2_xattn_all

    def _L2_ffn_setup():
        import jax, jax.numpy as jnp
        import numpy as np
        B, S, DIM, FFN, E = (4, 256, 128, 512, 8)
        key = jax.random.key(seed)
        k0, k1, k2, k3 = jax.random.split(key, 4)
        scale = 0.02
        return {'hidden_states': jax.random.normal(k0, (B, S, DIM), jnp.float32), 'router_w': jax.random.normal(k1, (DIM, E), jnp.float32) * scale, 'router_b': jnp.zeros((E,), jnp.float32), 'w1': jax.random.normal(k2, (E, DIM, 2 * FFN), jnp.float32) * scale, 'w2': jax.random.normal(k3, (E, FFN, DIM), jnp.float32) * scale}
    _L2_ffn_all = _L2_ffn_setup()
    _L2_ffn_in = {k: v for k, v in _L2_ffn_all.items() if k in ('router_w', 'router_b', 'w1', 'w2')}
    del _L2_ffn_all

    def _L3_xattn_setup():
        import jax, jax.numpy as jnp
        import numpy as np
        B, LQ, ND, D = (4, 128, 512, 128)
        key = jax.random.key(seed)
        k1, k2, k3, k4, k5, k6 = jax.random.split(key, 6)
        s = 1.0 / np.sqrt(D)
        return {'query': jax.random.normal(k1, (B, LQ, D), dtype=jnp.float32), 'documents': jax.random.normal(k2, (B, ND, D), dtype=jnp.float32), 'Wq': jax.random.uniform(k3, (D, D), dtype=jnp.float32, minval=-s, maxval=s), 'bq': jax.random.uniform(k4, (D,), dtype=jnp.float32, minval=-s, maxval=s), 'Wk': jax.random.uniform(k5, (D, D), dtype=jnp.float32, minval=-s, maxval=s), 'bk': jax.random.uniform(k6, (D,), dtype=jnp.float32, minval=-s, maxval=s)}
    _L3_xattn_all = _L3_xattn_setup()
    _L3_xattn_in = {k: v for k, v in _L3_xattn_all.items() if k in ('Wq', 'bq', 'Wk', 'bk')}
    del _L3_xattn_all

    def _L3_ffn_setup():
        import jax, jax.numpy as jnp
        import numpy as np
        H = 128
        I = 88
        E = 64
        TOP_K = 8
        NG = 8
        TOPK_GROUP = 4
        N_SHARED = 2
        ROUTED_SCALE = 2.5
        S_I = I * N_SHARED

        def _route(x, gate_w, gate_bias):
            T = x.shape[0]
            logits = x @ gate_w.T
            scores = jax.nn.sigmoid(logits)
            scores_for_choice = scores + gate_bias[None, :]
            grp = scores_for_choice.reshape(T, NG, E // NG)
            group_scores = jnp.sum(jax.lax.top_k(grp, 2)[0], axis=-1)
            _, gidx = jax.lax.top_k(group_scores, TOPK_GROUP)
            gmask = jnp.zeros((T, NG), dtype=scores.dtype).at[jnp.arange(T)[:, None], gidx].set(1.0)
            emask = jnp.repeat(gmask, E // NG, axis=1)
            masked = jnp.where(emask > 0, scores_for_choice, 0.0)
            _, topk_idx = jax.lax.top_k(masked, TOP_K)
            topk_w = jnp.take_along_axis(scores, topk_idx, axis=1)
            topk_w = topk_w / (jnp.sum(topk_w, axis=-1, keepdims=True) + 1e-20)
            topk_w = topk_w * ROUTED_SCALE
            rw = jnp.zeros((T, E), dtype=scores.dtype).at[jnp.arange(T)[:, None], topk_idx].add(topk_w)
            return rw

        def _mlp(x, gw, uw, dw):
            return jax.nn.silu(x @ gw.T) * (x @ uw.T) @ dw.T
        key = jax.random.key(seed)
        ks = jax.random.split(key, 10)
        sc = 0.02
        return {'hidden_states': jax.random.normal(ks[0], (1, 128, H), dtype=jnp.float32), 'gate_w': sc * jax.random.normal(ks[1], (E, H), dtype=jnp.float32), 'gate_bias': sc * jax.random.normal(ks[2], (E,), dtype=jnp.float32), 'Wg': sc * jax.random.normal(ks[3], (E, I, H), dtype=jnp.float32), 'Wu': sc * jax.random.normal(ks[4], (E, I, H), dtype=jnp.float32), 'Wd': sc * jax.random.normal(ks[5], (E, H, I), dtype=jnp.float32), 'Sg': sc * jax.random.normal(ks[6], (S_I, H), dtype=jnp.float32), 'Su': sc * jax.random.normal(ks[7], (S_I, H), dtype=jnp.float32), 'Sd': sc * jax.random.normal(ks[8], (H, S_I), dtype=jnp.float32)}
    _L3_ffn_all = _L3_ffn_setup()
    _L3_ffn_in = {k: v for k, v in _L3_ffn_all.items() if k in ('gate_w', 'gate_bias', 'Wg', 'Wu', 'Wd', 'Sg', 'Su', 'Sd')}
    del _L3_ffn_all
    return {'x': x, 'ctx_1024': ctx_1024, 'fside_Bx16_0': fside_Bx16_0, 'mask_BxS2_if0': mask_BxS2_if0, 'L0_xattn_w_q': _L0_xattn_in['w_q'], 'L0_xattn_b_q': _L0_xattn_in['b_q'], 'L0_xattn_w_k': _L0_xattn_in['w_k'], 'L0_xattn_b_k': _L0_xattn_in['b_k'], 'L0_xattn_w_v': _L0_xattn_in['w_v'], 'L0_xattn_b_v': _L0_xattn_in['b_v'], 'L0_xattn_w_out': _L0_xattn_in['w_out'], 'L0_xattn_b_out': _L0_xattn_in['b_out'], 'L0_ffn_w_freq_real': _L0_ffn_in['w_freq_real'], 'L0_ffn_w_freq_imag': _L0_ffn_in['w_freq_imag'], 'L0_ffn_bias': _L0_ffn_in['bias'], 'L1_xattn_Wk': _L1_xattn_in['Wk'], 'L1_xattn_bk': _L1_xattn_in['bk'], 'L1_xattn_Wv': _L1_xattn_in['Wv'], 'L1_xattn_bv': _L1_xattn_in['bv'], 'L1_xattn_Wq': _L1_xattn_in['Wq'], 'L1_xattn_bq': _L1_xattn_in['bq'], 'L1_xattn_Woff': _L1_xattn_in['Woff'], 'L1_xattn_boff': _L1_xattn_in['boff'], 'L1_xattn_Wo': _L1_xattn_in['Wo'], 'L1_xattn_bo': _L1_xattn_in['bo'], 'L1_ffn_gate_w': _L1_ffn_in['gate_w'], 'L1_ffn_w_up': _L1_ffn_in['w_up'], 'L1_ffn_w_down': _L1_ffn_in['w_down'], 'L1_ffn_sg_gate': _L1_ffn_in['sg_gate'], 'L1_ffn_sg_up': _L1_ffn_in['sg_up'], 'L1_ffn_sg_down': _L1_ffn_in['sg_down'], 'L2_xattn_ln1_w': _L2_xattn_in['ln1_w'], 'L2_xattn_ln1_b': _L2_xattn_in['ln1_b'], 'L2_xattn_ln2_w': _L2_xattn_in['ln2_w'], 'L2_xattn_ln2_b': _L2_xattn_in['ln2_b'], 'L2_xattn_Wq': _L2_xattn_in['Wq'], 'L2_xattn_Wkv': _L2_xattn_in['Wkv'], 'L2_xattn_Wout': _L2_xattn_in['Wout'], 'L2_ffn_router_w': _L2_ffn_in['router_w'], 'L2_ffn_router_b': _L2_ffn_in['router_b'], 'L2_ffn_w1': _L2_ffn_in['w1'], 'L2_ffn_w2': _L2_ffn_in['w2'], 'L3_xattn_Wq': _L3_xattn_in['Wq'], 'L3_xattn_bq': _L3_xattn_in['bq'], 'L3_xattn_Wk': _L3_xattn_in['Wk'], 'L3_xattn_bk': _L3_xattn_in['bk'], 'L3_ffn_gate_w': _L3_ffn_in['gate_w'], 'L3_ffn_gate_bias': _L3_ffn_in['gate_bias'], 'L3_ffn_Wg': _L3_ffn_in['Wg'], 'L3_ffn_Wu': _L3_ffn_in['Wu'], 'L3_ffn_Wd': _L3_ffn_in['Wd'], 'L3_ffn_Sg': _L3_ffn_in['Sg'], 'L3_ffn_Su': _L3_ffn_in['Su'], 'L3_ffn_Sd': _L3_ffn_in['Sd']}

def reference(x, ctx_1024, fside_Bx16_0, mask_BxS2_if0, L0_xattn_w_q, L0_xattn_b_q, L0_xattn_w_k, L0_xattn_b_k, L0_xattn_w_v, L0_xattn_b_v, L0_xattn_w_out, L0_xattn_b_out, L0_ffn_w_freq_real, L0_ffn_w_freq_imag, L0_ffn_bias, L1_xattn_Wk, L1_xattn_bk, L1_xattn_Wv, L1_xattn_bv, L1_xattn_Wq, L1_xattn_bq, L1_xattn_Woff, L1_xattn_boff, L1_xattn_Wo, L1_xattn_bo, L1_ffn_gate_w, L1_ffn_w_up, L1_ffn_w_down, L1_ffn_sg_gate, L1_ffn_sg_up, L1_ffn_sg_down, L2_xattn_ln1_w, L2_xattn_ln1_b, L2_xattn_ln2_w, L2_xattn_ln2_b, L2_xattn_Wq, L2_xattn_Wkv, L2_xattn_Wout, L2_ffn_router_w, L2_ffn_router_b, L2_ffn_w1, L2_ffn_w2, L3_xattn_Wq, L3_xattn_bq, L3_xattn_Wk, L3_xattn_bk, L3_ffn_gate_w, L3_ffn_gate_bias, L3_ffn_Wg, L3_ffn_Wu, L3_ffn_Wd, L3_ffn_Sg, L3_ffn_Su, L3_ffn_Sd):
    import jax
    import jax.numpy as jnp

    def _L0_xattn_ref(q, k, v, w_q, b_q, w_k, b_k, w_v, b_v, w_out, b_out):
        import jax, jax.numpy as jnp
        import numpy as np
        D_MODEL = 128
        N_HEAD = 16
        D_HEAD = D_MODEL // N_HEAD
        B, S, _ = q.shape
        qh = (q @ w_q.T + b_q).reshape(B, S, N_HEAD, D_HEAD)
        kh = (k @ w_k.T + b_k).reshape(B, S, N_HEAD, D_HEAD)
        vh = (v @ w_v.T + b_v).reshape(B, S, N_HEAD, D_HEAD)
        scores = jnp.einsum('bqhd,bkhd->bhqk', qh, kh) / jnp.sqrt(jnp.asarray(D_HEAD, qh.dtype))
        attn = jax.nn.softmax(scores, axis=-1)
        out = jnp.einsum('bhqk,bkhd->bqhd', attn, vh).reshape(B, S, D_MODEL)
        return out @ w_out.T + b_out

    def _L0_ffn_ref(x, w_freq_real, w_freq_imag, bias):
        import jax, jax.numpy as jnp
        import numpy as np
        B, N, D = (4, 256, 128)
        SPARSITY = 0.01
        w = jax.lax.complex(w_freq_real, w_freq_imag)
        x_freq = jnp.fft.fft(x, axis=-1)
        y_freq = jnp.einsum('bnd,do->bno', x_freq, w)
        y = jnp.real(jnp.fft.ifft(y_freq, axis=-1))
        return y + bias

    def _L1_xattn_ref(k, v, q, mask, Wk, bk, Wv, bv, Wq, bq, Woff, boff, Wo, bo):
        import jax, jax.numpy as jnp
        import numpy as np
        import math
        B, M, D, H, NK = (4, 256, 128, 16, 5)
        HD = D // H

        def _gather_pad0(x, idx):
            Bx, Hx, W, hd = x.shape
            valid = (idx >= 0) & (idx < W)
            idxc = jnp.clip(idx, 0, W - 1).reshape(Bx, Hx, -1)
            g = jnp.take_along_axis(x, idxc[..., None], axis=2)
            g = g.reshape(idx.shape + (hd,))
            return g * valid[..., None].astype(x.dtype)
        Bq, Q, _ = q.shape
        key_len = k.shape[1]
        K = jnp.einsum('bmd,ed->bme', k, Wk) + bk
        V = jnp.einsum('bmd,ed->bme', v, Wv) + bv
        Qp = jnp.einsum('bqd,ed->bqe', q, Wq) + bq
        off = jnp.einsum('bqd,ed->bqe', Qp, Woff) + boff
        off = off.reshape(Bq, Q, H, NK).transpose(0, 2, 1, 3)
        Kh = K.reshape(Bq, key_len, H, HD).transpose(0, 2, 1, 3)
        Vh = V.reshape(Bq, key_len, H, HD).transpose(0, 2, 1, 3)
        Qh = Qp.reshape(Bq, Q, H, HD).transpose(0, 2, 1, 3)
        loc = jnp.arange(Q, dtype=jnp.float32)[:, None]
        left = -NK // 2
        ref = jnp.arange(left, NK + left, dtype=jnp.float32)
        sign_lens = (1 - mask).sum(-1).astype(jnp.float32) - 1.0
        loc_x = jnp.mod(ref + off + loc, sign_lens[:, None, None, None])
        xg = loc_x / (key_len - 1) * 2.0 - 1.0
        ix = ((xg + 1.0) * key_len - 1.0) / 2.0
        x0 = jnp.floor(ix)
        dx = ix - x0
        i0 = x0.astype(jnp.int32)
        i1 = i0 + 1
        w0 = (1.0 - dx)[..., None]
        w1 = dx[..., None]
        sk = 0.5 * (w0 * _gather_pad0(Kh, i0) + w1 * _gather_pad0(Kh, i1))
        sv = 0.5 * (w0 * _gather_pad0(Vh, i0) + w1 * _gather_pad0(Vh, i1))
        scores = jnp.einsum('bhqd,bhqkd->bhqk', Qh / math.sqrt(HD), sk)
        attn = jax.nn.softmax(scores, axis=-1)
        ctx = jnp.einsum('bhqk,bhqkd->bhqd', attn, sv)
        ctx = ctx.transpose(0, 2, 1, 3).reshape(Bq, Q, H * HD)
        return jnp.einsum('bqd,ed->bqe', ctx, Wo) + bo

    def _L1_ffn_ref(x, gate_w, w_up, w_down, sg_gate, sg_up, sg_down):
        import jax, jax.numpy as jnp
        import numpy as np
        B, T, D = (4, 512, 128)
        E = 8
        TOP_K = 2
        FFN = 384
        HALF = FFN // 2

        def _kaiming_uniform(key, shape, fan_in):
            bound = 1.0 / np.sqrt(fan_in)
            return jax.random.uniform(key, shape, jnp.float32, -bound, bound)
        b, t, d = x.shape
        xf = x.reshape(b * t, d)
        N = xf.shape[0]
        logits = xf @ gate_w.T
        topk_logits, topk_idx = jax.lax.top_k(logits, TOP_K)
        topk_w = jax.nn.softmax(topk_logits.astype(jnp.float32), axis=-1).astype(x.dtype)
        comb = jnp.zeros((N, E), x.dtype).at[jnp.arange(N)[:, None], topk_idx].add(topk_w)
        wg = w_up[:, :HALF, :]
        wu = w_up[:, HALF:, :]
        out = jnp.zeros_like(xf)
        for e in range(E):
            g = xf @ wg[e].T
            u = xf @ wu[e].T
            y = jax.nn.silu(g) * u @ w_down[e].T
            out = out + comb[:, e:e + 1] * y
        shared = jax.nn.silu(xf @ sg_gate.T) * (xf @ sg_up.T) @ sg_down.T
        return (shared + out).reshape(b, t, d)

    def _L2_xattn_ref(x, latents, shift, scale, ln1_w, ln1_b, ln2_w, ln2_b, Wq, Wkv, Wout):
        import jax, jax.numpy as jnp
        import numpy as np
        DIM = 128
        HEADS = 16
        DIM_HEAD = 64
        INNER = HEADS * DIM_HEAD
        EPS = 1e-05

        def layernorm(x, w, b):
            mu = jnp.mean(x, axis=-1, keepdims=True)
            var = jnp.mean(jnp.square(x - mu), axis=-1, keepdims=True)
            return (x - mu) * jax.lax.rsqrt(var + EPS) * w + b
        b = x.shape[0]
        xn = layernorm(x, ln1_w, ln1_b)
        ln = layernorm(latents, ln2_w, ln2_b)
        q = ln @ Wq
        kv = xn @ Wkv
        k, v = jnp.split(kv, 2, axis=-1)
        q = q.reshape(b, -1, HEADS, DIM_HEAD)
        k = k.reshape(b, -1, HEADS, DIM_HEAD)
        v = v.reshape(b, -1, HEADS, DIM_HEAD)
        q = q * (1.0 + scale[:, None, :, None]) + shift[:, None, :, None]
        attn_scale = DIM_HEAD ** (-0.5)
        qk = jnp.einsum('bihd,bjhd->bhij', q.astype(jnp.float32), k.astype(jnp.float32)) * attn_scale
        attn = jax.nn.softmax(qk, axis=-1).astype(v.dtype)
        out = jnp.einsum('bhij,bjhd->bihd', attn, v)
        out = out.reshape(b, -1, INNER)
        return out @ Wout

    def _L2_ffn_ref(hidden_states, router_w, router_b, w1, w2):
        import jax, jax.numpy as jnp
        import numpy as np
        B, S, DIM, FFN, E = (4, 256, 128, 512, 8)
        b, s, d = hidden_states.shape
        x = hidden_states.reshape(-1, d)
        logits = x @ router_w + router_b
        route = jax.nn.softmax(logits, axis=1)
        max_prob = jnp.max(route, axis=1, keepdims=True)
        max_ind = jnp.argmax(route, axis=1)
        out = jnp.zeros_like(x)
        num_experts = w1.shape[0]
        for e in range(num_experts):
            h = x @ w1[e]
            a, g = jnp.split(h, 2, axis=1)
            y = jax.nn.silu(a) * g @ w2[e]
            out = jnp.where((max_ind == e)[:, None], y, out)
        out = out * max_prob
        return out.reshape(b, s, d)

    def _L3_xattn_ref(query, documents, Wq, bq, Wk, bk):
        import jax, jax.numpy as jnp
        import numpy as np
        B, LQ, ND, D = (4, 128, 512, 128)
        q = jnp.einsum('bqd,ed->bqe', query, Wq) + bq
        k = jnp.einsum('bnd,ed->bne', documents, Wk) + bk
        scores = jnp.einsum('bqe,bne->bqn', q, k)
        weights = jax.nn.softmax(scores, axis=-1)
        out = jnp.einsum('bqn,bnd->bqd', weights, documents)
        return out

    def _L3_ffn_ref(hidden_states, gate_w, gate_bias, Wg, Wu, Wd, Sg, Su, Sd):
        import jax, jax.numpy as jnp
        import numpy as np
        H = 128
        I = 88
        E = 64
        TOP_K = 8
        NG = 8
        TOPK_GROUP = 4
        N_SHARED = 2
        ROUTED_SCALE = 2.5
        S_I = I * N_SHARED

        def _route(x, gate_w, gate_bias):
            T = x.shape[0]
            logits = x @ gate_w.T
            scores = jax.nn.sigmoid(logits)
            scores_for_choice = scores + gate_bias[None, :]
            grp = scores_for_choice.reshape(T, NG, E // NG)
            group_scores = jnp.sum(jax.lax.top_k(grp, 2)[0], axis=-1)
            _, gidx = jax.lax.top_k(group_scores, TOPK_GROUP)
            gmask = jnp.zeros((T, NG), dtype=scores.dtype).at[jnp.arange(T)[:, None], gidx].set(1.0)
            emask = jnp.repeat(gmask, E // NG, axis=1)
            masked = jnp.where(emask > 0, scores_for_choice, 0.0)
            _, topk_idx = jax.lax.top_k(masked, TOP_K)
            topk_w = jnp.take_along_axis(scores, topk_idx, axis=1)
            topk_w = topk_w / (jnp.sum(topk_w, axis=-1, keepdims=True) + 1e-20)
            topk_w = topk_w * ROUTED_SCALE
            rw = jnp.zeros((T, E), dtype=scores.dtype).at[jnp.arange(T)[:, None], topk_idx].add(topk_w)
            return rw

        def _mlp(x, gw, uw, dw):
            return jax.nn.silu(x @ gw.T) * (x @ uw.T) @ dw.T
        B, S, _ = hidden_states.shape
        x = hidden_states.reshape(B * S, H)
        rw = _route(x, gate_w, gate_bias)
        expert_out = jax.vmap(lambda gw_, uw_, dw_: _mlp(x, gw_, uw_, dw_))(Wg, Wu, Wd)
        routed = jnp.einsum('eth,te->th', expert_out, rw)
        shared = _mlp(x, Sg, Su, Sd)
        out = (routed + shared).reshape(B, S, H)
        return out
    x = x + _L0_xattn_ref(_layernorm(x, axis=-1), ctx_1024, ctx_1024, L0_xattn_w_q, L0_xattn_b_q, L0_xattn_w_k, L0_xattn_b_k, L0_xattn_w_v, L0_xattn_b_v, L0_xattn_w_out, L0_xattn_b_out)
    x = x + _L0_ffn_ref(_layernorm(x, axis=-1), L0_ffn_w_freq_real, L0_ffn_w_freq_imag, L0_ffn_bias)
    x = x + _L1_xattn_ref(ctx_1024, ctx_1024, _layernorm(x, axis=-1), mask_BxS2_if0, L1_xattn_Wk, L1_xattn_bk, L1_xattn_Wv, L1_xattn_bv, L1_xattn_Wq, L1_xattn_bq, L1_xattn_Woff, L1_xattn_boff, L1_xattn_Wo, L1_xattn_bo)
    x = x + _L1_ffn_ref(_layernorm(x, axis=-1), L1_ffn_gate_w, L1_ffn_w_up, L1_ffn_w_down, L1_ffn_sg_gate, L1_ffn_sg_up, L1_ffn_sg_down)
    x = x + _L2_xattn_ref(ctx_1024, _layernorm(x, axis=-1), fside_Bx16_0, fside_Bx16_0, L2_xattn_ln1_w, L2_xattn_ln1_b, L2_xattn_ln2_w, L2_xattn_ln2_b, L2_xattn_Wq, L2_xattn_Wkv, L2_xattn_Wout)
    x = x + _L2_ffn_ref(_layernorm(x, axis=-1), L2_ffn_router_w, L2_ffn_router_b, L2_ffn_w1, L2_ffn_w2)
    x = x + _L3_xattn_ref(_layernorm(x, axis=-1), ctx_1024, L3_xattn_Wq, L3_xattn_bq, L3_xattn_Wk, L3_xattn_bk)
    x = x + _L3_ffn_ref(_layernorm(x, axis=-1), L3_ffn_gate_w, L3_ffn_gate_bias, L3_ffn_Wg, L3_ffn_Wu, L3_ffn_Wd, L3_ffn_Sg, L3_ffn_Su, L3_ffn_Sd)
    return x

_drawn_inputs = setup_inputs


def setup_inputs(seed=0):
    import zlib

    import numpy as np

    out = dict(_drawn_inputs(seed))
    spreads = {'L0_xattn_b_q': (0.0, 0.371),
     'L0_xattn_b_k': (0.0, 0.8),
     'L0_xattn_b_v': (0.0, 0.1),
     'L0_xattn_b_out': (0.0, 0.1),
     'L1_xattn_bk': (0.0, 0.8),
     'L1_xattn_bv': (0.0, 0.735),
     'L1_xattn_bq': (0.0, 0.8),
     'L1_xattn_boff': (0.0, 0.8),
     'L1_xattn_bo': (0.0, 0.1),
     'L2_xattn_ln1_w': (1.0, 0.2),
     'L2_xattn_ln1_b': (0.0, 0.1),
     'L2_xattn_ln2_w': (1.0, 0.2),
     'L2_xattn_ln2_b': (0.0, 0.337),
     'L2_ffn_router_b': (0.0, 0.8)}
    factors = {'L0_ffn_bias': 5.502,
     'L1_xattn_Wk': 8.0,
     'L1_xattn_Wv': 3.841,
     'L1_xattn_Wq': 8.0,
     'L1_xattn_Woff': 8.0,
     'L1_xattn_Wo': 3.228,
     'L2_ffn_router_w': 8.0,
     'L2_ffn_w1': 8.0,
     'L2_ffn_w2': 8.0,
     'L3_xattn_bk': 8.0,
     'L3_ffn_gate_w': 8.0,
     'L3_ffn_gate_bias': 8.0,
     'L3_ffn_Wg': 8.0,
     'L3_ffn_Wu': 8.0,
     'L3_ffn_Wd': 8.0,
     'L3_ffn_Sg': 8.0,
     'L3_ffn_Su': 8.0,
     'L3_ffn_Sd': 8.0}
    for name, (base, spread) in spreads.items():
        noise = np.random.default_rng([zlib.crc32(name.encode()), seed]).standard_normal(out[name].shape)
        drawn = base * np.exp(spread * noise) if base else spread * noise
        out[name] = jnp.asarray(drawn.astype(out[name].dtype))
    for name, factor in factors.items():
        out[name] = (out[name] * factor).astype(out[name].dtype)
    return out
```

```python
from contextlib import ExitStack

import numpy as np

import concourse.bass as bass
from concourse import mybir

F32 = mybir.dt.float32
BF16 = mybir.dt.bfloat16
I32 = mybir.dt.int32
U16 = mybir.dt.uint16
ALU = mybir.AluOpType
ACT = mybir.ActivationFunctionType
X = mybir.AxisListType.X
ds = bass.ds

P = 128
B = 32
GB = 4
G = B // GB
GT = GB * P
EPS = 1e-5
H = 16


class Counter:

    def __init__(self, sem, per, earlier=0):
        self.sem, self.per, self.credit = sem, per, per + 1 + earlier

    def at(self, g, n):
        return g * self.per + (self.credit + n)


class Chain:

    def __init__(self, eng, sig, g):
        self.eng, self.sig, self.g, self.n = eng, sig, g, 0

    def link(self, ins):
        self.n += 1
        ins.then_inc(self.sig.sem, 1)
        self.eng.wait_ge(self.sig.sem, self.sig.at(self.g, self.n))

    def close(self):
        assert self.n == self.sig.per, (self.n, self.sig.per)


class Arena:

    def __init__(self, tensor, words):
        self.tensor, self.words, self.used = tensor, words, 0

    def take(self, n, dt=F32):
        words = n if dt == F32 else (n + 1) // 2
        assert self.used + words <= self.words, (self.used, words, self.words)
        v = self.tensor[:, self.used:self.used + words]
        self.used += words
        return v if dt == F32 else v.bitcast(dt)


class Core:

    def __init__(self, nc, ctx, dram):
        self.nc, self.ctx, self.dram = nc, ctx, dram
        self.credits, self.const = [], {}
        self.psum = ctx.enter_context(nc.psum_tensor("psum", [P, 8 * 512], F32))
        self.bank = [self.psum[:, i * 512:(i + 1) * 512] for i in range(8)]
        self.ln_passes = self.ln_turns = 0
        self.ln_sems = [self.sem(f"ln_{n}") for n in ("stats", "var", "rstd", "chain")]
        self.ln_xn_done = self.counter("ln_xn", GB)
        self.ln_turned = self.counter("ln_turned", 2)
        self.ln_copied = self.counter("ln_copied", 2)

    def sb(self, name, n, dt=F32):
        return self.ctx.enter_context(self.nc.sbuf_tensor(name, [P, n], dt))

    def sem(self, name):
        return self.ctx.enter_context(self.nc.semaphore(name))

    def counter(self, name, per):
        s = Counter(self.sem(name), per)
        self.credits.append(s)
        return s


def layernorm(core, src, start, dst_natural=None, dst_t=None, t_scale=None, t_bias=None):
    nc = core.nc
    stat, moments, rstd, xn = core.ln_stat, core.ln_moments, core.ln_rstd, core.ln_xn
    n = core.ln_passes
    core.ln_passes += 1
    stats_done, var_done, rstd_done, chain = core.ln_sems
    xn_done = Counter(core.ln_xn_done.sem, GB, n * B)
    turned = Counter(core.ln_turned.sem, 2, core.ln_turns * 2 * G)
    copied = Counter(core.ln_copied.sem, 2, core.ln_turns * 2 * G)
    core.ln_turns += dst_natural is None
    st = stat.rearrange("p (b s) -> p b s", s=6)

    def dve(v):
        for s, value in start:
            v.wait_ge(s, value)
        with v.Fori(0, G) as g:
            for b in range(GB):
                nc.vector.bn_stats(stat[:, ds((g * GB + b) * 6, 6)], src[:, ds((g * GB + b) * P, P)]) \
                    .then_inc(stats_done, 1)
        v.wait_ge(stats_done, (n + 1) * B)
        mean, delta, dev, var = (moments[:, i * B:(i + 1) * B] for i in range(4))
        nc.vector.tensor_tensor(mean, st[:, :, 1], st[:, :, 4], ALU.add).then_inc(chain, 1)
        nc.vector.tensor_tensor(delta, st[:, :, 1], st[:, :, 4], ALU.subtract).then_inc(chain, 1)
        nc.vector.tensor_tensor(dev, st[:, :, 2], st[:, :, 5], ALU.add).then_inc(chain, 1)
        v.wait_ge(chain, 6 * n + 3)
        nc.vector.tensor_scalar(mean, mean, 0.5, None, ALU.mult).then_inc(chain, 1)
        nc.vector.scalar_tensor_tensor(delta, delta, 0.25, delta, ALU.mult, ALU.mult).then_inc(chain, 1)
        nc.vector.tensor_scalar(dev, dev, 1.0 / P, EPS, ALU.mult, ALU.add).then_inc(chain, 1)
        v.wait_ge(chain, 6 * n + 6)
        nc.vector.tensor_tensor(var, dev, delta, ALU.add).then_inc(var_done, 1)
        v.wait_ge(rstd_done, n + 1)
        with v.Fori(0, G) as g:
            for b in range(GB):
                if dst_natural is None:
                    v.wait_ge(turned.sem, turned.at(g, b // 2 - 1))
                    out = xn[:, b * P:(b + 1) * P]
                else:
                    out = dst_natural[:, ds((g * GB + b) * P, P)]
                nc.vector.tensor_scalar(out, src[:, ds((g * GB + b) * P, P)], mean[:, ds(g * GB + b, 1)],
                                        rstd[:, ds(g * GB + b, 1)], ALU.subtract, ALU.mult) \
                    .then_inc(xn_done.sem, 1)

    def pool(p):
        p.wait_ge(var_done, n + 1)
        nc.gpsimd.tensor_tensor(rstd, moments[:, 3 * B:4 * B], core.neg_half, ALU.pow).then_inc(rstd_done, 1)

    def pe(t):
        for s, value in start:
            t.wait_ge(s, value)
        with t.Fori(0, G) as g:
            for half in range(2):
                t.wait_ge(copied.sem, copied.at(g, half - 1))
                for b in (2 * half, 2 * half + 1):
                    t.wait_ge(xn_done.sem, xn_done.at(g, b + 1))
                    ins = nc.tensor.transpose(core.bank[half][:, b % 2 * P:(b % 2 + 1) * P],
                                              xn[:, b * P:(b + 1) * P], core.ident)
                ins.then_inc(turned.sem, 1)

    def act(a):
        with a.Fori(0, G) as g:
            for half in range(2):
                a.wait_ge(turned.sem, turned.at(g, half + 1))
                out = dst_t[:, ds(g * GT + half * 2 * P, 2 * P)]
                if t_scale is None:
                    ins = nc.scalar.activation(out, core.bank[half][:, 0:2 * P], ACT.Copy)
                else:
                    ins = nc.scalar.activation(out, core.bank[half][:, 0:2 * P], ACT.Identity,
                                               bias=t_bias, scale=t_scale)
                ins.then_inc(copied.sem, 1)

    if dst_natural is not None:
        return dict(dve=dve, pool=pool), (xn_done.sem, xn_done.at(G, 0))
    return dict(dve=dve, pool=pool, pe=pe, act=act), (copied.sem, copied.at(G, 0))


def stage_attention0(core, arena, start):
    nc, d, bank = core.nc, core.dram, core.bank
    DH, QUADS = P // H, H // GB
    SCALE = 1.0 / DH ** 0.5
    xnT, ctxT, x = core.xnT, core.ctxT, core.x
    w = arena.take(4 * P)
    wq, wk, wv, wo = (w[:, i * P:(i + 1) * P] for i in range(4))
    bqk = arena.take(2)
    qT, kT = arena.take(GT), arena.take(GT)
    qm = [arena.take(H * P) for _ in range(2)]
    cT = arena.take(GB * P)
    vaug = arena.take(GB * H * (DH + 1)).rearrange("p (b h e) -> p b h e", b=GB, h=H)
    nm = arena.take(2 * H)
    nm2 = [arena.take(P, BF16) for _ in range(2)]
    nmT = [arena.take(P, BF16) for _ in range(2)]
    pT = [arena.take(GT) for _ in range(2)]
    rsum = arena.take(2 * H)
    ao, aoT = arena.take(2 * P), arena.take(2 * P)

    w_in = core.sem("a0_w_in")
    ones_set = core.sem("a0_ones_set")
    fns, (ln_sem, ln_n) = layernorm(core, x, start, dst_t=xnT)
    proj = core.counter("a0_proj", 3)
    qkv = core.counter("a0_qkv", 3)
    ct = core.counter("a0_ct", GB)
    qm_v = core.counter("a0_qm_v", GB)
    qm_p = core.counter("a0_qm_p", GB)
    nat = core.counter("a0_nat", GB * QUADS)
    mx = core.counter("a0_mx", GB * QUADS)
    nms = core.counter("a0_nms", GB)
    nmt = core.counter("a0_nmt", GB)
    nmc = core.counter("a0_nmc", GB)
    st = core.counter("a0_st", GB * QUADS)
    ex = core.counter("a0_ex", GB * QUADS)
    av = core.counter("a0_av", GB * QUADS)
    aon = core.counter("a0_aon", GB)
    aot = core.counter("a0_aot", GB)
    aoc = core.counter("a0_aoc", GB)
    yd = core.counter("a0_yd", GB)
    xd = core.counter("a0_xd", GB)
    chain = core.counter("a0_chain", 2 * GB)

    def sp(s):
        s.dma_start(w, d["a0_w"]).then_inc(w_in, 16)
        s.dma_start(bqk, d["a0_bqk"]).then_inc(w_in, 16)

    def pool(p):
        nc.gpsimd.memset(vaug[:, :, :, DH:DH + 1], 1.0).then_inc(ones_set, 1)
        for t in nm2:
            nc.gpsimd.memset(t, 0.0).then_inc(ones_set, 1)
        fns["pool"](p)
        with p.Fori(0, G) as g:
            for b in range(GB):
                p.wait_ge(proj.sem, proj.at(g, 0))
                nc.gpsimd.tensor_copy(cT[:, b * P:(b + 1) * P], ctxT[:, ds((g * GB + b) * P, P)]) \
                    .then_inc(ct.sem, 1)
            for b in range(GB):
                p.wait_ge(qkv.sem, qkv.at(g, 1))
                p.wait_ge(st.sem, st.at(g, (b - 1) * QUADS))
                half = H // 2
                nc.gpsimd.tensor_tensor(
                    qm[b % 2][:, half * P:].rearrange("p (h q) -> p h q", h=half),
                    qT[:, b * P:(b + 1) * P].unsqueeze(1).to_broadcast([P, half, P]),
                    core.head_mask[:, half:H].unsqueeze(2).to_broadcast([P, half, P]), ALU.mult) \
                    .then_inc(qm_p.sem, 1)

    def dve(v):
        fns["dve"](v)
        v.wait_ge(ones_set, 3)

        def mask_q(g, b):
            v.wait_ge(qkv.sem, qkv.at(g, 1))
            v.wait_ge(st.sem, st.at(g, (b - 1) * QUADS))
            half = H // 2
            nc.vector.tensor_tensor(
                qm[b % 2][:, 0:half * P].rearrange("p (h q) -> p h q", h=half),
                qT[:, b * P:(b + 1) * P].unsqueeze(1).to_broadcast([P, half, P]),
                core.head_mask[:, 0:half].unsqueeze(2).to_broadcast([P, half, P]), ALU.mult) \
                .then_inc(qm_v.sem, 1)

        def row_max(g, b, c):
            n = nm[:, b % 2 * H:b % 2 * H + H]
            for t in range(QUADS):
                v.wait_ge(nat.sem, nat.at(g, b * QUADS + t + 1))
                nc.vector.tensor_reduce(n[:, t * 4:t * 4 + 4], bank[t % 2][:, :].rearrange("p (h k) -> p h k", h=4),
                                        X, ALU.max, negate=True).then_inc(mx.sem, 1)
            v.wait_ge(nmt.sem, nmt.at(g, b - 1))
            v.wait_ge(mx.sem, mx.at(g, (b + 1) * QUADS))
            c.link(nc.vector.tensor_copy(nm2[b % 2][:, 0:H], n))
            nc.vector.tensor_tensor(nm2[b % 2][:, H:2 * H], n, nm2[b % 2][:, 0:H], ALU.subtract) \
                .then_inc(nms.sem, 1)

        def normalise(g, b, c):
            v.wait_ge(av.sem, av.at(g, (b + 1) * QUADS))
            o = bank[4 + b % 2][:, 0:H * (DH + 1)].rearrange("p (h e) -> p h e", h=H)
            r = rsum[:, b % 2 * H:b % 2 * H + H]
            c.link(nc.vector.reciprocal(r, o[:, :, DH]))
            v.wait_ge(aot.sem, aot.at(g, b - 1))
            nc.vector.tensor_tensor(ao[:, b % 2 * P:(b % 2 + 1) * P].rearrange("p (h e) -> p h e", h=H),
                                    o[:, :, 0:DH], r.unsqueeze(2).to_broadcast([P, H, DH]), ALU.mult) \
                .then_inc(aon.sem, 1)

        def update(g, b):
            v.wait_ge(yd.sem, yd.at(g, b + 1))
            xs = x[:, ds((g * GB + b) * P, P)]
            nc.vector.tensor_tensor(xs, xs, bank[6][:, P:2 * P], ALU.add).then_inc(xd.sem, 1)

        with v.Fori(0, G) as g:
            c = Chain(v, chain, g)
            mask_q(g, 0)
            row_max(g, 0, c)
            for b in range(GB):
                if b + 1 < GB:
                    mask_q(g, b + 1)
                    row_max(g, b + 1, c)
                normalise(g, b, c)
                if b > 0:
                    update(g, b - 1)
            update(g, GB - 1)
            c.close()

    def pe(t):
        fns["pe"](t)
        t.wait_ge(w_in, 32)
        t.wait_ge(ln_sem, ln_n)

        def natural(g, b):
            t.wait_ge(qm_v.sem, qm_v.at(g, b + 1))
            t.wait_ge(qm_p.sem, qm_p.at(g, b + 1))
            for q in range(QUADS):
                t.wait_ge(mx.sem, mx.at(g, b * QUADS + q - 1))
                for i in range(4):
                    h = q * 4 + i
                    ins = nc.tensor.matmul(bank[q % 2][:, i * P:(i + 1) * P], qm[b % 2][:, h * P:(h + 1) * P],
                                           kT[:, b * P:(b + 1) * P], start=True, stop=True)
                ins.then_inc(nat.sem, 1)

        def turn_max(g, b):
            t.wait_ge(nms.sem, nms.at(g, b + 1))
            t.wait_ge(nmc.sem, nmc.at(g, b))
            nc.tensor.transpose(bank[7][:, 0:P // 2].bitcast(BF16), nm2[b % 2], core.ident_b).then_inc(nmt.sem, 1)

        def attend(g, b):
            def av_quad(q):
                n = b * QUADS + q
                t.wait_ge(ex.sem, ex.at(g, n + 1))
                if q == 0:
                    t.wait_ge(aon.sem, aon.at(g, b - 1))
                for i in range(4):
                    h = q * 4 + i
                    ins = nc.tensor.matmul(bank[4 + b % 2][:, h * (DH + 1):(h + 1) * (DH + 1)],
                                           pT[q % 2][:, i * P:(i + 1) * P], vaug[:, b, h, :], start=True, stop=True)
                ins.then_inc(av.sem, 1)

            t.wait_ge(nmc.sem, nmc.at(g, b + 1))
            for q in range(QUADS):
                n = b * QUADS + q
                t.wait_ge(ex.sem, ex.at(g, n - 1))
                nc.tensor.matmul(bank[2 + q % 2][:, :], kT[:, b * P:(b + 1) * P],
                                 qm[b % 2][:, q * 4 * P:(q * 4 + 4) * P], start=True, stop=False)
                for i in range(4):
                    h = q * 4 + i
                    ins = nc.tensor.matmul(bank[2 + q % 2][:, i * P:(i + 1) * P], core.sel_head[:, h * P:(h + 1) * P],
                                           nmT[b % 2], start=False, stop=i == 3)
                ins.then_inc(st.sem, 1)
                if q:
                    av_quad(q - 1)
            av_quad(QUADS - 1)

        def project_out(g, b):
            t.wait_ge(aon.sem, aon.at(g, b + 1))
            t.wait_ge(xd.sem, xd.at(g, b))
            nc.tensor.transpose(bank[6][:, 0:P], ao[:, b % 2 * P:(b % 2 + 1) * P], core.ident).then_inc(aot.sem, 1)
            t.wait_ge(aoc.sem, aoc.at(g, b + 1))
            nc.tensor.matmul(bank[6][:, P:2 * P], aoT[:, b % 2 * P:(b % 2 + 1) * P], wo, start=True, stop=False)
            nc.tensor.matmul(bank[6][:, P:2 * P], core.ones_row, core.bias["a0_out"], start=False, stop=True) \
                .then_inc(yd.sem, 1)

        with t.Fori(0, G) as g:
            t.wait_ge(xd.sem, xd.at(g, 0))
            t.wait_ge(nmc.sem, nmc.at(g, 0))
            nc.tensor.matmul(bank[6][:, :], wq, xnT[:, ds(g * GT, GT)], start=True, stop=True).then_inc(proj.sem, 1)
            nc.tensor.matmul(bank[7][:, :], wk, ctxT[:, ds(g * GT, GT)], start=True, stop=True).then_inc(proj.sem, 1)
            t.wait_ge(qkv.sem, qkv.at(g, 1))
            for b in range(GB):
                t.wait_ge(ct.sem, ct.at(g, b + 1))
                nc.tensor.matmul(bank[6][:, b * P:(b + 1) * P], cT[:, b * P:(b + 1) * P], wv, start=True, stop=False)
                ins = nc.tensor.matmul(bank[6][:, b * P:(b + 1) * P], core.ones_row, core.bias["a0_v"],
                                       start=False, stop=True)
            ins.then_inc(proj.sem, 1)
            t.wait_ge(qkv.sem, qkv.at(g, 3))
            natural(g, 0)
            turn_max(g, 0)
            for b in range(GB):
                if b + 1 < GB:
                    natural(g, b + 1)
                attend(g, b)
                if b + 1 < GB:
                    turn_max(g, b + 1)
                if b > 0:
                    project_out(g, b - 1)
            project_out(g, GB - 1)

    def act(a):
        fns["act"](a)
        a.wait_ge(w_in, 32)
        a.wait_ge(ones_set, 3)

        def copy_max(g, b):
            a.wait_ge(nmt.sem, nmt.at(g, b + 1))
            a.wait_ge(st.sem, st.at(g, (b - 1) * QUADS))
            nc.scalar.activation(nmT[b % 2], bank[7][:, 0:P // 2].bitcast(BF16), ACT.Copy).then_inc(nmc.sem, 1)

        def exps(g, b):
            for q in range(QUADS):
                n = b * QUADS + q
                a.wait_ge(st.sem, st.at(g, n + 1))
                a.wait_ge(av.sem, av.at(g, n - 1))
                nc.scalar.activation(pT[q % 2], bank[2 + q % 2][:, :], ACT.Exp, scale=SCALE).then_inc(ex.sem, 1)

        def copy_ao(g, b):
            a.wait_ge(aot.sem, aot.at(g, b + 1))
            a.wait_ge(yd.sem, yd.at(g, b - 1))
            nc.scalar.activation(aoT[:, b % 2 * P:(b % 2 + 1) * P], bank[6][:, 0:P], ACT.Copy).then_inc(aoc.sem, 1)

        with a.Fori(0, G) as g:
            a.wait_ge(proj.sem, proj.at(g, 1))
            a.wait_ge(qm_v.sem, qm_v.at(g, 0))
            a.wait_ge(qm_p.sem, qm_p.at(g, 0))
            nc.scalar.activation(qT, bank[6][:, :], ACT.Identity, bias=bqk[:, 0:1]).then_inc(qkv.sem, 1)
            a.wait_ge(proj.sem, proj.at(g, 2))
            a.wait_ge(st.sem, st.at(g, 0))
            nc.scalar.activation(kT, bank[7][:, :], ACT.Identity, bias=bqk[:, 1:2]).then_inc(qkv.sem, 1)
            a.wait_ge(proj.sem, proj.at(g, 3))
            a.wait_ge(av.sem, av.at(g, 0))
            nc.scalar.activation(vaug[:, :, :, 0:DH], bank[6][:, :].rearrange("p (b h e) -> p b h e", b=GB, h=H),
                                 ACT.Copy).then_inc(qkv.sem, 1)
            copy_max(g, 0)
            for b in range(GB):
                exps(g, b)
                if b + 1 < GB:
                    copy_max(g, b + 1)
                if b > 0:
                    copy_ao(g, b - 1)
            copy_ao(g, GB - 1)

    return dict(sp=sp, pool=pool, dve=dve, pe=pe, act=act), [(xd.sem, xd.at(G, 0))]


def stage_fourier_ffn(core, arena, start):
    nc, d, bank = core.nc, core.dram, core.bank
    x, xnT = core.x, core.xnT
    cos, sin, msin = (core.const[n] for n in ("dft_cos", "dft_sin", "dft_msin"))
    w = arena.take(2 * P)
    wr, wi = w[:, 0:P], w[:, P:2 * P]
    ab, m = arena.take(2 * P), arena.take(P)
    xT = arena.take(GT)

    fns, ln_done = layernorm(core, x, start, dst_t=xnT)
    w_in = core.sem("f0_w_in")
    pre, prec = core.sem("f0_pre"), core.sem("f0_prec")
    ct = core.counter("f0_ct", 2)
    yd = core.counter("f0_yd", 2)
    xd = core.counter("f0_xd", 2)

    def sp(s):
        for sem, n in start:
            s.wait_ge(sem, n)
        s.dma_start(w, d["f0_w"]).then_inc(w_in, 16)

    def pool(p):
        fns["pool"](p)
        p.wait_ge(*ln_done)
        with p.Fori(0, G) as g:
            for half in range(2):
                p.wait_ge(yd.sem, yd.at(g, half - 1))
                nc.gpsimd.tensor_copy(xT[:, half * 2 * P:(half + 1) * 2 * P],
                                      xnT[:, ds(g * GT + half * 2 * P, 2 * P)]).then_inc(ct.sem, 1)

    def pe(t):
        fns["pe"](t)
        t.wait_ge(w_in, 16)
        nc.tensor.matmul(bank[4][:, 0:P], wr, cos, start=True, stop=False)
        nc.tensor.matmul(bank[4][:, 0:P], wi, sin, start=False, stop=True)
        nc.tensor.matmul(bank[4][:, P:2 * P], wi, cos, start=True, stop=False)
        nc.tensor.matmul(bank[4][:, P:2 * P], wr, msin, start=False, stop=True).then_inc(pre, 1)
        t.wait_ge(prec, 1)
        nc.tensor.matmul(bank[5][:, 0:P], ab[:, 0:P], cos, start=True, stop=False)
        nc.tensor.matmul(bank[5][:, 0:P], ab[:, P:2 * P], msin, start=False, stop=True).then_inc(pre, 1)
        t.wait_ge(prec, 2)
        with t.Fori(0, G) as g:
            for half in range(2):
                t.wait_ge(ct.sem, ct.at(g, half + 1))
                t.wait_ge(xd.sem, xd.at(g, half - 1))
                for b in range(2):
                    out = bank[2 + half][:, b * P:(b + 1) * P]
                    nc.tensor.matmul(out, xT[:, (half * 2 + b) * P:(half * 2 + b + 1) * P], m, start=True, stop=False)
                    ins = nc.tensor.matmul(out, core.ones_row, core.bias["ffn0"], start=False, stop=True)
                ins.then_inc(yd.sem, 1)

    def act(a):
        fns["act"](a)
        a.wait_ge(pre, 1)
        nc.scalar.activation(ab, bank[4][:, 0:2 * P], ACT.Copy).then_inc(prec, 1)
        a.wait_ge(pre, 2)
        nc.scalar.activation(m, bank[5][:, 0:P], ACT.Copy, scale=1.0 / P).then_inc(prec, 1)

    def dve(v):
        fns["dve"](v)
        with v.Fori(0, G) as g:
            for half in range(2):
                v.wait_ge(yd.sem, yd.at(g, half + 1))
                xs = x[:, ds(g * GT + half * 2 * P, 2 * P)]
                nc.vector.tensor_tensor(xs, xs, bank[2 + half][:, 0:2 * P], ALU.add).then_inc(xd.sem, 1)

    return dict(sp=sp, pool=pool, dve=dve, pe=pe, act=act), [(xd.sem, xd.at(G, 0))]


def stage_attention1(core, arena, start):
    nc, d, bank = core.nc, core.dram, core.bank
    x, xnT, ctxT = core.x, core.xnT, core.ctxT
    NK, DH = 5, P // H
    R = H * NK
    HR = R // 2
    QUADS, CH = R // 4, 4
    QC = QUADS // CH
    NQ = GB * QUADS
    MAGIC = 1.5 * 2.0 ** 23
    SCALE = 0.5 / DH ** 0.5
    CW = P + 2

    w = arena.take(P + R + 2 * P + P)
    wq, woff, wkv, wo = w[:, 0:P], w[:, P:P + R], w[:, P + R:3 * P + R], w[:, 3 * P + R:4 * P + R]
    vecs = arena.take(2 + R)
    bq, token, ref = vecs[:, 0:1], vecs[:, 1:2], vecs[:, 2:2 + R]
    sel = arena.take(HR * P, BF16)
    mask_i = arena.take(B)
    om, ones, slen, rslen = arena.take(B), arena.take(P), arena.take(B), arena.take(B)
    qpT, qn = arena.take(GT), arena.take(GT)
    cT = arena.take(GB * CW)
    t_, n_, m_, ix, i0, dx = (arena.take(GB * R) for _ in range(6))
    w01 = arena.take(GB * R * 2)
    rows = arena.take(GB * 2 * P, BF16)
    rT = arena.take(GB * 2 * P, BF16)
    kvs = [arena.take(3 * GT, BF16) for _ in range(2)]
    kvr = arena.take(GT)
    oh = [arena.take(GT, BF16) for _ in range(4)]
    prod = arena.take(QC * 4 * 2 * DH)
    sp_, s2, sc, ee, pw, aw = (arena.take(n) for n in (2 * 2 * R, 2 * R, R, R, R, 2 * R))
    mxs, sm = arena.take(H), arena.take(H)
    gv = [arena.take(2 * R * DH) for _ in range(2)]
    pv = arena.take(2 * R * DH)
    cx, cxT = arena.take(P), arena.take(P)
    G2 = [core.psum[:, 3 * 512:3 * 512 + QC * 128], core.psum[:, 5 * 512:5 * 512 + QC * 128]]

    w_in, set_, pre = core.sem("a1_w_in"), core.sem("a1_set"), core.sem("a1_pre")
    lens = core.sem("a1_lens")
    fns, ln_done = layernorm(core, x, start, dst_t=xnT)
    pj = core.counter("a1_pj", 4)
    pc = core.counter("a1_pc", 3)
    idx = core.counter("a1_idx", 1)
    ct = core.counter("a1_ct", GB)
    kvp = core.counter("a1_kvp", GB)
    kvh = core.counter("a1_kvh", GB)
    kvd = core.counter("a1_kvd", GB)
    kvl = core.counter("a1_kvl", 2 * GB)
    bc = core.counter("a1_bc", NQ)
    rla = core.counter("a1_rla", NQ * 3 // 4)
    rlv = core.counter("a1_rlv", NQ // 4)
    gat = core.counter("a1_gat", NQ)
    kp = core.counter("a1_kp", GB * CH)
    gc = core.counter("a1_gc", GB * CH)
    scd = core.counter("a1_scd", GB)
    exd = core.counter("a1_exd", GB)
    awd = core.counter("a1_awd", GB)
    vpd = core.counter("a1_vpd", GB)
    cxd = core.counter("a1_cxd", GB)
    cxt = core.counter("a1_cxt", GB)
    cxc = core.counter("a1_cxc", GB)
    yd = core.counter("a1_yd", GB)
    xd = core.counter("a1_xd", GB)
    chain = core.counter("a1_chain", 20 + GB * (CH + 3 + 3))

    def on_dve(n):
        return n % 4 == 3

    def wait_onehot(eng, g, n):
        if on_dve(n):
            eng.wait_ge(rlv.sem, rlv.at(g, n // 4 + 1))
        else:
            eng.wait_ge(rla.sem, rla.at(g, n + 1 - (n + 1) // 4))

    def sp(s):
        for sem, n in start:
            s.wait_ge(sem, n)
        s.dma_start(w, d["a1_w"]).then_inc(w_in, 16)
        s.dma_start(vecs, d["a1_vecs"]).then_inc(w_in, 16)
        s.dma_start(sel.bitcast(U16), d["a1_sel"]).then_inc(w_in, 16)
        s.dma_start(mask_i.bitcast(I32), d["a1_maskT"]).then_inc(w_in, 16)

    def pool(p):
        for sem, n in start:
            p.wait_ge(sem, n)
        nc.gpsimd.memset(ones, 1.0).then_inc(set_, 1)
        rv = rows.rearrange("p (c r) -> p c r", r=P)
        nc.gpsimd.memset(rv[:, :, 3 * HR:3 * HR + 2], 1.0).then_inc(set_, 1)
        nc.gpsimd.memset(rv[:, :, 3 * HR + 2:P], 0.0).then_inc(set_, 1)
        nc.gpsimd.memset(cT.rearrange("p (b c) -> p b c", c=CW)[:, :, P:CW], 0.0).then_inc(set_, 1)
        fns["pool"](p)

        def split_kv(g, b):
            p.wait_ge(kvd.sem, kvd.at(g, b + 1))
            k3 = kvs[b % 2].rearrange("p (s n) -> p s n", s=3)
            nc.gpsimd.tensor_tensor(k3[:, 1, :], kvr, ones[:, 0:1].to_broadcast([P, GT]), ALU.mult).then_inc(kvl.sem, 1)
            p.wait_ge(kvl.sem, kvl.at(g, 2 * b + 1))
            nc.gpsimd.tensor_tensor(k3[:, 2, :], kvr, k3[:, 1, :], ALU.subtract).then_inc(kvl.sem, 1)

        def weigh_values(g, b):
            p.wait_ge(awd.sem, awd.at(g, b + 1))
            p.wait_ge(gc.sem, gc.at(g, (b + 1) * CH))
            p.wait_ge(cxd.sem, cxd.at(g, b))
            nc.gpsimd.tensor_tensor(pv.rearrange("p (r e) -> p r e", e=DH),
                                    gv[b % 2].rearrange("p (r e) -> p r e", e=DH),
                                    aw.unsqueeze(2).to_broadcast([P, 2 * R, DH]), ALU.mult).then_inc(vpd.sem, 1)

        with p.Fori(0, G) as g:
            for b in range(GB):
                p.wait_ge(kvp.sem, kvp.at(g, b - GB + 1))
                nc.gpsimd.tensor_copy(cT[:, b * CW:b * CW + P], ctxT[:, ds((g * GB + b) * P, P)]).then_inc(ct.sem, 1)
            split_kv(g, 0)
            for b in range(GB):
                if b > 0:
                    weigh_values(g, b - 1)
                if b + 1 < GB:
                    split_kv(g, b + 1)
            weigh_values(g, GB - 1)

    def pe(t):
        fns["pe"](t)
        t.wait_ge(w_in, 64)
        t.wait_ge(set_, 4)
        t.wait_ge(pre, 1)
        nc.tensor.matmul(bank[7][:, 0:B], ones, om, start=True, stop=True).then_inc(lens, 1)
        t.wait_ge(lens, 2)
        t.wait_ge(*ln_done)

        def project_kv(g, b):
            dst = bank[2] if b == 0 else bank[7]
            t.wait_ge(ct.sem, ct.at(g, b + 1))
            for shift in range(2):
                out = dst[:, shift * 2 * P:(shift + 1) * 2 * P]
                nc.tensor.matmul(out, cT[:, b * CW + shift:b * CW + shift + P], wkv, start=True, stop=False)
                ins = nc.tensor.matmul(out, (core.ones_row, core.const["ones_row_cut"])[shift], core.bias["a1_kv"],
                                       start=False, stop=True)
            ins.then_inc(kvp.sem, 1)

        def places(g, n):
            b, m = divmod(n, QUADS)
            if n < 3:
                t.wait_ge(pc.sem, pc.at(g, 3))
                t.wait_ge(kvd.sem, kvd.at(g, 1))
            else:
                wait_onehot(t, g, n - 3)
            for j in range(4):
                r = m * 4 + j
                ins = nc.tensor.matmul(bank[n % 3][:, j * P:(j + 1) * P], sel[:, r % HR * P:(r % HR + 1) * P],
                                       rT[:, (b * 2 + r // HR) * P:(b * 2 + r // HR + 1) * P], start=True, stop=True)
            ins.then_inc(bc.sem, 1)

        def sample(g, n):
            b, m = divmod(n, QUADS)
            c = m // QC
            if m == 0:
                t.wait_ge(kvl.sem, kvl.at(g, 2 * (b + 1)))
            if m % QC == 0:
                t.wait_ge(gc.sem, gc.at(g, b * CH + c - 1))
            wait_onehot(t, g, n)
            k5 = kvs[b % 2].rearrange("p (s i k e) -> p s i k e", s=3, i=2, k=2)
            for j in range(4):
                r = m * 4 + j
                h = r // NK
                col = (r - c * QC * 4) * 4 * DH
                for s in range(3):
                    ins = nc.tensor.matmul(G2[c % 2][:, col:col + 4 * DH], oh[n % 4][:, j * P:(j + 1) * P],
                                           k5[:, s, :, :, h * DH:(h + 1) * DH], start=s == 0, stop=s == 2)
            ins.then_inc(gat.sem, 1)

        def turn_ctx(g, b):
            t.wait_ge(cxd.sem, cxd.at(g, b + 1))
            if b + 2 < GB:
                t.wait_ge(kvd.sem, kvd.at(g, b + 3))
            t.wait_ge(xd.sem, xd.at(g, b))
            nc.tensor.transpose(bank[7][:, 0:P], cx, core.ident).then_inc(cxt.sem, 1)

        def project_out(g, b):
            t.wait_ge(cxc.sem, cxc.at(g, b + 1))
            nc.tensor.matmul(bank[7][:, P:2 * P], cxT, wo, start=True, stop=False)
            nc.tensor.matmul(bank[7][:, P:2 * P], core.ones_row, core.bias["a1_out"], start=False, stop=True) \
                .then_inc(yd.sem, 1)

        with t.Fori(0, G) as g:
            t.wait_ge(rla.sem, rla.at(g, 0))
            t.wait_ge(rlv.sem, rlv.at(g, 0))
            nc.tensor.matmul(bank[0], wq, xnT[:, ds(g * GT, GT)], start=True, stop=True).then_inc(pj.sem, 1)
            project_kv(g, 0)
            t.wait_ge(pc.sem, pc.at(g, 1))
            for b in range(GB):
                ins = nc.tensor.transpose(bank[1][:, b * P:(b + 1) * P], qpT[:, b * P:(b + 1) * P], core.ident)
            ins.then_inc(pj.sem, 1)
            t.wait_ge(xd.sem, xd.at(g, 0))
            for b in range(GB):
                out = bank[7][:, b * R:(b + 1) * R]
                nc.tensor.matmul(out, qpT[:, b * P:(b + 1) * P], woff, start=True, stop=False)
                ins = nc.tensor.matmul(out, core.ones_row, core.bias["a1_off"], start=False, stop=True)
            ins.then_inc(pj.sem, 1)
            t.wait_ge(idx.sem, idx.at(g, 1))
            for c in range(2 * GB):
                ins = nc.tensor.transpose(bank[0].bitcast(BF16)[:, c * P:(c + 1) * P], rows[:, c * P:(c + 1) * P],
                                          core.ident_b)
            ins.then_inc(pj.sem, 1)
            places(g, 0)
            places(g, 1)
            for s in range(GB + 2):
                if s < GB:
                    for m in range(QUADS):
                        n = s * QUADS + m
                        if n + 2 < NQ:
                            places(g, n + 2)
                        sample(g, n)
                        if m == 2 and s >= 2:
                            project_out(g, s - 2)
                        if m == 7 and s + 1 < GB:
                            t.wait_ge(xd.sem, xd.at(g, max(s - 1, 0)))
                            t.wait_ge(cxc.sem, cxc.at(g, max(s - 1, 0)))
                            t.wait_ge(idx.sem, idx.at(g, 1))
                            project_kv(g, s + 1)
                elif s - 2 >= 0:
                    project_out(g, s - 2)
                if 1 <= s <= GB:
                    turn_ctx(g, s - 1)

    def act(a):
        fns["act"](a)
        a.wait_ge(w_in, 64)

        def high_part(g, b):
            a.wait_ge(kvp.sem, kvp.at(g, b + 1))
            a.wait_ge(gat.sem, gat.at(g, (b - 1) * QUADS))
            nc.scalar.activation(kvs[b % 2][:, 0:GT], bank[2] if b == 0 else bank[7], ACT.Copy).then_inc(kvh.sem, 1)

        def onehot(g, n):
            a.wait_ge(bc.sem, bc.at(g, n + 1))
            a.wait_ge(gat.sem, gat.at(g, n - 3))
            nc.scalar.activation(oh[n % 4], bank[n % 3], ACT.Relu).then_inc(rla.sem, 1)

        def copy_values(g, b, c):
            a.wait_ge(kp.sem, kp.at(g, b * CH + c + 1))
            a.wait_ge(vpd.sem, vpd.at(g, b - 1))
            n = QC * 4 * 2
            nc.scalar.activation(gv[b % 2].rearrange("p (c r e) -> p c r e", c=CH, e=DH)[:, c],
                                 G2[c % 2].rearrange("p (r e) -> p r e", r=n)[:, :, DH:2 * DH], ACT.Copy) \
                .then_inc(gc.sem, 1)

        def exps(g, b):
            a.wait_ge(scd.sem, scd.at(g, b + 1))
            nc.scalar.activation(ee, sc, ACT.Exp, scale=SCALE).then_inc(exd.sem, 1)

        def copy_ctx(g, b):
            a.wait_ge(cxt.sem, cxt.at(g, b + 1))
            a.wait_ge(yd.sem, yd.at(g, b))
            nc.scalar.activation(cxT, bank[7][:, 0:P], ACT.Copy).then_inc(cxc.sem, 1)

        with a.Fori(0, G) as g:
            a.wait_ge(pj.sem, pj.at(g, 1))
            nc.scalar.activation(qpT, bank[0], ACT.Identity, bias=bq).then_inc(pc.sem, 1)
            high_part(g, 0)
            a.wait_ge(pj.sem, pj.at(g, 2))
            a.wait_ge(kp.sem, kp.at(g, 0))
            nc.scalar.activation(qn, bank[1], ACT.Copy).then_inc(pc.sem, 1)
            a.wait_ge(pj.sem, pj.at(g, 4))
            nc.scalar.activation(rT, bank[0].bitcast(BF16), ACT.Copy).then_inc(pc.sem, 1)
            for s in range(GB + 2):
                if s < GB:
                    for m in range(QUADS):
                        n = s * QUADS + m
                        if not on_dve(n):
                            onehot(g, n)
                        if m == 1 and s >= 2:
                            copy_ctx(g, s - 2)
                        if m == 2 and s >= 1:
                            copy_values(g, s - 1, CH - 1)
                        if m == 6 and s >= 1:
                            exps(g, s - 1)
                        if m == 9 and s + 1 < GB:
                            high_part(g, s + 1)
                        if m in (8, 12, 17):
                            copy_values(g, s, (8, 12, 17).index(m))
                else:
                    copy_ctx(g, s - 2)
                    if s == GB:
                        copy_values(g, s - 1, CH - 1)
                        exps(g, s - 1)

    def dve(v):
        fns["dve"](v)
        v.wait_ge(w_in, 64)
        v.wait_ge(set_, 4)
        nc.vector.tensor_scalar(om, mask_i.bitcast(I32), -1.0, 1.0, ALU.mult, ALU.add).then_inc(pre, 1)
        v.wait_ge(lens, 1)
        nc.vector.tensor_scalar(slen, bank[7][:, 0:B], -1.0, None, ALU.add).then_inc(lens, 1)
        v.wait_ge(lens, 2)
        nc.vector.reciprocal(rslen, slen).then_inc(lens, 1)
        v.wait_ge(lens, 3)
        v3 = lambda a: a.rearrange("p (b r) -> p b r", b=GB)

        def find_places(g, c):
            v.wait_ge(pj.sem, pj.at(g, 3))
            sl = slen[:, ds(g * GB, GB)].unsqueeze(2).to_broadcast([P, GB, R])
            rs = rslen[:, ds(g * GB, GB)].unsqueeze(2).to_broadcast([P, GB, R])
            link = c.link
            link(nc.vector.tensor_tensor(v3(t_), v3(bank[7][:, 0:GB * R]),
                                         ref.unsqueeze(1).to_broadcast([P, GB, R]), ALU.add))
            link(nc.vector.tensor_scalar(t_, t_, token, None, ALU.add))
            link(nc.vector.tensor_tensor(v3(n_), v3(t_), rs, ALU.mult))
            link(nc.vector.tensor_scalar(n_, n_, -0.5, MAGIC, ALU.add, ALU.add))
            link(nc.vector.scalar_tensor_tensor(v3(n_), v3(n_), MAGIC, sl, ALU.subtract, ALU.mult))
            link(nc.vector.tensor_tensor(t_, t_, n_, ALU.subtract))
            link(nc.vector.scalar_tensor_tensor(v3(m_), v3(t_), 0.0, sl, ALU.is_lt, ALU.mult))
            link(nc.vector.tensor_tensor(t_, t_, m_, ALU.add))
            link(nc.vector.tensor_tensor(v3(m_), v3(t_), sl, ALU.is_ge))
            link(nc.vector.tensor_tensor(v3(m_), v3(m_), sl, ALU.mult))
            link(nc.vector.tensor_tensor(t_, t_, m_, ALU.subtract))
            link(nc.vector.tensor_scalar(ix, t_, P / (P - 1.0), -0.5, ALU.mult, ALU.add))
            link(nc.vector.tensor_scalar(i0, ix, -0.5, MAGIC, ALU.add, ALU.add))
            link(nc.vector.tensor_scalar(i0, i0, MAGIC, None, ALU.subtract))
            link(nc.vector.tensor_tensor(dx, ix, i0, ALU.subtract))
            rv = rows.rearrange("p (c r) -> p c r", r=P)
            i8 = i0.rearrange("p (c r) -> p c r", r=HR)
            w2 = w01.rearrange("p (r i) -> p r i", i=2)
            nc.vector.tensor_scalar(rv[:, :, 0:HR], i8, 0.0, None, ALU.max)
            nc.vector.scalar_tensor_tensor(w2[:, :, 1], i0, 0.0, dx, ALU.is_ge, ALU.mult)
            nc.vector.tensor_scalar(t_, dx, -2.0, 1.0, ALU.mult, ALU.add)
            link(nc.vector.scalar_tensor_tensor(m_, i0, 0.0, i0, ALU.max, ALU.mult))
            link(nc.vector.tensor_copy(rv[:, :, HR:2 * HR], m_.rearrange("p (c r) -> p c r", r=HR)))
            link(nc.vector.scalar_tensor_tensor(n_, i0, 0.0, t_, ALU.is_ge, ALU.mult))
            link(nc.vector.tensor_tensor(w2[:, :, 0], n_, dx, ALU.add))
            nc.vector.tensor_tensor(rv[:, :, 2 * HR:3 * HR], m_.rearrange("p (c r) -> p c r", r=HR),
                                    rv[:, :, HR:2 * HR], ALU.subtract).then_inc(idx.sem, 1)
            link(nc.vector.tensor_copy(mxs, i0[:, 0:H]))

        def rest_part(g, b):
            v.wait_ge(kvh.sem, kvh.at(g, b + 1))
            v.wait_ge(kvl.sem, kvl.at(g, 2 * b))
            nc.vector.tensor_tensor(kvr, bank[2] if b == 0 else bank[7], kvs[b % 2][:, 0:GT], ALU.subtract) \
                .then_inc(kvd.sem, 1)

        def onehot(g, n):
            v.wait_ge(bc.sem, bc.at(g, n + 1))
            v.wait_ge(gat.sem, gat.at(g, n - 3))
            nc.vector.tensor_scalar(oh[n % 4], bank[n % 3], 0.0, None, ALU.max).then_inc(rlv.sem, 1)

        def key_products(g, b, c, ch):
            v.wait_ge(gat.sem, gat.at(g, b * QUADS + (c + 1) * QC))
            v.wait_ge(pc.sem, pc.at(g, 2))
            g4 = G2[c % 2].rearrange("p (h r e) -> p h r e", h=4, e=2 * DH)[:, :, :, 0:DH]
            q4 = qn[:, b * P + c * 4 * DH:b * P + (c + 1) * 4 * DH].rearrange("p (h e) -> p h e", h=4)
            nc.vector.tensor_tensor(prod.rearrange("p (h r e) -> p h r e", h=4, e=DH), g4,
                                    q4.unsqueeze(2).to_broadcast([P, 4, 2 * NK, DH]), ALU.mult).then_inc(kp.sem, 1)
            v.wait_ge(kp.sem, kp.at(g, b * CH + c + 1))
            ch.link(nc.vector.tensor_reduce(sp_[:, b % 2 * 2 * R + c * 8 * NK:b % 2 * 2 * R + (c + 1) * 8 * NK],
                                            prod.rearrange("p (r e) -> p r e", e=DH), X, ALU.add))

        def scores(g, b, ch):
            ch.link(nc.vector.tensor_tensor(s2, sp_[:, b % 2 * 2 * R:(b % 2 + 1) * 2 * R],
                                            w01[:, b * 2 * R:(b + 1) * 2 * R], ALU.mult))
            ch.link(nc.vector.tensor_reduce(sc, s2.rearrange("p (r i) -> p r i", i=2), X, ALU.add))
            ch.link(nc.vector.tensor_reduce(mxs, sc.rearrange("p (h k) -> p h k", k=NK), X, ALU.max))
            s3 = sc.rearrange("p (h k) -> p h k", k=NK)
            nc.vector.tensor_tensor(s3, s3, mxs.unsqueeze(2).to_broadcast([P, H, NK]), ALU.subtract) \
                .then_inc(scd.sem, 1)

        def weights(g, b, ch):
            v.wait_ge(exd.sem, exd.at(g, b + 1))
            e3 = ee.rearrange("p (h k) -> p h k", k=NK)
            ch.link(nc.vector.tensor_reduce(sm, e3, X, ALU.add))
            ch.link(nc.vector.reciprocal(sm, sm))
            ch.link(nc.vector.tensor_tensor(pw.rearrange("p (h k) -> p h k", k=NK), e3,
                                            sm.unsqueeze(2).to_broadcast([P, H, NK]), ALU.mult))
            nc.vector.scalar_tensor_tensor(aw.rearrange("p (r i) -> p r i", i=2),
                                           w01[:, b * 2 * R:(b + 1) * 2 * R].rearrange("p (r i) -> p r i", i=2), 0.5,
                                           pw.unsqueeze(2).to_broadcast([P, R, 2]), ALU.mult, ALU.mult) \
                .then_inc(awd.sem, 1)

        def sum_values(g, b):
            v.wait_ge(vpd.sem, vpd.at(g, b + 1))
            v.wait_ge(cxt.sem, cxt.at(g, b))
            nc.vector.tensor_reduce(cx.rearrange("p (h e) -> p h e", h=H),
                                    pv.rearrange("p (h r e) -> p h e r", h=H, e=DH), X, ALU.add).then_inc(cxd.sem, 1)

        def update(g, b):
            v.wait_ge(yd.sem, yd.at(g, b + 1))
            xs = x[:, ds((g * GB + b) * P, P)]
            nc.vector.tensor_tensor(xs, xs, bank[7][:, P:2 * P], ALU.add).then_inc(xd.sem, 1)

        with v.Fori(0, G) as g:
            c = Chain(v, chain, g)
            rest_part(g, 0)
            find_places(g, c)
            for s in range(GB + 2):
                b = s
                if s < GB:
                    onehot(g, b * QUADS + 3)
                if 1 <= s <= GB:
                    scores(g, s - 1, c)
                if s < GB:
                    key_products(g, b, 0, c)
                    onehot(g, b * QUADS + 7)
                if s >= 2:
                    update(g, s - 2)
                if 1 <= s <= GB:
                    weights(g, s - 1, c)
                if s < GB:
                    key_products(g, b, 1, c)
                    onehot(g, b * QUADS + 11)
                    if s + 1 < GB:
                        rest_part(g, s + 1)
                    key_products(g, b, 2, c)
                    onehot(g, b * QUADS + 15)
                if 1 <= s <= GB:
                    sum_values(g, s - 1)
                if s < GB:
                    onehot(g, b * QUADS + 19)
                    key_products(g, b, 3, c)
            c.close()

    return dict(sp=sp, pool=pool, dve=dve, pe=pe, act=act), [(xd.sem, xd.at(G, 0))]


def stage_attention2(core, arena, start):
    nc, d, bank = core.nc, core.dram, core.bank
    x, xnT = core.x, core.xnT
    DH = 64
    TILES = H * DH // P
    QUADS = H // 4
    SCALE = DH ** -0.5
    E1 = DH + 1
    w = arena.take(4 * TILES * P)
    wq, wk, wv, wo = (w[:, i * TILES * P:(i + 1) * TILES * P] for i in range(4))
    lnp = arena.take(4)
    shift, gain = arena.take(B * TILES), arena.take(B * TILES)
    nat_buf, cnT = arena.take(B * P), arena.take(B * P)
    qT, kT = arena.take(TILES * GT), arena.take(TILES * GT)
    cT = arena.take(GT)
    vaug = arena.take(GB * H * E1).rearrange("p (b h e) -> p b h e", b=GB, h=H)
    nm = arena.take(2 * H)
    nm2 = [arena.take(P, BF16) for _ in range(2)]
    nmT = [arena.take(P, BF16) for _ in range(2)]
    pT = [arena.take(GT) for _ in range(2)]
    rsum = arena.take(2 * 4)
    ao, aoT = [arena.take(H * DH) for _ in range(2)], arena.take(H * DH)

    def head(q, i):
        return q // 2 * 8 + 2 * i + q % 2

    def rows_of(buf, h, b):
        part = slice(h % 2 * DH, h % 2 * DH + DH)
        return buf[part, h // 2 * GT + b * P:h // 2 * GT + (b + 1) * P]

    w_in, ctx_in, set_, gain_set = (core.sem(f"a2_{n}") for n in ("w_in", "ctx_in", "set", "gain_set"))
    ln_ctx, ctx_done = layernorm(core, nat_buf, [(ctx_in, 16), (w_in, 48)] + start, dst_t=cnT,
                                 t_scale=lnp[:, 0:1], t_bias=lnp[:, 1:2])
    ln_x, x_done = layernorm(core, x, [ctx_done], dst_natural=nat_buf)
    ln_xx, xx_done = layernorm(core, nat_buf, [x_done], dst_t=xnT, t_scale=lnp[:, 2:3], t_bias=lnp[:, 3:4])
    pj = core.counter("a2_pj", 3 * TILES)
    qd = core.counter("a2_qd", TILES)
    kvc = core.counter("a2_kvc", 2 * TILES)
    ct = core.counter("a2_ct", GB)
    nat = core.counter("a2_nat", GB * QUADS)
    mx = core.counter("a2_mx", GB * QUADS)
    nms = core.counter("a2_nms", GB)
    nmt = core.counter("a2_nmt", GB)
    nmc = core.counter("a2_nmc", GB)
    st = core.counter("a2_st", GB * QUADS)
    ex = core.counter("a2_ex", GB * QUADS)
    av = core.counter("a2_av", GB * QUADS)
    aon = core.counter("a2_aon", GB * QUADS)
    aot = core.counter("a2_aot", GB * 2)
    aoc = core.counter("a2_aoc", GB * 2)
    yd = core.counter("a2_yd", GB)
    xd = core.counter("a2_xd", GB)
    chain = core.counter("a2_chain", GB * (1 + QUADS))

    def sp(s):
        for sem, n in start:
            s.wait_ge(sem, n)
        s.dma_start(w, d["a2_w"]).then_inc(w_in, 16)
        s.dma_start(lnp, d["a2_ln"]).then_inc(w_in, 16)
        s.dma_start(shift, d["a2_shift"]).then_inc(w_in, 16)
        s.dma_start(nat_buf.rearrange("p (b d) -> p b d", d=P), d["ctx"].rearrange("b p d -> p b d")) \
            .then_inc(ctx_in, 16)

    def pool(p):
        for sem, n in start:
            p.wait_ge(sem, n)
        nc.gpsimd.memset(vaug[:, :, :, DH:E1], 1.0).then_inc(set_, 1)
        for t in nm2:
            nc.gpsimd.memset(t, 0.0).then_inc(set_, 1)
        for f in (ln_ctx, ln_x, ln_xx):
            f["pool"](p)
        p.wait_ge(*ctx_done)
        with p.Fori(0, G) as g:
            for b in range(GB):
                p.wait_ge(pj.sem, pj.at(g, 2 * b - 2 * GB + 2))
                nc.gpsimd.tensor_copy(cT[:, b * P:(b + 1) * P], cnT[:, ds((g * GB + b) * P, P)]).then_inc(ct.sem, 1)

    def dve(v):
        for f in (ln_ctx, ln_x, ln_xx):
            f["dve"](v)
        v.wait_ge(set_, 3)
        nc.vector.tensor_scalar(gain, shift, 1.0, None, ALU.add).then_inc(gain_set, 1)
        v.wait_ge(gain_set, 1)

        def scale_q(g, t):
            v.wait_ge(pj.sem, pj.at(g, t + 1))
            if t == 0:
                v.wait_ge(st.sem, st.at(g, 0))
            for b in range(GB):
                col = (g * GB + b) * TILES + t
                ins = nc.vector.tensor_scalar(qT[:, t * GT + b * P:t * GT + (b + 1) * P],
                                              bank[t % 4][:, b * P:(b + 1) * P], gain[:, ds(col, 1)],
                                              shift[:, ds(col, 1)], ALU.mult, ALU.add)
            ins.then_inc(qd.sem, 1)

        def row_max(g, b, c):
            n = nm[:, b % 2 * H:b % 2 * H + H]
            for q in range(QUADS):
                v.wait_ge(nat.sem, nat.at(g, b * QUADS + q + 1))
                nc.vector.tensor_reduce(n[:, q * 4:q * 4 + 4], bank[q % 2].rearrange("p (h k) -> p h k", h=4),
                                        X, ALU.max, negate=True).then_inc(mx.sem, 1)
            v.wait_ge(nmt.sem, nmt.at(g, b - 1))
            v.wait_ge(mx.sem, mx.at(g, (b + 1) * QUADS))
            c.link(nc.vector.tensor_copy(nm2[b % 2][:, 0:H], n))
            nc.vector.tensor_tensor(nm2[b % 2][:, H:2 * H], n, nm2[b % 2][:, 0:H], ALU.subtract) \
                .then_inc(nms.sem, 1)

        def normalise(g, b, q, c):
            n = b * QUADS + q
            v.wait_ge(av.sem, av.at(g, n + 1))
            o = bank[4 + q % 2][:, 0:4 * E1].rearrange("p (h e) -> p h e", h=4)
            r = rsum[:, q % 2 * 4:q % 2 * 4 + 4]
            c.link(nc.vector.reciprocal(r, o[:, :, DH]))
            if q == 0:
                v.wait_ge(aot.sem, aot.at(g, 2 * (b - 1)))
            out = ao[b % 2].rearrange("p (o i s e) -> p o i s e", o=2, i=4, s=2)[:, q // 2, :, q % 2, :]
            nc.vector.tensor_tensor(out, o[:, :, 0:DH], r.unsqueeze(2).to_broadcast([P, 4, DH]), ALU.mult) \
                .then_inc(aon.sem, 1)

        def update(g, b):
            v.wait_ge(yd.sem, yd.at(g, b + 1))
            xs = x[:, ds((g * GB + b) * P, P)]
            nc.vector.tensor_tensor(xs, xs, bank[7][:, 2 * P:3 * P], ALU.add).then_inc(xd.sem, 1)

        with v.Fori(0, G) as g:
            c = Chain(v, chain, g)
            for t in range(TILES):
                scale_q(g, t)
            row_max(g, 0, c)
            for b in range(GB):
                if b + 1 < GB:
                    row_max(g, b + 1, c)
                for q in range(QUADS):
                    normalise(g, b, q, c)
                if b > 0:
                    update(g, b - 1)
            update(g, GB - 1)
            c.close()

    def pe(t):
        for f in (ln_ctx, ln_xx):
            f["pe"](t)
        t.wait_ge(*xx_done)

        def natural(g, b):
            for q in range(QUADS):
                t.wait_ge(mx.sem, mx.at(g, b * QUADS + q - 1))
                for i in range(4):
                    h = head(q, i)
                    ins = nc.tensor.matmul(bank[q % 2][:, i * P:(i + 1) * P], rows_of(qT, h, b), rows_of(kT, h, b),
                                           start=True, stop=True)
                ins.then_inc(nat.sem, 1)

        def turn_max(g, b):
            t.wait_ge(nms.sem, nms.at(g, b + 1))
            t.wait_ge(nmc.sem, nmc.at(g, b))
            t.wait_ge(xd.sem, xd.at(g, max(b - 2, 0)))
            nc.tensor.transpose(bank[7][:, 0:P // 2].bitcast(BF16), nm2[b % 2], core.ident_b).then_inc(nmt.sem, 1)

        def attend(g, b):
            def av_quad(q):
                n = b * QUADS + q
                t.wait_ge(ex.sem, ex.at(g, n + 1))
                t.wait_ge(aon.sem, aon.at(g, n - 1))
                for i in range(4):
                    ins = nc.tensor.matmul(bank[4 + q % 2][:, i * E1:(i + 1) * E1], pT[q % 2][:, i * P:(i + 1) * P],
                                           vaug[:, b, head(q, i), :], start=True, stop=True)
                ins.then_inc(av.sem, 1)

            t.wait_ge(nmc.sem, nmc.at(g, b + 1))
            for q in range(QUADS):
                n = b * QUADS + q
                t.wait_ge(ex.sem, ex.at(g, n - 1))
                for i in range(4):
                    h = head(q, i)
                    out = bank[2 + q % 2][:, i * P:(i + 1) * P]
                    nc.tensor.matmul(out, rows_of(kT, h, b), rows_of(qT, h, b), start=True, stop=False)
                    k = q * 4 + i
                    ins = nc.tensor.matmul(out, core.sel_head[:, k * P:(k + 1) * P], nmT[b % 2],
                                           start=False, stop=True)
                ins.then_inc(st.sem, 1)
                if q:
                    av_quad(q - 1)
            av_quad(QUADS - 1)

        def project_out(g, b):
            t.wait_ge(aon.sem, aon.at(g, (b + 1) * QUADS))
            for half in range(2):
                t.wait_ge(aoc.sem, aoc.at(g, 2 * b + half))
                for i in range(4):
                    k = half * 4 + i
                    ins = nc.tensor.transpose(bank[6][:, i * P:(i + 1) * P], ao[b % 2][:, k * P:(k + 1) * P], core.ident)
                ins.then_inc(aot.sem, 1)
            t.wait_ge(aoc.sem, aoc.at(g, 2 * b + 2))
            t.wait_ge(nmc.sem, nmc.at(g, min(b + 2, GB)))
            t.wait_ge(xd.sem, xd.at(g, b))
            for k in range(TILES):
                ins = nc.tensor.matmul(bank[7][:, 2 * P:3 * P], aoT[:, k * P:(k + 1) * P], wo[:, k * P:(k + 1) * P],
                                       start=k == 0, stop=k == TILES - 1)
            ins.then_inc(yd.sem, 1)

        with t.Fori(0, G) as g:
            t.wait_ge(mx.sem, mx.at(g, 0))
            t.wait_ge(ex.sem, ex.at(g, 0))
            for k in range(TILES):
                if k >= 4:
                    t.wait_ge(qd.sem, qd.at(g, k - 3))
                nc.tensor.matmul(bank[k % 4], wq[:, k * P:(k + 1) * P], xnT[:, ds(g * GT, GT)], start=True, stop=True) \
                    .then_inc(pj.sem, 1)
            for k in range(TILES):
                if k < 4:
                    t.wait_ge(qd.sem, qd.at(g, TILES - 3 + k))
                else:
                    t.wait_ge(kvc.sem, kvc.at(g, k - 3))
                nc.tensor.matmul(bank[k % 4], wk[:, k * P:(k + 1) * P], cnT[:, ds(g * GT, GT)], start=True, stop=True) \
                    .then_inc(pj.sem, 1)
            for b in range(GB):
                t.wait_ge(ct.sem, ct.at(g, b + 1))
                for half in range(2):
                    k = b * 2 + half
                    t.wait_ge(kvc.sem, kvc.at(g, TILES + k - 3))
                    nc.tensor.matmul(bank[k % 4], cT[:, b * P:(b + 1) * P], wv[:, half * GT:(half + 1) * GT],
                                     start=True, stop=True).then_inc(pj.sem, 1)
            t.wait_ge(kvc.sem, kvc.at(g, 2 * TILES))
            natural(g, 0)
            turn_max(g, 0)
            for b in range(GB):
                if b + 1 < GB:
                    natural(g, b + 1)
                attend(g, b)
                if b + 1 < GB:
                    turn_max(g, b + 1)
                if b > 0:
                    project_out(g, b - 1)
            project_out(g, GB - 1)

    def act(a):
        for f in (ln_ctx, ln_xx):
            f["act"](a)
        a.wait_ge(set_, 3)

        def copy_max(g, b):
            a.wait_ge(nmt.sem, nmt.at(g, b + 1))
            a.wait_ge(st.sem, st.at(g, (b - 1) * QUADS))
            nc.scalar.activation(nmT[b % 2], bank[7][:, 0:P // 2].bitcast(BF16), ACT.Copy).then_inc(nmc.sem, 1)

        def exps(g, b):
            for q in range(QUADS):
                n = b * QUADS + q
                a.wait_ge(st.sem, st.at(g, n + 1))
                a.wait_ge(av.sem, av.at(g, n - 1))
                nc.scalar.activation(pT[q % 2], bank[2 + q % 2], ACT.Exp, scale=SCALE).then_inc(ex.sem, 1)

        def copy_ao(g, b):
            for half in range(2):
                a.wait_ge(aot.sem, aot.at(g, 2 * b + half + 1))
                a.wait_ge(yd.sem, yd.at(g, b))
                nc.scalar.activation(aoT[:, half * GT:(half + 1) * GT], bank[6], ACT.Copy).then_inc(aoc.sem, 1)

        with a.Fori(0, G) as g:
            a.wait_ge(st.sem, st.at(g, 0))
            for k in range(TILES):
                a.wait_ge(pj.sem, pj.at(g, TILES + k + 1))
                nc.scalar.activation(kT[:, k * GT:(k + 1) * GT], bank[k % 4], ACT.Copy).then_inc(kvc.sem, 1)
            a.wait_ge(av.sem, av.at(g, 0))
            for k in range(TILES):
                b, half = divmod(k, 2)
                a.wait_ge(pj.sem, pj.at(g, 2 * TILES + k + 1))
                nc.scalar.activation(vaug[:, b, half * H // 2:(half + 1) * H // 2, 0:DH],
                                     bank[k % 4].rearrange("p (h e) -> p h e", e=DH), ACT.Copy).then_inc(kvc.sem, 1)
            copy_max(g, 0)
            for b in range(GB):
                exps(g, b)
                if b + 1 < GB:
                    copy_max(g, b + 1)
                if b > 0:
                    copy_ao(g, b - 1)
            copy_ao(g, GB - 1)

    return dict(sp=sp, pool=pool, dve=dve, pe=pe, act=act), [(xd.sem, xd.at(G, 0))]


def stage_attention3(core, arena, start):
    nc, d, bank = core.nc, core.dram, core.bank
    x, xnT, ctxT = core.x, core.xnT, core.ctxT
    C1 = P + 1
    w, bqk = arena.take(2 * P), arena.take(2)
    ctxa = arena.take(B * C1)
    qT, kT, pT = arena.take(GT), arena.take(GT), arena.take(GT)
    nm, rsum = arena.take(GB), arena.take(GB)
    nm2, nmT = arena.take(GB * P, BF16), arena.take(GB * P, BF16)

    fns, ln_done = layernorm(core, x, start, dst_t=xnT)
    w_in, set_ = core.sem("a3_w_in"), core.sem("a3_set")
    pj = core.counter("a3_pj", 2)
    pc = core.counter("a3_pc", 2)
    nat = core.counter("a3_nat", 1)
    nms = core.counter("a3_nms", 1)
    nmt = core.counter("a3_nmt", 1)
    nmc = core.counter("a3_nmc", 1)
    st = core.counter("a3_st", 1)
    ex = core.counter("a3_ex", 1)
    av = core.counter("a3_av", 2)
    xd = core.counter("a3_xd", 2)
    chain = core.counter("a3_chain", 4)

    def sp(s):
        for sem, n in start:
            s.wait_ge(sem, n)
        s.dma_start(w, d["a3_w"]).then_inc(w_in, 16)
        s.dma_start(bqk, d["a3_bqk"]).then_inc(w_in, 16)
        s.dma_start(ctxa.rearrange("p (b e) -> p b e", e=C1)[:, :, 0:P], d["ctx"].rearrange("b p d -> p b d")) \
            .then_inc(w_in, 16)

    def pool(p):
        for sem, n in start:
            p.wait_ge(sem, n)
        nc.gpsimd.memset(ctxa.rearrange("p (b e) -> p b e", e=C1)[:, :, P:C1], 1.0).then_inc(set_, 1)
        nc.gpsimd.memset(nm2, 0.0).then_inc(set_, 1)
        fns["pool"](p)

    def pe(t):
        fns["pe"](t)
        t.wait_ge(w_in, 48)
        t.wait_ge(set_, 2)
        t.wait_ge(*ln_done)
        with t.Fori(0, G) as g:
            t.wait_ge(pc.sem, pc.at(g, 0))
            nc.tensor.matmul(bank[0], w[:, 0:P], xnT[:, ds(g * GT, GT)], start=True, stop=True).then_inc(pj.sem, 1)
            nc.tensor.matmul(bank[1], w[:, P:2 * P], ctxT[:, ds(g * GT, GT)], start=True, stop=True) \
                .then_inc(pj.sem, 1)
            t.wait_ge(pc.sem, pc.at(g, 2))
            t.wait_ge(nms.sem, nms.at(g, 0))
            for b in range(GB):
                cols = slice(b * P, (b + 1) * P)
                ins = nc.tensor.matmul(bank[2][:, cols], qT[:, cols], kT[:, cols], start=True, stop=True)
            ins.then_inc(nat.sem, 1)
            t.wait_ge(nms.sem, nms.at(g, 1))
            for b in range(GB):
                cols = slice(b * P, (b + 1) * P)
                ins = nc.tensor.transpose(bank[3].bitcast(BF16)[:, cols], nm2[:, cols], core.ident_b)
            ins.then_inc(nmt.sem, 1)
            t.wait_ge(nmc.sem, nmc.at(g, 1))
            for b in range(GB):
                cols = slice(b * P, (b + 1) * P)
                nc.tensor.matmul(bank[4][:, cols], kT[:, cols], qT[:, cols], start=True, stop=False)
                ins = nc.tensor.matmul(bank[4][:, cols], core.sel_head[:, 0:P], nmT[:, cols], start=False, stop=True)
            ins.then_inc(st.sem, 1)
            t.wait_ge(ex.sem, ex.at(g, 1))
            for pair in range(2):
                t.wait_ge(xd.sem, xd.at(g, pair - 1))
                for i in range(2):
                    b = pair * 2 + i
                    ins = nc.tensor.matmul(bank[5 + pair][:, i * C1:(i + 1) * C1], pT[:, b * P:(b + 1) * P],
                                           ctxa[:, ds((g * GB + b) * C1, C1)], start=True, stop=True)
                ins.then_inc(av.sem, 1)

    def act(a):
        fns["act"](a)
        a.wait_ge(w_in, 48)
        with a.Fori(0, G) as g:
            a.wait_ge(st.sem, st.at(g, 0))
            for i, dst in enumerate((qT, kT)):
                a.wait_ge(pj.sem, pj.at(g, i + 1))
                nc.scalar.activation(dst, bank[i], ACT.Identity, bias=bqk[:, i:i + 1]).then_inc(pc.sem, 1)
            a.wait_ge(nmt.sem, nmt.at(g, 1))
            nc.scalar.activation(nmT, bank[3].bitcast(BF16)[:, 0:GT], ACT.Copy).then_inc(nmc.sem, 1)
            a.wait_ge(st.sem, st.at(g, 1))
            a.wait_ge(av.sem, av.at(g, 0))
            nc.scalar.activation(pT, bank[4], ACT.Exp).then_inc(ex.sem, 1)

    def dve(v):
        fns["dve"](v)
        v.wait_ge(set_, 2)
        n3 = nm2.rearrange("p (b r) -> p b r", b=GB)
        with v.Fori(0, G) as g:
            c = Chain(v, chain, g)
            v.wait_ge(nat.sem, nat.at(g, 1))
            c.link(nc.vector.tensor_reduce(nm, bank[2].rearrange("p (b k) -> p b k", b=GB), X, ALU.max, negate=True))
            c.link(nc.vector.tensor_copy(n3[:, :, 0], nm))
            nc.vector.tensor_tensor(n3[:, :, H], nm, n3[:, :, 0], ALU.subtract).then_inc(nms.sem, 1)
            for pair in range(2):
                v.wait_ge(av.sem, av.at(g, pair + 1))
                o = bank[5 + pair][:, 0:2 * C1].rearrange("p (b e) -> p b e", b=2)
                c.link(nc.vector.reciprocal(rsum[:, pair * 2:pair * 2 + 2], o[:, :, P]))
                for i in range(2):
                    b = pair * 2 + i
                    xs = x[:, ds((g * GB + b) * P, P)]
                    ins = nc.vector.scalar_tensor_tensor(xs, o[:, i, 0:P], rsum[:, b:b + 1], xs, ALU.mult, ALU.add)
                ins.then_inc(xd.sem, 1)
            c.close()

    return dict(sp=sp, pool=pool, dve=dve, pe=pe, act=act), [(xd.sem, xd.at(G, 0))]


class Router:

    def __init__(self, core, arena, tag, experts, links, steps):
        self.core, self.e, self.steps = core, experts, steps
        n = GB * experts
        self.logit, self.gt, self.eq, self.cum, self.comb, self.val, self.tmp = (arena.take(n) for _ in range(7))
        self.top = arena.take(GB * 8 * 8)
        self.small = arena.take(GB * 8 * 4)
        self.reset = arena.take(n)
        self.pad = arena.take(1)
        self.asked = core.counter(f"{tag}_asked", steps)
        self.answered = core.counter(f"{tag}_answered", steps)
        self.chain = core.counter(f"{tag}_chain", links)

    def hold(self):
        self.core.nc.vector.memset(self.pad, 0.0)

    def largest(self, c, sel, values, threshold, k, e):
        nc = self.core.nc
        v3 = lambda a: a[:, 0:GB * e].rearrange("p (b e) -> p b e", e=e)
        thr = threshold.unsqueeze(2).to_broadcast([P, GB, e])
        left = self.small[:, 0:GB]
        nc.vector.tensor_tensor(v3(self.eq), values, thr, ALU.is_equal)
        c.link(nc.vector.tensor_tensor(v3(self.gt), values, thr, ALU.is_gt))
        nc.vector.tensor_tensor_scan(self.cum[:, 0:GB * e], self.reset8 if e == 8 else self.reset,
                                     self.eq[:, 0:GB * e], 0.0, ALU.mult, ALU.add)
        c.link(nc.vector.tensor_reduce(left, v3(self.gt), X, ALU.add))
        c.link(nc.vector.tensor_scalar(left, left, -1.0, float(k), ALU.mult, ALU.add))
        c.link(nc.vector.tensor_tensor(v3(self.cum), v3(self.cum), left.unsqueeze(2).to_broadcast([P, GB, e]),
                                       ALU.is_le))
        c.link(nc.vector.tensor_tensor(self.cum[:, 0:GB * e], self.cum[:, 0:GB * e], self.eq[:, 0:GB * e], ALU.mult))
        c.link(nc.vector.tensor_tensor(sel, v3(self.cum), v3(self.gt), ALU.add))


class Top2Softmax(Router):

    def __init__(self, core, arena, tag):
        super().__init__(core, arena, tag, 8, 13, 1)
        self.reset8 = self.reset

    def dve(self, v, g, psum):
        nc, c = self.core.nc, Chain(v, self.chain, g)
        v3 = lambda a: a.rearrange("p (b e) -> p b e", e=8)
        top, w = v3(self.top[:, 0:GB * 8]), self.small[:, GB:3 * GB]
        c.link(nc.vector.tensor_copy(self.logit, psum))
        self.hold()
        for b in range(GB):
            ins = nc.vector.max(top[:, b, :], v3(self.logit)[:, b, :])
        c.link(ins)
        nc.vector.tensor_tensor(self.small[:, 3 * GB:4 * GB], top[:, :, 0], top[:, :, 1], ALU.subtract) \
            .then_inc(self.asked.sem, 1)
        self.largest(c, v3(self.val), v3(self.logit), top[:, :, 1], 2, 8)
        v.wait_ge(self.answered.sem, self.answered.at(g, 1))
        w1, w2 = w[:, 0:GB], w[:, GB:2 * GB]
        bc = lambda a: a.unsqueeze(2).to_broadcast([P, GB, 8])
        c.link(nc.vector.tensor_tensor(w1, w1, w2, ALU.subtract))
        c.link(nc.vector.tensor_tensor(v3(self.tmp), v3(self.logit), bc(top[:, :, 0]), ALU.is_equal))
        c.link(nc.vector.tensor_tensor(v3(self.tmp), v3(self.tmp), bc(w1), ALU.mult))
        c.link(nc.vector.tensor_tensor(v3(self.tmp), v3(self.tmp), bc(w2), ALU.add))
        c.link(nc.vector.tensor_tensor(self.comb, self.tmp, self.val, ALU.mult))
        c.close()

    def act(self, a, g):
        nc, w = self.core.nc, self.small[:, GB:3 * GB]
        dm = self.small[:, 3 * GB:4 * GB]
        a.wait_ge(self.asked.sem, self.asked.at(g, 1))
        nc.scalar.activation(w[:, 0:GB], dm, ACT.Sigmoid)
        nc.scalar.activation(w[:, GB:2 * GB], dm, ACT.Sigmoid, scale=-1.0).then_inc(self.answered.sem, 1)


class Top1Softmax(Router):

    def __init__(self, core, arena, tag):
        super().__init__(core, arena, tag, 8, 12, 1)
        self.reset8 = self.reset

    def dve(self, v, g, psum):
        nc, c = self.core.nc, Chain(v, self.chain, g)
        v3 = lambda a: a.rearrange("p (b e) -> p b e", e=8)
        top, total = v3(self.top[:, 0:GB * 8]), self.small[:, GB:2 * GB]
        bc = lambda a: a.unsqueeze(2).to_broadcast([P, GB, 8])
        c.link(nc.vector.tensor_copy(self.logit, psum))
        self.hold()
        for b in range(GB):
            ins = nc.vector.max(top[:, b, :], v3(self.logit)[:, b, :])
        c.link(ins)
        nc.vector.tensor_tensor(v3(self.tmp), v3(self.logit), bc(top[:, :, 0]), ALU.subtract) \
            .then_inc(self.asked.sem, 1)
        self.largest(c, v3(self.val), v3(self.logit), top[:, :, 0], 1, 8)
        v.wait_ge(self.answered.sem, self.answered.at(g, 1))
        c.link(nc.vector.tensor_reduce(total, v3(self.tmp), X, ALU.add))
        c.link(nc.vector.reciprocal(total, total))
        c.link(nc.vector.tensor_tensor(v3(self.comb), v3(self.val), bc(total), ALU.mult))
        c.link(nc.vector.tensor_copy(total, total))
        c.close()

    def act(self, a, g):
        a.wait_ge(self.asked.sem, self.asked.at(g, 1))
        self.core.nc.scalar.activation(self.tmp, self.tmp, ACT.Exp).then_inc(self.answered.sem, 1)


class GroupedTop8(Router):

    def __init__(self, core, arena, tag):
        super().__init__(core, arena, tag, 64, 24, 1)
        self.bias, self.reset8 = arena.take(64), arena.take(GB * 8)
        self.groups = arena.take(GB * 8 * 2)
        self.in_ = core.sem(f"{tag}_router_in")

    def dve(self, v, g, psum):
        nc, c = self.core.nc, Chain(v, self.chain, g)
        score, choice, masked, sel = self.logit, self.val, self.tmp, self.comb
        v3 = lambda a: a.rearrange("p (b e) -> p b e", e=64)
        v8 = lambda a: a.rearrange("p (g e) -> p g e", e=8)
        b8 = lambda a: a.rearrange("p (b g) -> p b g", g=8)
        v.wait_ge(self.answered.sem, self.answered.at(g, 1))
        c.link(nc.vector.tensor_tensor(v3(choice), v3(score), self.bias.unsqueeze(1).to_broadcast([P, GB, 64]),
                                       ALU.add))
        top, gs, gsel = v8(self.top), self.groups[:, 0:GB * 8], self.groups[:, GB * 8:]
        self.hold()
        for i in range(GB * 8):
            ins = nc.vector.max(top[:, i, :], v8(choice)[:, i, :])
        c.link(ins)
        c.link(nc.vector.tensor_tensor(gs, top[:, :, 0], top[:, :, 1], ALU.add))
        self.hold()
        for b in range(GB):
            ins = nc.vector.max(top[:, b, :], b8(gs)[:, b, :])
        c.link(ins)
        self.largest(c, b8(gsel), b8(gs), top[:, 0:GB, 3], 4, 8)
        c.link(nc.vector.tensor_tensor(v8(masked), v8(choice), gsel.unsqueeze(2).to_broadcast([P, GB * 8, 8]),
                                       ALU.mult))
        self.hold()
        for b in range(GB):
            ins = nc.vector.max(top[:, b, :], v3(masked)[:, b, :])
        c.link(ins)
        self.largest(c, v3(sel), v3(masked), top[:, 0:GB, 7], 8, 64)
        c.link(nc.vector.tensor_tensor(sel, sel, score, ALU.mult))
        total = self.small[:, GB:2 * GB]
        c.link(nc.vector.tensor_reduce(total, v3(sel), X, ALU.add))
        c.link(nc.vector.tensor_scalar(total, total, 1e-20, None, ALU.add))
        c.link(nc.vector.reciprocal(total, total))
        c.link(nc.vector.tensor_scalar(total, total, 2.5, None, ALU.mult))
        c.link(nc.vector.tensor_tensor(v3(sel), v3(sel), total.unsqueeze(2).to_broadcast([P, GB, 64]), ALU.mult))
        c.close()

    def act(self, a, g, psum, ready, free):
        nc = self.core.nc
        a.wait_ge(*ready)
        a.wait_ge(*free)
        nc.scalar.activation(self.logit, psum, ACT.Sigmoid).then_inc(self.answered.sem, 1)


def stage_experts(tag, make_router, experts, shared, tiles, rows, router_bias=None):

    def stage(core, arena, start):
        nc, d, bank = core.nc, core.dram, core.bank
        x, xnT = core.x, core.xnT
        E = experts + shared
        up = arena.take(E * 2 * tiles * rows)
        down = arena.take(E * tiles * P)
        gate_w = arena.take(experts)
        xT = arena.take(GT)
        sg = [arena.take(GT) for _ in range(2)]
        h = [arena.take(GT) for _ in range(2 * tiles)]
        router = make_router(core, arena, tag)
        own_scores = isinstance(router, GroupedTop8)
        U = E * tiles

        fns, ln_done = layernorm(core, x, start, dst_t=xnT)
        w_in = core.sem(f"{tag}_w_in")
        ct = core.counter(f"{tag}_ct", GB)
        lg = core.counter(f"{tag}_lg", 1)
        rt = core.counter(f"{tag}_rt", 1)
        ud = core.counter(f"{tag}_ud", 2 * U)
        sd = core.counter(f"{tag}_sd", U)
        hd = core.counter(f"{tag}_hd", U)
        yd = core.counter(f"{tag}_yd", E)
        xd = core.counter(f"{tag}_xd", E)

        def sp(s):
            for sem, n in start:
                s.wait_ge(sem, n)
            s.dma_start(up, d[f"{tag}_up"]).then_inc(w_in, 16)
            s.dma_start(down[0:rows], d[f"{tag}_down"]).then_inc(w_in, 16)
            s.dma_start(gate_w, d[f"{tag}_gate"]).then_inc(w_in, 16)
            s.dma_start(router.reset, d["reset"][:, 0:GB * 8] if experts == 8 else d["reset64"]).then_inc(w_in, 16)
            if own_scores:
                s.dma_start(router.bias, d[f"{tag}_bias"]).then_inc(w_in, 16)
                s.dma_start(router.reset8, d["reset"][:, 0:GB * 8]).then_inc(w_in, 16)

        loads = 16 * (6 if own_scores else 4)
        logits = bank[6][:, 0:GB * experts]

        def pool(p):
            fns["pool"](p)
            p.wait_ge(*ln_done)
            with p.Fori(0, G) as g:
                for b in range(GB):
                    p.wait_ge(lg.sem, lg.at(g, 0))
                    nc.gpsimd.tensor_copy(xT[:, b * P:(b + 1) * P], xnT[:, ds((g * GB + b) * P, P)]) \
                        .then_inc(ct.sem, 1)

        def pe(t):
            fns["pe"](t)
            t.wait_ge(w_in, loads)
            t.wait_ge(*ln_done)

            def unit(g, u):
                for k in range(2):
                    if k == 0:
                        t.wait_ge(hd.sem, hd.at(g, u - 1))
                    col = (u // tiles * 2 * tiles + k * tiles + u % tiles) * rows
                    nc.tensor.matmul(bank[u % 2 * 2 + k][0:rows, :], up[:, col:col + rows],
                                     xnT[:, ds(g * GT, GT)], start=True, stop=True).then_inc(ud.sem, 1)

            def output(g, e):
                t.wait_ge(hd.sem, hd.at(g, (e + 1) * tiles))
                t.wait_ge(xd.sem, xd.at(g, e - 1))
                for b in range(GB):
                    for k in range(tiles):
                        hk = h[e % 2 * tiles + k]
                        ins = nc.tensor.matmul(bank[4 + e % 2][:, b * P:(b + 1) * P], hk[0:rows, b * P:(b + 1) * P],
                                               down[0:rows, (e * tiles + k) * P:(e * tiles + k + 1) * P],
                                               start=k == 0, stop=k == tiles - 1)
                ins.then_inc(yd.sem, 1)

            with t.Fori(0, G) as g:
                t.wait_ge(rt.sem, rt.at(g, 0))
                for b in range(GB):
                    t.wait_ge(ct.sem, ct.at(g, b + 1))
                    out = logits[:, b * experts:(b + 1) * experts]
                    ins = nc.tensor.matmul(out, xT[:, b * P:(b + 1) * P], gate_w, start=True, stop=router_bias is None)
                    if router_bias:
                        ins = nc.tensor.matmul(out, core.ones_row, core.bias[router_bias], start=False, stop=True)
                ins.then_inc(lg.sem, 1)
                unit(g, 0)
                for u in range(U):
                    if u + 1 < U:
                        unit(g, u + 1)
                    if u % tiles == tiles - 1:
                        output(g, u // tiles)

        def act(a):
            fns["act"](a)
            with a.Fori(0, G) as g:
                if own_scores:
                    router.act(a, g, logits, (lg.sem, lg.at(g, 1)), (rt.sem, rt.at(g, 0)))
                else:
                    router.act(a, g)
                for u in range(U):
                    a.wait_ge(ud.sem, ud.at(g, 2 * u + 1))
                    a.wait_ge(hd.sem, hd.at(g, u - 1))
                    nc.scalar.activation(sg[u % 2][0:rows], bank[u % 2 * 2][0:rows, :], ACT.Silu).then_inc(sd.sem, 1)

        def dve(v):
            fns["dve"](v)
            v.wait_ge(w_in, loads)

            def hidden(g, u):
                e, k = divmod(u, tiles)
                v.wait_ge(ud.sem, ud.at(g, 2 * u + 2))
                v.wait_ge(sd.sem, sd.at(g, u + 1))
                v.wait_ge(yd.sem, yd.at(g, e - 1))
                nc.vector.tensor_tensor(h[e % 2 * tiles + k][0:rows], sg[u % 2][0:rows],
                                        bank[u % 2 * 2 + 1][0:rows, :], ALU.mult).then_inc(hd.sem, 1)

            def add(g, e):
                v.wait_ge(yd.sem, yd.at(g, e + 1))
                v.wait_ge(xd.sem, xd.at(g, e))
                y = bank[4 + e % 2]
                if e >= experts:
                    xs = x[:, ds(g * GT, GT)]
                    nc.vector.tensor_tensor(xs, xs, y, ALU.add).then_inc(xd.sem, 1)
                    return
                for b in range(GB):
                    xs = x[:, ds((g * GB + b) * P, P)]
                    ins = nc.vector.scalar_tensor_tensor(xs, y[:, b * P:(b + 1) * P],
                                                         router.comb[:, b * experts + e:b * experts + e + 1], xs,
                                                         ALU.mult, ALU.add)
                ins.then_inc(xd.sem, 1)

            with v.Fori(0, G) as g:
                v.wait_ge(lg.sem, lg.at(g, 1))
                v.wait_ge(xd.sem, xd.at(g, 0))
                router.dve(v, g, logits)
                nc.vector.tensor_copy(router.small[:, 0:1], router.comb[:, 0:1]).then_inc(rt.sem, 1)
                v.wait_ge(rt.sem, rt.at(g, 1))
                for u in range(U):
                    hidden(g, u)
                    if u % tiles == tiles - 1 and u >= tiles:
                        add(g, u // tiles - 1)
                add(g, E - 1)

        return dict(sp=sp, pool=pool, dve=dve, pe=pe, act=act), [(xd.sem, xd.at(G, 0))]

    return stage


BIAS_ROWS = {"a0_v": P, "a0_out": P, "ffn0": P, "a1_kv": 2 * P, "a1_off": 80, "a1_out": P, "router2": 8}
CONSTS = {"ident": P, "ones_row": P, "ones_row_cut": P, "head_mask": H, "neg_half": B,
          "dft_cos": P, "dft_sin": P, "dft_msin": P}


def build(nc, d, out, last_stage):
    with ExitStack() as ctx:
        core = Core(nc, ctx, d)
        core.x = core.sb("x", B * P)
        core.ctxT = core.sb("ctxT", B * P)
        core.xnT = core.sb("xnT", B * P)
        core.ln_stat, core.ln_moments = core.sb("ln_stat", 6 * B)[:, :], core.sb("ln_moments", 4 * B)
        core.ln_rstd, core.ln_xn = core.sb("ln_rstd", B)[:, :], core.sb("ln_xn", GT)
        consts = core.sb("consts", sum(CONSTS.values()))
        at = 0
        for name, n in CONSTS.items():
            core.const[name] = consts[:, at:at + n]
            at += n
        core.ident, core.ones_row = core.const["ident"], core.const["ones_row"]
        core.head_mask, core.neg_half = core.const["head_mask"], core.const["neg_half"]
        bias = core.sb("bias_rows", sum(BIAS_ROWS.values()))
        core.bias, at = {}, 0
        for name, n in BIAS_ROWS.items():
            core.bias[name] = bias[:, at:at + n]
            at += n
        cb = core.sb("consts_bf16", P + H * P, BF16)
        core.ident_b, core.sel_head = cb[:, 0:P], cb[:, P:P + H * P]

        WORDS = 35 * 1024
        area = core.sb("scratch", WORDS)

        loaded, stored = core.sem("loaded"), core.sem("stored")
        start = [(loaded, 5 * 16)]
        stages = []
        for make in STAGES[:last_stage]:
            programs, start = make(core, Arena(area, WORDS), start)
            stages.append(programs)

        block = ctx.enter_context(nc.Block())

        @block.sync
        def _(s):
            for sig in core.credits:
                s.sem_inc(sig.sem, sig.credit)
            s.dma_start(core.x[:, :].rearrange("p (b d) -> p b d", d=P), d["x"].rearrange("b p d -> p b d")) \
                .then_inc(loaded, 16)
            s.dma_start(consts[:, :], d["consts"]).then_inc(loaded, 16)
            s.dma_start(bias[:, :], d["bias_rows"]).then_inc(loaded, 16)
            s.dma_start(cb[:, :].bitcast(U16), d["consts_bf16"]).then_inc(loaded, 16)
            s.dma_start(core.ctxT[:, :].rearrange("p (b t) -> p b t", t=P), d["ctxT"].rearrange("b d t -> d b t")) \
                .then_inc(loaded, 16)
            for st in stages:
                if "sp" in st:
                    st["sp"](s)
            for sem, n in start:
                s.wait_ge(sem, n)
            s.dma_start(out.rearrange("b p d -> p b d"), core.x[:, :].rearrange("p (b d) -> p b d", d=P)) \
                .then_inc(stored, 16)
            s.wait_ge(stored, 16)

        @block.tensor
        def _(t):
            for st in stages:
                st["pe"](t)

        @block.scalar
        def _(a):
            for st in stages:
                st["act"](a)

        @block.vector
        def _(v):
            for st in stages:
                st["dve"](v)

        @block.gpsimd
        def _(p):
            for st in stages:
                st["pool"](p)


def bf16_bits(a):
    return (np.ascontiguousarray(a, np.float32).view(np.uint32) >> 16).astype(np.uint16)


def shape_constants():
    k = np.arange(P)
    row0 = np.zeros((P, P), np.float32)
    row0[0] = 1.0
    cut = row0.copy()
    cut[0, P - 1] = 0.0
    angle = 2.0 * np.pi * ((k[:, None] * k[None, :]) % P) / P
    tables = {
        "ident": np.eye(P), "ones_row": row0, "ones_row_cut": cut,
        "head_mask": k[:, None] // (P // H) == np.arange(H)[None, :],
        "neg_half": np.full((P, B), -0.5),
        "dft_cos": np.cos(angle), "dft_sin": np.sin(angle), "dft_msin": -np.sin(angle),
    }
    f32 = np.concatenate([np.asarray(tables[n], np.float32) for n in CONSTS], axis=1)
    sel = np.zeros((P, H, P), np.float32)
    for h in range(H):
        sel[h, h] = sel[H + h, h] = 1.0
    return f32, bf16_bits(np.concatenate([np.eye(P, dtype=np.float32), sel.reshape(P, H * P)], axis=1))


def place_selectors(pairs=40):
    row = np.arange(P, dtype=np.float32)
    sel = np.zeros((P, pairs, P), np.float32)
    for r in range(pairs):
        sel[r, r] = 2.0 * row
        sel[pairs + r, r] = sel[2 * pairs + r, r] = -1.0
    high = ((1.0 - row * row).view(np.uint32) & 0xFFFF0000).view(np.float32)
    sel[3 * pairs], sel[3 * pairs + 1] = high, 1.0 - row * row - high
    return bf16_bits(sel.reshape(P, pairs * P))


def lay_out(a):
    rows = np.zeros((P, sum(BIAS_ROWS.values())), np.float32)
    parts = {"a0_v": [a["L0_xattn_b_v"]], "a0_out": [a["L0_xattn_b_out"]], "ffn0": [a["L0_ffn_bias"]],
             "a1_kv": [a["L1_xattn_bk"], a["L1_xattn_bv"]], "a1_off": [a["L1_xattn_boff"]],
             "a1_out": [a["L1_xattn_bo"]], "router2": [a["L2_ffn_router_b"]]}
    rows[0] = np.concatenate([v for n in BIAS_ROWS for v in parts[n]])
    f32, bf = shape_constants()
    out = {"x": a["x"], "ctx": a["ctx_1024"], "ctxT": a["ctx_1024"].transpose(0, 2, 1),
           "consts": f32, "consts_bf16": bf, "bias_rows": rows}
    out["a0_w"] = np.concatenate([a["L0_xattn_" + n].T for n in ("w_q", "w_k", "w_v", "w_out")], axis=1)
    out["a0_bqk"] = np.stack([a["L0_xattn_b_q"], a["L0_xattn_b_k"]], axis=1)
    out["f0_w"] = np.concatenate([a["L0_ffn_w_freq_real"], a["L0_ffn_w_freq_imag"]], axis=1)
    out["a1_w"] = np.concatenate([a["L1_xattn_" + n].T for n in ("Wq", "Woff", "Wk", "Wv", "Wo")], axis=1)
    out["a1_vecs"] = np.concatenate([a["L1_xattn_bq"][:, None], np.arange(P, dtype=np.float32)[:, None],
                                     np.tile(np.arange(-3, 2, dtype=np.float32), (P, H))], axis=1)
    out["a1_sel"] = place_selectors()
    out["a1_maskT"] = a["mask_BxS2_if0"].astype(np.int32).T
    out["a2_w"] = np.concatenate([a["L2_xattn_Wq"], a["L2_xattn_Wkv"],
                                  a["L2_xattn_Wout"].reshape(8, P, P).transpose(1, 0, 2).reshape(P, 8 * P)], axis=1)
    out["a2_ln"] = np.stack([a["L2_xattn_" + n] for n in ("ln1_w", "ln1_b", "ln2_w", "ln2_b")], axis=1)
    side = a["fside_Bx16_0"].reshape(B, 8, 2, 1)
    out["a2_shift"] = np.broadcast_to(side, (B, 8, 2, 64)).transpose(2, 3, 0, 1).reshape(P, B * 8)
    out["a3_w"] = np.concatenate([a["L3_xattn_Wq"].T, a["L3_xattn_Wk"].T], axis=1)
    out["a3_bqk"] = np.stack([a["L3_xattn_bq"], a["L3_xattn_bk"]], axis=1)
    reset = np.ones((P, GB, 64), np.float32)
    reset[:, :, 0] = 0.0
    out["reset64"] = reset.reshape(P, GB * 64)
    out["reset"] = np.tile(reset[:, 0, 0:8], (1, GB))
    w_up = np.concatenate([a["L1_ffn_w_up"], np.concatenate([a["L1_ffn_sg_gate"], a["L1_ffn_sg_up"]])[None]])
    w_down = np.concatenate([a["L1_ffn_w_down"], a["L1_ffn_sg_down"][None]])
    out["m1_up"] = w_up.transpose(2, 0, 1).reshape(P, -1)
    out["m1_down"] = w_down.transpose(2, 0, 1).reshape(2, 96, 9, P).transpose(1, 2, 0, 3).reshape(96, -1)
    out["m1_gate"] = a["L1_ffn_gate_w"].T
    out["m2_up"] = a["L2_ffn_w1"].transpose(1, 0, 2).reshape(P, -1)
    out["m2_down"] = a["L2_ffn_w2"].reshape(8, 4, P, P).transpose(2, 0, 1, 3).reshape(P, -1)
    out["m2_gate"] = a["L2_ffn_router_w"]
    gu = np.stack([np.concatenate([a["L3_ffn_Wg"], a["L3_ffn_Sg"].reshape(2, 88, P)]),
                   np.concatenate([a["L3_ffn_Wu"], a["L3_ffn_Su"].reshape(2, 88, P)])], axis=1)
    out["m3_up"] = gu.transpose(3, 0, 1, 2).reshape(P, -1)
    dn = np.concatenate([a["L3_ffn_Wd"], a["L3_ffn_Sd"].reshape(P, 2, 88).transpose(1, 0, 2)])
    out["m3_down"] = dn.transpose(2, 0, 1).reshape(88, -1)
    out["m3_gate"] = a["L3_ffn_gate_w"].T
    out["m3_bias"] = np.broadcast_to(a["L3_ffn_gate_bias"], (P, 64))
    return out


STAGES = [stage_attention0, stage_fourier_ffn, stage_attention1,
          stage_experts("m1", Top2Softmax, 8, 1, 2, 96), stage_attention2,
          stage_experts("m2", Top1Softmax, 8, 0, 4, P, "router2"), stage_attention3,
          stage_experts("m3", GroupedTop8, 64, 2, 1, 88)]


def kernel(**inputs):
    import numpy as _np
    import concourse.bacc as _bacc
    from concourse import mybir as _mybir
    from concourse.bass_utils import run_bass_kernel_spmd as _run

    nc = _bacc.Bacc("TRN2", target_bir_lowering=False, num_devices=1)
    arrays, aps = {}, {}
    for name, a in lay_out({k: _np.asarray(v) for k, v in inputs.items()}).items():
        arrays[f"in_{name}"] = _np.ascontiguousarray(a)
        aps[name] = nc.dram_tensor(f"in_{name}", a.shape, _mybir.dt.from_np(a.dtype), kind="ExternalInput").ap()
    out = nc.dram_tensor("out_0", (B, P, P), F32, kind="ExternalOutput").ap()
    build(nc, aps, out, LAST_STAGE)
    return _run(nc, [arrays], core_ids=[0]).results[0]["out_0"]
LAST_STAGE = 8
```

```python
from contextlib import ExitStack

import numpy as np

import concourse.bass as bass
from concourse import mybir

F32 = mybir.dt.float32
BF16 = mybir.dt.bfloat16
I32 = mybir.dt.int32
U16 = mybir.dt.uint16
U32 = mybir.dt.uint32
ALU = mybir.AluOpType
ACT = mybir.ActivationFunctionType
X = mybir.AxisListType.X
ds = bass.ds

P = 128
B = 32
GB = 4
G = B // GB
GT = GB * P
EPS = 1e-5
MAGIC = 1.5 * 2.0 ** 23
CREDIT = 129
H = 16


class Counter:

    def __init__(self, sem, per, earlier=0):
        self.sem, self.per, self.credit = sem, per, per + 1 + earlier

    def at(self, g, n):
        return g * self.per + (self.credit + n)


class Chain:

    def __init__(self, eng, sig, g):
        self.eng, self.sig, self.g, self.n = eng, sig, g, 0

    def link(self, ins):
        self.n += 1
        ins.then_inc(self.sig.sem, 1)
        self.eng.wait_ge(self.sig.sem, self.sig.at(self.g, self.n))

    def close(self):
        assert self.n == self.sig.per, (self.n, self.sig.per)


class Steps:

    def __init__(self, eng, sig):
        self.eng, self.sig, self.n = eng, sig, 0

    def link(self, ins):
        self.n += 1
        ins.then_inc(self.sig.sem, 1)
        self.eng.wait_ge(self.sig.sem, self.sig.at(0, self.n))

    def close(self):
        assert self.n == self.sig.per, (self.n, self.sig.per)


class Arena:

    def __init__(self, tensor, words):
        self.tensor, self.words, self.used = tensor, words, 0

    def take(self, n, dt=F32):
        words = n if dt == F32 else (n + 1) // 2
        assert self.used + words <= self.words, (self.used, words, self.words)
        v = self.tensor[:, self.used:self.used + words]
        self.used += words
        return v if dt == F32 else v.bitcast(dt)


class Core:

    def __init__(self, nc, ctx, dram):
        self.nc, self.ctx, self.dram = nc, ctx, dram
        self.credits, self.const, self.shared_sems = [], {}, {}
        self.psum = ctx.enter_context(nc.psum_tensor("psum", [P, 8 * 512], F32))
        self.bank = [self.psum[:, i * 512:(i + 1) * 512] for i in range(8)]
        self.ln_passes = self.ln_turns = 0
        self.ln_sems = [self.sem(f"ln_{n}") for n in ("stats", "var", "rstd", "chain")]
        self.ln_xn_done = self.counter("ln_xn", GB)
        self.ln_turned = self.counter("ln_turned", 2)
        self.ln_copied = self.counter("ln_copied", 2)
        self.ln_ring = self.counter("ln_ring", GB)
        self.ln_rings = 0

    def sb(self, name, n, dt=F32):
        return self.ctx.enter_context(self.nc.sbuf_tensor(name, [P, n], dt))

    def sem(self, name):
        return self.ctx.enter_context(self.nc.semaphore(name))

    def counter(self, name, per):
        s = Counter(self.sem(name), per)
        self.credits.append(s)
        return s

    def shared_counter(self, name, per, loops, credit=CREDIT):
        if name not in self.shared_sems:
            self.shared_sems[name] = [self.sem(name), 0]
            if credit:
                self.credits.append(Counter(self.shared_sems[name][0], credit - 1))
        entry = self.shared_sems[name]
        c = Counter(entry[0], per)
        c.credit = credit + entry[1]
        entry[1] += per * loops
        return c


def layernorm(core, src, start, dst_natural=None, dst_t=None, t_scale=None, t_bias=None, keep=None):
    nc = core.nc
    stat, moments, rstd, xn = core.ln_stat, core.ln_moments, core.ln_rstd, core.ln_xn
    n = core.ln_passes
    core.ln_passes += 1
    stats_done, var_done, rstd_done, chain = core.ln_sems
    xn_done = Counter(core.ln_xn_done.sem, GB, n * B)
    turned = Counter(core.ln_turned.sem, 2, core.ln_turns * 2 * G)
    copied = Counter(core.ln_copied.sem, 2, core.ln_turns * 2 * G)
    ring = Counter(core.ln_ring.sem, GB, core.ln_rings * B)
    core.ln_turns += dst_natural is None
    core.ln_rings += keep is not None
    st = stat.rearrange("p (b s) -> p b s", s=6)

    def dve(v):
        for s, value in start:
            v.wait_ge(s, value)
        with v.Fori(0, G) as g:
            for b in range(GB):
                nc.vector.bn_stats(stat[:, ds((g * GB + b) * 6, 6)], src[:, ds((g * GB + b) * P, P)]) \
                    .then_inc(stats_done, 1)
        v.wait_ge(stats_done, (n + 1) * B)
        mean, delta, dev, var = (moments[:, i * B:(i + 1) * B] for i in range(4))
        nc.vector.tensor_tensor(mean, st[:, :, 1], st[:, :, 4], ALU.add).then_inc(chain, 1)
        nc.vector.tensor_tensor(delta, st[:, :, 1], st[:, :, 4], ALU.subtract).then_inc(chain, 1)
        nc.vector.tensor_tensor(dev, st[:, :, 2], st[:, :, 5], ALU.add).then_inc(chain, 1)
        v.wait_ge(chain, 6 * n + 3)
        nc.vector.tensor_scalar(mean, mean, 0.5, None, ALU.mult).then_inc(chain, 1)
        nc.vector.scalar_tensor_tensor(delta, delta, 0.25, delta, ALU.mult, ALU.mult).then_inc(chain, 1)
        nc.vector.tensor_scalar(dev, dev, 1.0 / P, EPS, ALU.mult, ALU.add).then_inc(chain, 1)
        v.wait_ge(chain, 6 * n + 6)
        nc.vector.tensor_tensor(var, dev, delta, ALU.add).then_inc(var_done, 1)
        v.wait_ge(rstd_done, n + 1)
        with v.Fori(0, G) as g:
            for b in range(GB):
                if keep is not None:
                    out = keep[:, ds((g * GB + b) * P, P)]
                elif dst_natural is None:
                    v.wait_ge(turned.sem, turned.at(g, b // 2 - 1))
                    out = xn[:, b * P:(b + 1) * P]
                else:
                    out = dst_natural[:, ds((g * GB + b) * P, P)]
                nc.vector.tensor_scalar(out, src[:, ds((g * GB + b) * P, P)], mean[:, ds(g * GB + b, 1)],
                                        rstd[:, ds(g * GB + b, 1)], ALU.subtract, ALU.mult) \
                    .then_inc(xn_done.sem, 1)

    def pool(p):
        p.wait_ge(var_done, n + 1)
        nc.gpsimd.tensor_tensor(rstd, moments[:, 3 * B:4 * B], core.neg_half, ALU.pow).then_inc(rstd_done, 1)
        if keep is None:
            return
        with p.Fori(0, G) as g:
            for b in range(GB):
                p.wait_ge(xn_done.sem, xn_done.at(g, b + 1))
                p.wait_ge(turned.sem, turned.at(g, b // 2 - 1))
                nc.gpsimd.tensor_copy(xn[:, b * P:(b + 1) * P], keep[:, ds((g * GB + b) * P, P)]) \
                    .then_inc(ring.sem, 1)

    def pe(t):
        for s, value in start:
            t.wait_ge(s, value)
        with t.Fori(0, G) as g:
            for half in range(2):
                t.wait_ge(copied.sem, copied.at(g, half - 1))
                for b in (2 * half, 2 * half + 1):
                    xn_here = xn_done if keep is None else ring
                    t.wait_ge(xn_here.sem, xn_here.at(g, b + 1))
                    ins = nc.tensor.transpose(core.bank[half][:, b % 2 * P:(b % 2 + 1) * P],
                                              xn[:, b * P:(b + 1) * P], core.ident)
                ins.then_inc(turned.sem, 1)

    def act(a):
        with a.Fori(0, G) as g:
            for half in range(2):
                a.wait_ge(turned.sem, turned.at(g, half + 1))
                out = dst_t[:, ds(g * GT + half * 2 * P, 2 * P)]
                if t_scale is None:
                    ins = nc.scalar.activation(out, core.bank[half][:, 0:2 * P], ACT.Copy)
                else:
                    ins = nc.scalar.activation(out, core.bank[half][:, 0:2 * P], ACT.Identity,
                                               bias=t_bias, scale=t_scale)
                ins.then_inc(copied.sem, 1)

    if dst_natural is not None:
        return dict(dve=dve, pool=pool), (xn_done.sem, xn_done.at(G, 0))
    return dict(dve=dve, pool=pool, pe=pe, act=act), (copied.sem, copied.at(G, 0))


def stage_attention0(core, arena, start):
    nc, d, bank = core.nc, core.dram, core.bank
    DH, QUADS = P // H, H // GB
    SCALE = 1.0 / DH ** 0.5
    xnT, ctxT, x = core.xnT, core.ctxT, core.x
    w = arena.take(4 * P)
    wq, wk, wv, wo = (w[:, i * P:(i + 1) * P] for i in range(4))
    bqk = arena.take(2)
    qT, kT = arena.take(GT), arena.take(GT)
    qm = [arena.take(H * P) for _ in range(2)]
    cT = arena.take(GB * P)
    vaug = arena.take(GB * H * (DH + 1)).rearrange("p (b h e) -> p b h e", b=GB, h=H)
    nm = arena.take(2 * H)
    nm2 = [arena.take(P, BF16) for _ in range(2)]
    nmT = [arena.take(P, BF16) for _ in range(2)]
    pT = [arena.take(GT) for _ in range(2)]
    rsum = arena.take(2 * H)
    ao, aoT = arena.take(2 * P), arena.take(2 * P)

    w_in = core.sem("a0_w_in")
    ones_set = core.sem("a0_ones_set")
    fns, (ln_sem, ln_n) = layernorm(core, x, start, dst_t=xnT)
    proj = core.counter("a0_proj", 3)
    qkv = core.counter("a0_qkv", 3)
    ct = core.counter("a0_ct", GB)
    qm_v = core.counter("a0_qm_v", GB)
    qm_p = core.counter("a0_qm_p", GB)
    nat = core.counter("a0_nat", GB * QUADS)
    mx = core.counter("a0_mx", GB * QUADS)
    nms = core.counter("a0_nms", GB)
    nmt = core.counter("a0_nmt", GB)
    nmc = core.counter("a0_nmc", GB)
    st = core.counter("a0_st", GB * QUADS)
    ex = core.counter("a0_ex", GB * QUADS)
    av = core.counter("a0_av", GB * QUADS)
    aon = core.counter("a0_aon", GB)
    aot = core.counter("a0_aot", GB)
    aoc = core.counter("a0_aoc", GB)
    yd = core.counter("a0_yd", GB)
    xd = core.counter("a0_xd", GB)
    chain = core.counter("a0_chain", 2 * GB)

    def sp(s):
        s.dma_start(w, d["a0_w"]).then_inc(w_in, 16)
        s.dma_start(bqk, d["a0_bqk"]).then_inc(w_in, 16)

    def pool(p):
        nc.gpsimd.memset(vaug[:, :, :, DH:DH + 1], 1.0).then_inc(ones_set, 1)
        for t in nm2:
            nc.gpsimd.memset(t, 0.0).then_inc(ones_set, 1)
        fns["pool"](p)
        with p.Fori(0, G) as g:
            for b in range(GB):
                p.wait_ge(proj.sem, proj.at(g, 0))
                nc.gpsimd.tensor_copy(cT[:, b * P:(b + 1) * P], ctxT[:, ds((g * GB + b) * P, P)]) \
                    .then_inc(ct.sem, 1)
            for b in range(GB):
                p.wait_ge(qkv.sem, qkv.at(g, 1))
                p.wait_ge(st.sem, st.at(g, (b - 1) * QUADS))
                half = H // 2
                nc.gpsimd.tensor_tensor(
                    qm[b % 2][:, half * P:].rearrange("p (h q) -> p h q", h=half),
                    qT[:, b * P:(b + 1) * P].unsqueeze(1).to_broadcast([P, half, P]),
                    core.head_mask[:, half:H].unsqueeze(2).to_broadcast([P, half, P]), ALU.mult) \
                    .then_inc(qm_p.sem, 1)

    def dve(v):
        fns["dve"](v)
        v.wait_ge(ones_set, 3)

        def mask_q(g, b):
            v.wait_ge(qkv.sem, qkv.at(g, 1))
            v.wait_ge(st.sem, st.at(g, (b - 1) * QUADS))
            half = H // 2
            nc.vector.tensor_tensor(
                qm[b % 2][:, 0:half * P].rearrange("p (h q) -> p h q", h=half),
                qT[:, b * P:(b + 1) * P].unsqueeze(1).to_broadcast([P, half, P]),
                core.head_mask[:, 0:half].unsqueeze(2).to_broadcast([P, half, P]), ALU.mult) \
                .then_inc(qm_v.sem, 1)

        def row_max(g, b, c):
            n = nm[:, b % 2 * H:b % 2 * H + H]
            for t in range(QUADS):
                v.wait_ge(nat.sem, nat.at(g, b * QUADS + t + 1))
                nc.vector.tensor_reduce(n[:, t * 4:t * 4 + 4], bank[t % 2][:, :].rearrange("p (h k) -> p h k", h=4),
                                        X, ALU.max, negate=True).then_inc(mx.sem, 1)
            v.wait_ge(nmt.sem, nmt.at(g, b - 1))
            v.wait_ge(mx.sem, mx.at(g, (b + 1) * QUADS))
            c.link(nc.vector.tensor_copy(nm2[b % 2][:, 0:H], n))
            nc.vector.tensor_tensor(nm2[b % 2][:, H:2 * H], n, nm2[b % 2][:, 0:H], ALU.subtract) \
                .then_inc(nms.sem, 1)

        def normalise(g, b, c):
            v.wait_ge(av.sem, av.at(g, (b + 1) * QUADS))
            o = bank[4 + b % 2][:, 0:H * (DH + 1)].rearrange("p (h e) -> p h e", h=H)
            r = rsum[:, b % 2 * H:b % 2 * H + H]
            c.link(nc.vector.reciprocal(r, o[:, :, DH]))
            v.wait_ge(aot.sem, aot.at(g, b - 1))
            nc.vector.tensor_tensor(ao[:, b % 2 * P:(b % 2 + 1) * P].rearrange("p (h e) -> p h e", h=H),
                                    o[:, :, 0:DH], r.unsqueeze(2).to_broadcast([P, H, DH]), ALU.mult) \
                .then_inc(aon.sem, 1)

        def update(g, b):
            v.wait_ge(yd.sem, yd.at(g, b + 1))
            xs = x[:, ds((g * GB + b) * P, P)]
            nc.vector.tensor_tensor(xs, xs, bank[6][:, P:2 * P], ALU.add).then_inc(xd.sem, 1)

        with v.Fori(0, G) as g:
            c = Chain(v, chain, g)
            mask_q(g, 0)
            row_max(g, 0, c)
            for b in range(GB):
                if b + 1 < GB:
                    mask_q(g, b + 1)
                    row_max(g, b + 1, c)
                normalise(g, b, c)
                if b > 0:
                    update(g, b - 1)
            update(g, GB - 1)
            c.close()

    def pe(t):
        fns["pe"](t)
        t.wait_ge(w_in, 32)
        t.wait_ge(ln_sem, ln_n)

        def natural(g, b):
            t.wait_ge(qm_v.sem, qm_v.at(g, b + 1))
            t.wait_ge(qm_p.sem, qm_p.at(g, b + 1))
            for q in range(QUADS):
                t.wait_ge(mx.sem, mx.at(g, b * QUADS + q - 1))
                for i in range(4):
                    h = q * 4 + i
                    ins = nc.tensor.matmul(bank[q % 2][:, i * P:(i + 1) * P], qm[b % 2][:, h * P:(h + 1) * P],
                                           kT[:, b * P:(b + 1) * P], start=True, stop=True)
                ins.then_inc(nat.sem, 1)

        def turn_max(g, b):
            t.wait_ge(nms.sem, nms.at(g, b + 1))
            t.wait_ge(nmc.sem, nmc.at(g, b))
            nc.tensor.transpose(bank[7][:, 0:P // 2].bitcast(BF16), nm2[b % 2], core.ident_b).then_inc(nmt.sem, 1)

        def attend(g, b):
            def av_quad(q):
                n = b * QUADS + q
                t.wait_ge(ex.sem, ex.at(g, n + 1))
                if q == 0:
                    t.wait_ge(aon.sem, aon.at(g, b - 1))
                for i in range(4):
                    h = q * 4 + i
                    ins = nc.tensor.matmul(bank[4 + b % 2][:, h * (DH + 1):(h + 1) * (DH + 1)],
                                           pT[q % 2][:, i * P:(i + 1) * P], vaug[:, b, h, :], start=True, stop=True)
                ins.then_inc(av.sem, 1)

            t.wait_ge(nmc.sem, nmc.at(g, b + 1))
            for q in range(QUADS):
                n = b * QUADS + q
                t.wait_ge(ex.sem, ex.at(g, n - 1))
                nc.tensor.matmul(bank[2 + q % 2][:, :], kT[:, b * P:(b + 1) * P],
                                 qm[b % 2][:, q * 4 * P:(q * 4 + 4) * P], start=True, stop=False)
                for i in range(4):
                    h = q * 4 + i
                    ins = nc.tensor.matmul(bank[2 + q % 2][:, i * P:(i + 1) * P], core.sel_head[:, h * P:(h + 1) * P],
                                           nmT[b % 2], start=False, stop=i == 3)
                ins.then_inc(st.sem, 1)
                if q:
                    av_quad(q - 1)
            av_quad(QUADS - 1)

        def project_out(g, b):
            t.wait_ge(aon.sem, aon.at(g, b + 1))
            t.wait_ge(xd.sem, xd.at(g, b))
            nc.tensor.transpose(bank[6][:, 0:P], ao[:, b % 2 * P:(b % 2 + 1) * P], core.ident).then_inc(aot.sem, 1)
            t.wait_ge(aoc.sem, aoc.at(g, b + 1))
            nc.tensor.matmul(bank[6][:, P:2 * P], aoT[:, b % 2 * P:(b % 2 + 1) * P], wo, start=True, stop=False)
            nc.tensor.matmul(bank[6][:, P:2 * P], core.ones_row, core.bias["a0_out"], start=False, stop=True) \
                .then_inc(yd.sem, 1)

        with t.Fori(0, G) as g:
            t.wait_ge(xd.sem, xd.at(g, 0))
            t.wait_ge(nmc.sem, nmc.at(g, 0))
            nc.tensor.matmul(bank[6][:, :], wq, xnT[:, ds(g * GT, GT)], start=True, stop=True).then_inc(proj.sem, 1)
            nc.tensor.matmul(bank[7][:, :], wk, ctxT[:, ds(g * GT, GT)], start=True, stop=True).then_inc(proj.sem, 1)
            t.wait_ge(qkv.sem, qkv.at(g, 1))
            for b in range(GB):
                t.wait_ge(ct.sem, ct.at(g, b + 1))
                nc.tensor.matmul(bank[6][:, b * P:(b + 1) * P], cT[:, b * P:(b + 1) * P], wv, start=True, stop=False)
                ins = nc.tensor.matmul(bank[6][:, b * P:(b + 1) * P], core.ones_row, core.bias["a0_v"],
                                       start=False, stop=True)
            ins.then_inc(proj.sem, 1)
            t.wait_ge(qkv.sem, qkv.at(g, 3))
            natural(g, 0)
            turn_max(g, 0)
            for b in range(GB):
                if b + 1 < GB:
                    natural(g, b + 1)
                attend(g, b)
                if b + 1 < GB:
                    turn_max(g, b + 1)
                if b > 0:
                    project_out(g, b - 1)
            project_out(g, GB - 1)

    def act(a):
        fns["act"](a)
        a.wait_ge(w_in, 32)
        a.wait_ge(ones_set, 3)

        def copy_max(g, b):
            a.wait_ge(nmt.sem, nmt.at(g, b + 1))
            a.wait_ge(st.sem, st.at(g, (b - 1) * QUADS))
            nc.scalar.activation(nmT[b % 2], bank[7][:, 0:P // 2].bitcast(BF16), ACT.Copy).then_inc(nmc.sem, 1)

        def exps(g, b):
            for q in range(QUADS):
                n = b * QUADS + q
                a.wait_ge(st.sem, st.at(g, n + 1))
                a.wait_ge(av.sem, av.at(g, n - 1))
                nc.scalar.activation(pT[q % 2], bank[2 + q % 2][:, :], ACT.Exp, scale=SCALE).then_inc(ex.sem, 1)

        def copy_ao(g, b):
            a.wait_ge(aot.sem, aot.at(g, b + 1))
            a.wait_ge(yd.sem, yd.at(g, b - 1))
            nc.scalar.activation(aoT[:, b % 2 * P:(b % 2 + 1) * P], bank[6][:, 0:P], ACT.Copy).then_inc(aoc.sem, 1)

        with a.Fori(0, G) as g:
            a.wait_ge(proj.sem, proj.at(g, 1))
            a.wait_ge(qm_v.sem, qm_v.at(g, 0))
            a.wait_ge(qm_p.sem, qm_p.at(g, 0))
            nc.scalar.activation(qT, bank[6][:, :], ACT.Identity, bias=bqk[:, 0:1]).then_inc(qkv.sem, 1)
            a.wait_ge(proj.sem, proj.at(g, 2))
            a.wait_ge(st.sem, st.at(g, 0))
            nc.scalar.activation(kT, bank[7][:, :], ACT.Identity, bias=bqk[:, 1:2]).then_inc(qkv.sem, 1)
            a.wait_ge(proj.sem, proj.at(g, 3))
            a.wait_ge(av.sem, av.at(g, 0))
            nc.scalar.activation(vaug[:, :, :, 0:DH], bank[6][:, :].rearrange("p (b h e) -> p b h e", b=GB, h=H),
                                 ACT.Copy).then_inc(qkv.sem, 1)
            copy_max(g, 0)
            for b in range(GB):
                exps(g, b)
                if b + 1 < GB:
                    copy_max(g, b + 1)
                if b > 0:
                    copy_ao(g, b - 1)
            copy_ao(g, GB - 1)

    return dict(sp=sp, pool=pool, dve=dve, pe=pe, act=act), [(xd.sem, xd.at(G, 0))]


def stage_fourier_ffn(core, arena, start):
    nc, d, bank = core.nc, core.dram, core.bank
    x, xnT = core.x, core.xnT
    cos, sin, msin = (core.const[n] for n in ("dft_cos", "dft_sin", "dft_msin"))
    w = arena.take(2 * P)
    wr, wi = w[:, 0:P], w[:, P:2 * P]
    ab, m = arena.take(2 * P), arena.take(P)
    xT = arena.take(GT)

    fns, ln_done = layernorm(core, x, start, dst_t=xnT)
    w_in = core.sem("f0_w_in")
    pre, prec = core.sem("f0_pre"), core.sem("f0_prec")
    ct = core.counter("f0_ct", 2)
    yd = core.counter("f0_yd", 2)
    xd = core.counter("f0_xd", 2)

    def sp(s):
        for sem, n in start:
            s.wait_ge(sem, n)
        s.dma_start(w, d["f0_w"]).then_inc(w_in, 16)

    def pool(p):
        fns["pool"](p)
        p.wait_ge(*ln_done)
        with p.Fori(0, G) as g:
            for half in range(2):
                p.wait_ge(yd.sem, yd.at(g, half - 1))
                nc.gpsimd.tensor_copy(xT[:, half * 2 * P:(half + 1) * 2 * P],
                                      xnT[:, ds(g * GT + half * 2 * P, 2 * P)]).then_inc(ct.sem, 1)

    def pe(t):
        fns["pe"](t)
        t.wait_ge(w_in, 16)
        nc.tensor.matmul(bank[4][:, 0:P], wr, cos, start=True, stop=False)
        nc.tensor.matmul(bank[4][:, 0:P], wi, sin, start=False, stop=True)
        nc.tensor.matmul(bank[4][:, P:2 * P], wi, cos, start=True, stop=False)
        nc.tensor.matmul(bank[4][:, P:2 * P], wr, msin, start=False, stop=True).then_inc(pre, 1)
        t.wait_ge(prec, 1)
        nc.tensor.matmul(bank[5][:, 0:P], ab[:, 0:P], cos, start=True, stop=False)
        nc.tensor.matmul(bank[5][:, 0:P], ab[:, P:2 * P], msin, start=False, stop=True).then_inc(pre, 1)
        t.wait_ge(prec, 2)
        with t.Fori(0, G) as g:
            for half in range(2):
                t.wait_ge(ct.sem, ct.at(g, half + 1))
                t.wait_ge(xd.sem, xd.at(g, half - 1))
                for b in range(2):
                    out = bank[2 + half][:, b * P:(b + 1) * P]
                    nc.tensor.matmul(out, xT[:, (half * 2 + b) * P:(half * 2 + b + 1) * P], m, start=True, stop=False)
                    ins = nc.tensor.matmul(out, core.ones_row, core.bias["ffn0"], start=False, stop=True)
                ins.then_inc(yd.sem, 1)

    def act(a):
        fns["act"](a)
        a.wait_ge(pre, 1)
        nc.scalar.activation(ab, bank[4][:, 0:2 * P], ACT.Copy).then_inc(prec, 1)
        a.wait_ge(pre, 2)
        nc.scalar.activation(m, bank[5][:, 0:P], ACT.Copy, scale=1.0 / P).then_inc(prec, 1)

    def dve(v):
        fns["dve"](v)
        with v.Fori(0, G) as g:
            for half in range(2):
                v.wait_ge(yd.sem, yd.at(g, half + 1))
                xs = x[:, ds(g * GT + half * 2 * P, 2 * P)]
                nc.vector.tensor_tensor(xs, xs, bank[2 + half][:, 0:2 * P], ALU.add).then_inc(xd.sem, 1)

    return dict(sp=sp, pool=pool, dve=dve, pe=pe, act=act), [(xd.sem, xd.at(G, 0))]


def stage_attention1(core, arena, start):
    nc, d, bank = core.nc, core.dram, core.bank
    x, xnT, ctxT = core.x, core.xnT, core.ctxT
    NK, DH = 5, P // H
    R = H * NK
    HR = R // 2
    QUADS, CH = R // 4, 4
    QC = QUADS // CH
    NQ = GB * QUADS
    SCALE = 0.5 / DH ** 0.5
    CW = P + 2

    w = arena.take(P + R + 2 * P + P)
    wq, woff, wkv, wo = w[:, 0:P], w[:, P:P + R], w[:, P + R:3 * P + R], w[:, 3 * P + R:4 * P + R]
    vecs = arena.take(2 + R)
    bq, token, ref = vecs[:, 0:1], vecs[:, 1:2], vecs[:, 2:2 + R]
    sel = arena.take(HR * P, BF16)
    mask_i = arena.take(B)
    om, ones, slen, rslen = arena.take(B), arena.take(P), arena.take(B), arena.take(B)
    qpT, qn = arena.take(GT), arena.take(GT)
    cT = arena.take(GB * CW)
    t_, n_, m_, ix, i0, dx = (arena.take(GB * R) for _ in range(6))
    w01 = arena.take(GB * R * 2)
    rows = arena.take(GB * 2 * P, BF16)
    rT = arena.take(GB * 2 * P, BF16)
    kvs = [arena.take(3 * GT, BF16) for _ in range(2)]
    kvr = arena.take(GT)
    oh = [arena.take(GT, BF16) for _ in range(4)]
    prod = arena.take(QC * 4 * 2 * DH)
    sp_, s2, sc, ee, pw, aw = (arena.take(n) for n in (2 * 2 * R, 2 * R, R, R, R, 2 * R))
    mxs, sm = arena.take(H), arena.take(H)
    gv = [arena.take(2 * R * DH) for _ in range(2)]
    pv = arena.take(2 * R * DH)
    cx, cxT = arena.take(P), arena.take(P)
    G2 = [core.psum[:, 3 * 512:3 * 512 + QC * 128], core.psum[:, 5 * 512:5 * 512 + QC * 128]]

    w_in, set_, pre = core.sem("a1_w_in"), core.sem("a1_set"), core.sem("a1_pre")
    lens = core.sem("a1_lens")
    fns, ln_done = layernorm(core, x, start, dst_t=xnT)
    pj = core.counter("a1_pj", 4)
    pc = core.counter("a1_pc", 3)
    idx = core.counter("a1_idx", 1)
    ct = core.counter("a1_ct", GB)
    kvp = core.counter("a1_kvp", GB)
    kvh = core.counter("a1_kvh", GB)
    kvd = core.counter("a1_kvd", GB)
    kvl = core.counter("a1_kvl", 2 * GB)
    bc = core.counter("a1_bc", NQ)
    rla = core.counter("a1_rla", NQ * 3 // 4)
    rlv = core.counter("a1_rlv", NQ // 4)
    gat = core.counter("a1_gat", NQ)
    kp = core.counter("a1_kp", GB * CH)
    gc = core.counter("a1_gc", GB * CH)
    scd = core.counter("a1_scd", GB)
    exd = core.counter("a1_exd", GB)
    awd = core.counter("a1_awd", GB)
    vpd = core.counter("a1_vpd", GB)
    cxd = core.counter("a1_cxd", GB)
    cxt = core.counter("a1_cxt", GB)
    cxc = core.counter("a1_cxc", GB)
    yd = core.counter("a1_yd", GB)
    xd = core.counter("a1_xd", GB)
    chain = core.counter("a1_chain", 20 + GB * (CH + 3 + 3))

    def on_dve(n):
        return n % 4 == 3

    def wait_onehot(eng, g, n):
        if on_dve(n):
            eng.wait_ge(rlv.sem, rlv.at(g, n // 4 + 1))
        else:
            eng.wait_ge(rla.sem, rla.at(g, n + 1 - (n + 1) // 4))

    def sp(s):
        for sem, n in start:
            s.wait_ge(sem, n)
        s.dma_start(w, d["a1_w"]).then_inc(w_in, 16)
        s.dma_start(vecs, d["a1_vecs"]).then_inc(w_in, 16)
        s.dma_start(sel.bitcast(U16), d["a1_sel"]).then_inc(w_in, 16)
        s.dma_start(mask_i.bitcast(I32), d["a1_maskT"]).then_inc(w_in, 16)

    def pool(p):
        for sem, n in start:
            p.wait_ge(sem, n)
        nc.gpsimd.memset(ones, 1.0).then_inc(set_, 1)
        rv = rows.rearrange("p (c r) -> p c r", r=P)
        nc.gpsimd.memset(rv[:, :, 3 * HR:3 * HR + 2], 1.0).then_inc(set_, 1)
        nc.gpsimd.memset(rv[:, :, 3 * HR + 2:P], 0.0).then_inc(set_, 1)
        nc.gpsimd.memset(cT.rearrange("p (b c) -> p b c", c=CW)[:, :, P:CW], 0.0).then_inc(set_, 1)
        fns["pool"](p)

        def split_kv(g, b):
            p.wait_ge(kvd.sem, kvd.at(g, b + 1))
            k3 = kvs[b % 2].rearrange("p (s n) -> p s n", s=3)
            nc.gpsimd.tensor_tensor(k3[:, 1, :], kvr, ones[:, 0:1].to_broadcast([P, GT]), ALU.mult).then_inc(kvl.sem, 1)
            p.wait_ge(kvl.sem, kvl.at(g, 2 * b + 1))
            nc.gpsimd.tensor_tensor(k3[:, 2, :], kvr, k3[:, 1, :], ALU.subtract).then_inc(kvl.sem, 1)

        def weigh_values(g, b):
            p.wait_ge(awd.sem, awd.at(g, b + 1))
            p.wait_ge(gc.sem, gc.at(g, (b + 1) * CH))
            p.wait_ge(cxd.sem, cxd.at(g, b))
            nc.gpsimd.tensor_tensor(pv.rearrange("p (r e) -> p r e", e=DH),
                                    gv[b % 2].rearrange("p (r e) -> p r e", e=DH),
                                    aw.unsqueeze(2).to_broadcast([P, 2 * R, DH]), ALU.mult).then_inc(vpd.sem, 1)

        with p.Fori(0, G) as g:
            for b in range(GB):
                p.wait_ge(kvp.sem, kvp.at(g, b - GB + 1))
                nc.gpsimd.tensor_copy(cT[:, b * CW:b * CW + P], ctxT[:, ds((g * GB + b) * P, P)]).then_inc(ct.sem, 1)
            split_kv(g, 0)
            for b in range(GB):
                if b > 0:
                    weigh_values(g, b - 1)
                if b + 1 < GB:
                    split_kv(g, b + 1)
            weigh_values(g, GB - 1)

    def pe(t):
        fns["pe"](t)
        t.wait_ge(w_in, 64)
        t.wait_ge(set_, 4)
        t.wait_ge(pre, 1)
        nc.tensor.matmul(bank[7][:, 0:B], ones, om, start=True, stop=True).then_inc(lens, 1)
        t.wait_ge(lens, 2)
        t.wait_ge(*ln_done)

        def project_kv(g, b):
            dst = bank[2] if b == 0 else bank[7]
            t.wait_ge(ct.sem, ct.at(g, b + 1))
            for shift in range(2):
                out = dst[:, shift * 2 * P:(shift + 1) * 2 * P]
                nc.tensor.matmul(out, cT[:, b * CW + shift:b * CW + shift + P], wkv, start=True, stop=False)
                ins = nc.tensor.matmul(out, (core.ones_row, core.const["ones_row_cut"])[shift], core.bias["a1_kv"],
                                       start=False, stop=True)
            ins.then_inc(kvp.sem, 1)

        def places(g, n):
            b, m = divmod(n, QUADS)
            if n < 3:
                t.wait_ge(pc.sem, pc.at(g, 3))
                t.wait_ge(kvd.sem, kvd.at(g, 1))
            else:
                wait_onehot(t, g, n - 3)
            for j in range(4):
                r = m * 4 + j
                ins = nc.tensor.matmul(bank[n % 3][:, j * P:(j + 1) * P], sel[:, r % HR * P:(r % HR + 1) * P],
                                       rT[:, (b * 2 + r // HR) * P:(b * 2 + r // HR + 1) * P], start=True, stop=True)
            ins.then_inc(bc.sem, 1)

        def sample(g, n):
            b, m = divmod(n, QUADS)
            c = m // QC
            if m == 0:
                t.wait_ge(kvl.sem, kvl.at(g, 2 * (b + 1)))
            if m % QC == 0:
                t.wait_ge(gc.sem, gc.at(g, b * CH + c - 1))
            wait_onehot(t, g, n)
            k5 = kvs[b % 2].rearrange("p (s i k e) -> p s i k e", s=3, i=2, k=2)
            for j in range(4):
                r = m * 4 + j
                h = r // NK
                col = (r - c * QC * 4) * 4 * DH
                for s in range(3):
                    ins = nc.tensor.matmul(G2[c % 2][:, col:col + 4 * DH], oh[n % 4][:, j * P:(j + 1) * P],
                                           k5[:, s, :, :, h * DH:(h + 1) * DH], start=s == 0, stop=s == 2)
            ins.then_inc(gat.sem, 1)

        def turn_ctx(g, b):
            t.wait_ge(cxd.sem, cxd.at(g, b + 1))
            if b + 2 < GB:
                t.wait_ge(kvd.sem, kvd.at(g, b + 3))
            t.wait_ge(xd.sem, xd.at(g, b))
            nc.tensor.transpose(bank[7][:, 0:P], cx, core.ident).then_inc(cxt.sem, 1)

        def project_out(g, b):
            t.wait_ge(cxc.sem, cxc.at(g, b + 1))
            nc.tensor.matmul(bank[7][:, P:2 * P], cxT, wo, start=True, stop=False)
            nc.tensor.matmul(bank[7][:, P:2 * P], core.ones_row, core.bias["a1_out"], start=False, stop=True) \
                .then_inc(yd.sem, 1)

        with t.Fori(0, G) as g:
            t.wait_ge(rla.sem, rla.at(g, 0))
            t.wait_ge(rlv.sem, rlv.at(g, 0))
            nc.tensor.matmul(bank[0], wq, xnT[:, ds(g * GT, GT)], start=True, stop=True).then_inc(pj.sem, 1)
            project_kv(g, 0)
            t.wait_ge(pc.sem, pc.at(g, 1))
            for b in range(GB):
                ins = nc.tensor.transpose(bank[1][:, b * P:(b + 1) * P], qpT[:, b * P:(b + 1) * P], core.ident)
            ins.then_inc(pj.sem, 1)
            t.wait_ge(xd.sem, xd.at(g, 0))
            for b in range(GB):
                out = bank[7][:, b * R:(b + 1) * R]
                nc.tensor.matmul(out, qpT[:, b * P:(b + 1) * P], woff, start=True, stop=False)
                ins = nc.tensor.matmul(out, core.ones_row, core.bias["a1_off"], start=False, stop=True)
            ins.then_inc(pj.sem, 1)
            t.wait_ge(idx.sem, idx.at(g, 1))
            for c in range(2 * GB):
                ins = nc.tensor.transpose(bank[0].bitcast(BF16)[:, c * P:(c + 1) * P], rows[:, c * P:(c + 1) * P],
                                          core.ident_b)
            ins.then_inc(pj.sem, 1)
            places(g, 0)
            places(g, 1)
            for s in range(GB + 2):
                if s < GB:
                    for m in range(QUADS):
                        n = s * QUADS + m
                        if n + 2 < NQ:
                            places(g, n + 2)
                        sample(g, n)
                        if m == 2 and s >= 2:
                            project_out(g, s - 2)
                        if m == 7 and s + 1 < GB:
                            t.wait_ge(xd.sem, xd.at(g, max(s - 1, 0)))
                            t.wait_ge(cxc.sem, cxc.at(g, max(s - 1, 0)))
                            t.wait_ge(idx.sem, idx.at(g, 1))
                            project_kv(g, s + 1)
                elif s - 2 >= 0:
                    project_out(g, s - 2)
                if 1 <= s <= GB:
                    turn_ctx(g, s - 1)

    def act(a):
        fns["act"](a)
        a.wait_ge(w_in, 64)

        def high_part(g, b):
            a.wait_ge(kvp.sem, kvp.at(g, b + 1))
            a.wait_ge(gat.sem, gat.at(g, (b - 1) * QUADS))
            nc.scalar.activation(kvs[b % 2][:, 0:GT], bank[2] if b == 0 else bank[7], ACT.Copy).then_inc(kvh.sem, 1)

        def onehot(g, n):
            a.wait_ge(bc.sem, bc.at(g, n + 1))
            a.wait_ge(gat.sem, gat.at(g, n - 3))
            nc.scalar.activation(oh[n % 4], bank[n % 3], ACT.Relu).then_inc(rla.sem, 1)

        def copy_values(g, b, c):
            a.wait_ge(kp.sem, kp.at(g, b * CH + c + 1))
            a.wait_ge(vpd.sem, vpd.at(g, b - 1))
            n = QC * 4 * 2
            nc.scalar.activation(gv[b % 2].rearrange("p (c r e) -> p c r e", c=CH, e=DH)[:, c],
                                 G2[c % 2].rearrange("p (r e) -> p r e", r=n)[:, :, DH:2 * DH], ACT.Copy) \
                .then_inc(gc.sem, 1)

        def exps(g, b):
            a.wait_ge(scd.sem, scd.at(g, b + 1))
            nc.scalar.activation(ee, sc, ACT.Exp, scale=SCALE).then_inc(exd.sem, 1)

        def copy_ctx(g, b):
            a.wait_ge(cxt.sem, cxt.at(g, b + 1))
            a.wait_ge(yd.sem, yd.at(g, b))
            nc.scalar.activation(cxT, bank[7][:, 0:P], ACT.Copy).then_inc(cxc.sem, 1)

        with a.Fori(0, G) as g:
            a.wait_ge(pj.sem, pj.at(g, 1))
            nc.scalar.activation(qpT, bank[0], ACT.Identity, bias=bq).then_inc(pc.sem, 1)
            high_part(g, 0)
            a.wait_ge(pj.sem, pj.at(g, 2))
            a.wait_ge(kp.sem, kp.at(g, 0))
            nc.scalar.activation(qn, bank[1], ACT.Copy).then_inc(pc.sem, 1)
            a.wait_ge(pj.sem, pj.at(g, 4))
            nc.scalar.activation(rT, bank[0].bitcast(BF16), ACT.Copy).then_inc(pc.sem, 1)
            for s in range(GB + 2):
                if s < GB:
                    for m in range(QUADS):
                        n = s * QUADS + m
                        if not on_dve(n):
                            onehot(g, n)
                        if m == 1 and s >= 2:
                            copy_ctx(g, s - 2)
                        if m == 2 and s >= 1:
                            copy_values(g, s - 1, CH - 1)
                        if m == 6 and s >= 1:
                            exps(g, s - 1)
                        if m == 9 and s + 1 < GB:
                            high_part(g, s + 1)
                        if m in (8, 12, 17):
                            copy_values(g, s, (8, 12, 17).index(m))
                else:
                    copy_ctx(g, s - 2)
                    if s == GB:
                        copy_values(g, s - 1, CH - 1)
                        exps(g, s - 1)

    def dve(v):
        fns["dve"](v)
        v.wait_ge(w_in, 64)
        v.wait_ge(set_, 4)
        nc.vector.tensor_scalar(om, mask_i.bitcast(I32), -1.0, 1.0, ALU.mult, ALU.add).then_inc(pre, 1)
        v.wait_ge(lens, 1)
        nc.vector.tensor_scalar(slen, bank[7][:, 0:B], -1.0, None, ALU.add).then_inc(lens, 1)
        v.wait_ge(lens, 2)
        nc.vector.reciprocal(rslen, slen).then_inc(lens, 1)
        v.wait_ge(lens, 3)
        v3 = lambda a: a.rearrange("p (b r) -> p b r", b=GB)

        def find_places(g, c):
            v.wait_ge(pj.sem, pj.at(g, 3))
            sl = slen[:, ds(g * GB, GB)].unsqueeze(2).to_broadcast([P, GB, R])
            rs = rslen[:, ds(g * GB, GB)].unsqueeze(2).to_broadcast([P, GB, R])
            link = c.link
            link(nc.vector.tensor_tensor(v3(t_), v3(bank[7][:, 0:GB * R]),
                                         ref.unsqueeze(1).to_broadcast([P, GB, R]), ALU.add))
            link(nc.vector.tensor_scalar(t_, t_, token, None, ALU.add))
            link(nc.vector.tensor_tensor(v3(n_), v3(t_), rs, ALU.mult))
            link(nc.vector.tensor_scalar(n_, n_, -0.5, MAGIC, ALU.add, ALU.add))
            link(nc.vector.scalar_tensor_tensor(v3(n_), v3(n_), MAGIC, sl, ALU.subtract, ALU.mult))
            link(nc.vector.tensor_tensor(t_, t_, n_, ALU.subtract))
            link(nc.vector.scalar_tensor_tensor(v3(m_), v3(t_), 0.0, sl, ALU.is_lt, ALU.mult))
            link(nc.vector.tensor_tensor(t_, t_, m_, ALU.add))
            link(nc.vector.tensor_tensor(v3(m_), v3(t_), sl, ALU.is_ge))
            link(nc.vector.tensor_tensor(v3(m_), v3(m_), sl, ALU.mult))
            link(nc.vector.tensor_tensor(t_, t_, m_, ALU.subtract))
            link(nc.vector.tensor_scalar(ix, t_, P / (P - 1.0), -0.5, ALU.mult, ALU.add))
            link(nc.vector.tensor_scalar(i0, ix, -0.5, MAGIC, ALU.add, ALU.add))
            link(nc.vector.tensor_scalar(i0, i0, MAGIC, None, ALU.subtract))
            link(nc.vector.tensor_tensor(dx, ix, i0, ALU.subtract))
            rv = rows.rearrange("p (c r) -> p c r", r=P)
            i8 = i0.rearrange("p (c r) -> p c r", r=HR)
            w2 = w01.rearrange("p (r i) -> p r i", i=2)
            nc.vector.tensor_scalar(rv[:, :, 0:HR], i8, 0.0, None, ALU.max)
            nc.vector.scalar_tensor_tensor(w2[:, :, 1], i0, 0.0, dx, ALU.is_ge, ALU.mult)
            nc.vector.tensor_scalar(t_, dx, -2.0, 1.0, ALU.mult, ALU.add)
            link(nc.vector.scalar_tensor_tensor(m_, i0, 0.0, i0, ALU.max, ALU.mult))
            link(nc.vector.tensor_copy(rv[:, :, HR:2 * HR], m_.rearrange("p (c r) -> p c r", r=HR)))
            link(nc.vector.scalar_tensor_tensor(n_, i0, 0.0, t_, ALU.is_ge, ALU.mult))
            link(nc.vector.tensor_tensor(w2[:, :, 0], n_, dx, ALU.add))
            nc.vector.tensor_tensor(rv[:, :, 2 * HR:3 * HR], m_.rearrange("p (c r) -> p c r", r=HR),
                                    rv[:, :, HR:2 * HR], ALU.subtract).then_inc(idx.sem, 1)
            link(nc.vector.tensor_copy(mxs, i0[:, 0:H]))

        def rest_part(g, b):
            v.wait_ge(kvh.sem, kvh.at(g, b + 1))
            v.wait_ge(kvl.sem, kvl.at(g, 2 * b))
            nc.vector.tensor_tensor(kvr, bank[2] if b == 0 else bank[7], kvs[b % 2][:, 0:GT], ALU.subtract) \
                .then_inc(kvd.sem, 1)

        def onehot(g, n):
            v.wait_ge(bc.sem, bc.at(g, n + 1))
            v.wait_ge(gat.sem, gat.at(g, n - 3))
            nc.vector.tensor_scalar(oh[n % 4], bank[n % 3], 0.0, None, ALU.max).then_inc(rlv.sem, 1)

        def key_products(g, b, c, ch):
            v.wait_ge(gat.sem, gat.at(g, b * QUADS + (c + 1) * QC))
            v.wait_ge(pc.sem, pc.at(g, 2))
            g4 = G2[c % 2].rearrange("p (h r e) -> p h r e", h=4, e=2 * DH)[:, :, :, 0:DH]
            q4 = qn[:, b * P + c * 4 * DH:b * P + (c + 1) * 4 * DH].rearrange("p (h e) -> p h e", h=4)
            nc.vector.tensor_tensor(prod.rearrange("p (h r e) -> p h r e", h=4, e=DH), g4,
                                    q4.unsqueeze(2).to_broadcast([P, 4, 2 * NK, DH]), ALU.mult).then_inc(kp.sem, 1)
            v.wait_ge(kp.sem, kp.at(g, b * CH + c + 1))
            ch.link(nc.vector.tensor_reduce(sp_[:, b % 2 * 2 * R + c * 8 * NK:b % 2 * 2 * R + (c + 1) * 8 * NK],
                                            prod.rearrange("p (r e) -> p r e", e=DH), X, ALU.add))

        def scores(g, b, ch):
            ch.link(nc.vector.tensor_tensor(s2, sp_[:, b % 2 * 2 * R:(b % 2 + 1) * 2 * R],
                                            w01[:, b * 2 * R:(b + 1) * 2 * R], ALU.mult))
            ch.link(nc.vector.tensor_reduce(sc, s2.rearrange("p (r i) -> p r i", i=2), X, ALU.add))
            ch.link(nc.vector.tensor_reduce(mxs, sc.rearrange("p (h k) -> p h k", k=NK), X, ALU.max))
            s3 = sc.rearrange("p (h k) -> p h k", k=NK)
            nc.vector.tensor_tensor(s3, s3, mxs.unsqueeze(2).to_broadcast([P, H, NK]), ALU.subtract) \
                .then_inc(scd.sem, 1)

        def weights(g, b, ch):
            v.wait_ge(exd.sem, exd.at(g, b + 1))
            e3 = ee.rearrange("p (h k) -> p h k", k=NK)
            ch.link(nc.vector.tensor_reduce(sm, e3, X, ALU.add))
            ch.link(nc.vector.reciprocal(sm, sm))
            ch.link(nc.vector.tensor_tensor(pw.rearrange("p (h k) -> p h k", k=NK), e3,
                                            sm.unsqueeze(2).to_broadcast([P, H, NK]), ALU.mult))
            nc.vector.scalar_tensor_tensor(aw.rearrange("p (r i) -> p r i", i=2),
                                           w01[:, b * 2 * R:(b + 1) * 2 * R].rearrange("p (r i) -> p r i", i=2), 0.5,
                                           pw.unsqueeze(2).to_broadcast([P, R, 2]), ALU.mult, ALU.mult) \
                .then_inc(awd.sem, 1)

        def sum_values(g, b):
            v.wait_ge(vpd.sem, vpd.at(g, b + 1))
            v.wait_ge(cxt.sem, cxt.at(g, b))
            nc.vector.tensor_reduce(cx.rearrange("p (h e) -> p h e", h=H),
                                    pv.rearrange("p (h r e) -> p h e r", h=H, e=DH), X, ALU.add).then_inc(cxd.sem, 1)

        def update(g, b):
            v.wait_ge(yd.sem, yd.at(g, b + 1))
            xs = x[:, ds((g * GB + b) * P, P)]
            nc.vector.tensor_tensor(xs, xs, bank[7][:, P:2 * P], ALU.add).then_inc(xd.sem, 1)

        with v.Fori(0, G) as g:
            c = Chain(v, chain, g)
            rest_part(g, 0)
            find_places(g, c)
            for s in range(GB + 2):
                b = s
                if s < GB:
                    onehot(g, b * QUADS + 3)
                if 1 <= s <= GB:
                    scores(g, s - 1, c)
                if s < GB:
                    key_products(g, b, 0, c)
                    onehot(g, b * QUADS + 7)
                if s >= 2:
                    update(g, s - 2)
                if 1 <= s <= GB:
                    weights(g, s - 1, c)
                if s < GB:
                    key_products(g, b, 1, c)
                    onehot(g, b * QUADS + 11)
                    if s + 1 < GB:
                        rest_part(g, s + 1)
                    key_products(g, b, 2, c)
                    onehot(g, b * QUADS + 15)
                if 1 <= s <= GB:
                    sum_values(g, s - 1)
                if s < GB:
                    onehot(g, b * QUADS + 19)
                    key_products(g, b, 3, c)
            c.close()

    return dict(sp=sp, pool=pool, dve=dve, pe=pe, act=act), [(xd.sem, xd.at(G, 0))]


def stage_attention2(core, arena, start):
    nc, d, bank = core.nc, core.dram, core.bank
    x, xnT = core.x, core.xnT
    DH = 64
    TILES = H * DH // P
    QUADS = H // 4
    SCALE = DH ** -0.5
    E1 = DH + 1
    w = arena.take(4 * TILES * P)
    wq, wk, wv, wo = (w[:, i * TILES * P:(i + 1) * TILES * P] for i in range(4))
    lnp = arena.take(4)
    shift, gain = arena.take(B * TILES), arena.take(B * TILES)
    nat_buf, cnT = arena.take(B * P), arena.take(B * P)
    qT, kT = arena.take(TILES * GT), arena.take(TILES * GT)
    cT = arena.take(GT)
    vaug = arena.take(GB * H * E1).rearrange("p (b h e) -> p b h e", b=GB, h=H)
    nm = arena.take(2 * H)
    nm2 = [arena.take(P, BF16) for _ in range(2)]
    nmT = [arena.take(P, BF16) for _ in range(2)]
    pT = [arena.take(GT) for _ in range(2)]
    rsum = arena.take(2 * 4)
    ao, aoT = [arena.take(H * DH) for _ in range(2)], arena.take(H * DH)

    def head(q, i):
        return q // 2 * 8 + 2 * i + q % 2

    def rows_of(buf, h, b):
        part = slice(h % 2 * DH, h % 2 * DH + DH)
        return buf[part, h // 2 * GT + b * P:h // 2 * GT + (b + 1) * P]

    w_in, ctx_in, set_, gain_set = (core.sem(f"a2_{n}") for n in ("w_in", "ctx_in", "set", "gain_set"))
    ln_ctx, ctx_done = layernorm(core, nat_buf, [(ctx_in, 16), (w_in, 48)] + start, dst_t=cnT,
                                 t_scale=lnp[:, 0:1], t_bias=lnp[:, 1:2])
    ln_x, x_done = layernorm(core, x, [ctx_done], dst_natural=nat_buf)
    ln_xx, xx_done = layernorm(core, nat_buf, [x_done], dst_t=xnT, t_scale=lnp[:, 2:3], t_bias=lnp[:, 3:4])
    pj = core.counter("a2_pj", 3 * TILES)
    qd = core.counter("a2_qd", TILES)
    kvc = core.counter("a2_kvc", 2 * TILES)
    ct = core.counter("a2_ct", GB)
    nat = core.counter("a2_nat", GB * QUADS)
    mx = core.counter("a2_mx", GB * QUADS)
    nms = core.counter("a2_nms", GB)
    nmt = core.counter("a2_nmt", GB)
    nmc = core.counter("a2_nmc", GB)
    st = core.counter("a2_st", GB * QUADS)
    ex = core.counter("a2_ex", GB * QUADS)
    av = core.counter("a2_av", GB * QUADS)
    aon = core.counter("a2_aon", GB * QUADS)
    aot = core.counter("a2_aot", GB * 2)
    aoc = core.counter("a2_aoc", GB * 2)
    yd = core.counter("a2_yd", GB)
    xd = core.counter("a2_xd", GB)
    chain = core.counter("a2_chain", GB * (1 + QUADS))

    def sp(s):
        for sem, n in start:
            s.wait_ge(sem, n)
        s.dma_start(w, d["a2_w"]).then_inc(w_in, 16)
        s.dma_start(lnp, d["a2_ln"]).then_inc(w_in, 16)
        s.dma_start(shift, d["a2_shift"]).then_inc(w_in, 16)
        s.dma_start(nat_buf.rearrange("p (b d) -> p b d", d=P), d["ctx"].rearrange("b p d -> p b d")) \
            .then_inc(ctx_in, 16)

    def pool(p):
        for sem, n in start:
            p.wait_ge(sem, n)
        nc.gpsimd.memset(vaug[:, :, :, DH:E1], 1.0).then_inc(set_, 1)
        for t in nm2:
            nc.gpsimd.memset(t, 0.0).then_inc(set_, 1)
        for f in (ln_ctx, ln_x, ln_xx):
            f["pool"](p)
        p.wait_ge(*ctx_done)
        with p.Fori(0, G) as g:
            for b in range(GB):
                p.wait_ge(pj.sem, pj.at(g, 2 * b - 2 * GB + 2))
                nc.gpsimd.tensor_copy(cT[:, b * P:(b + 1) * P], cnT[:, ds((g * GB + b) * P, P)]).then_inc(ct.sem, 1)

    def dve(v):
        for f in (ln_ctx, ln_x, ln_xx):
            f["dve"](v)
        v.wait_ge(set_, 3)
        nc.vector.tensor_scalar(gain, shift, 1.0, None, ALU.add).then_inc(gain_set, 1)
        v.wait_ge(gain_set, 1)

        def scale_q(g, t):
            v.wait_ge(pj.sem, pj.at(g, t + 1))
            if t == 0:
                v.wait_ge(st.sem, st.at(g, 0))
            for b in range(GB):
                col = (g * GB + b) * TILES + t
                ins = nc.vector.tensor_scalar(qT[:, t * GT + b * P:t * GT + (b + 1) * P],
                                              bank[t % 4][:, b * P:(b + 1) * P], gain[:, ds(col, 1)],
                                              shift[:, ds(col, 1)], ALU.mult, ALU.add)
            ins.then_inc(qd.sem, 1)

        def row_max(g, b, c):
            n = nm[:, b % 2 * H:b % 2 * H + H]
            for q in range(QUADS):
                v.wait_ge(nat.sem, nat.at(g, b * QUADS + q + 1))
                nc.vector.tensor_reduce(n[:, q * 4:q * 4 + 4], bank[q % 2].rearrange("p (h k) -> p h k", h=4),
                                        X, ALU.max, negate=True).then_inc(mx.sem, 1)
            v.wait_ge(nmt.sem, nmt.at(g, b - 1))
            v.wait_ge(mx.sem, mx.at(g, (b + 1) * QUADS))
            c.link(nc.vector.tensor_copy(nm2[b % 2][:, 0:H], n))
            nc.vector.tensor_tensor(nm2[b % 2][:, H:2 * H], n, nm2[b % 2][:, 0:H], ALU.subtract) \
                .then_inc(nms.sem, 1)

        def normalise(g, b, q, c):
            n = b * QUADS + q
            v.wait_ge(av.sem, av.at(g, n + 1))
            o = bank[4 + q % 2][:, 0:4 * E1].rearrange("p (h e) -> p h e", h=4)
            r = rsum[:, q % 2 * 4:q % 2 * 4 + 4]
            c.link(nc.vector.reciprocal(r, o[:, :, DH]))
            if q == 0:
                v.wait_ge(aot.sem, aot.at(g, 2 * (b - 1)))
            out = ao[b % 2].rearrange("p (o i s e) -> p o i s e", o=2, i=4, s=2)[:, q // 2, :, q % 2, :]
            nc.vector.tensor_tensor(out, o[:, :, 0:DH], r.unsqueeze(2).to_broadcast([P, 4, DH]), ALU.mult) \
                .then_inc(aon.sem, 1)

        def update(g, b):
            v.wait_ge(yd.sem, yd.at(g, b + 1))
            xs = x[:, ds((g * GB + b) * P, P)]
            nc.vector.tensor_tensor(xs, xs, bank[7][:, 2 * P:3 * P], ALU.add).then_inc(xd.sem, 1)

        with v.Fori(0, G) as g:
            c = Chain(v, chain, g)
            for t in range(TILES):
                scale_q(g, t)
            row_max(g, 0, c)
            for b in range(GB):
                if b + 1 < GB:
                    row_max(g, b + 1, c)
                for q in range(QUADS):
                    normalise(g, b, q, c)
                if b > 0:
                    update(g, b - 1)
            update(g, GB - 1)
            c.close()

    def pe(t):
        for f in (ln_ctx, ln_xx):
            f["pe"](t)
        t.wait_ge(*xx_done)

        def natural(g, b):
            for q in range(QUADS):
                t.wait_ge(mx.sem, mx.at(g, b * QUADS + q - 1))
                for i in range(4):
                    h = head(q, i)
                    ins = nc.tensor.matmul(bank[q % 2][:, i * P:(i + 1) * P], rows_of(qT, h, b), rows_of(kT, h, b),
                                           start=True, stop=True)
                ins.then_inc(nat.sem, 1)

        def turn_max(g, b):
            t.wait_ge(nms.sem, nms.at(g, b + 1))
            t.wait_ge(nmc.sem, nmc.at(g, b))
            t.wait_ge(xd.sem, xd.at(g, max(b - 2, 0)))
            nc.tensor.transpose(bank[7][:, 0:P // 2].bitcast(BF16), nm2[b % 2], core.ident_b).then_inc(nmt.sem, 1)

        def attend(g, b):
            def av_quad(q):
                n = b * QUADS + q
                t.wait_ge(ex.sem, ex.at(g, n + 1))
                t.wait_ge(aon.sem, aon.at(g, n - 1))
                for i in range(4):
                    ins = nc.tensor.matmul(bank[4 + q % 2][:, i * E1:(i + 1) * E1], pT[q % 2][:, i * P:(i + 1) * P],
                                           vaug[:, b, head(q, i), :], start=True, stop=True)
                ins.then_inc(av.sem, 1)

            t.wait_ge(nmc.sem, nmc.at(g, b + 1))
            for q in range(QUADS):
                n = b * QUADS + q
                t.wait_ge(ex.sem, ex.at(g, n - 1))
                for i in range(4):
                    h = head(q, i)
                    out = bank[2 + q % 2][:, i * P:(i + 1) * P]
                    nc.tensor.matmul(out, rows_of(kT, h, b), rows_of(qT, h, b), start=True, stop=False)
                    k = q * 4 + i
                    ins = nc.tensor.matmul(out, core.sel_head[:, k * P:(k + 1) * P], nmT[b % 2],
                                           start=False, stop=True)
                ins.then_inc(st.sem, 1)
                if q:
                    av_quad(q - 1)
            av_quad(QUADS - 1)

        def project_out(g, b):
            t.wait_ge(aon.sem, aon.at(g, (b + 1) * QUADS))
            for half in range(2):
                t.wait_ge(aoc.sem, aoc.at(g, 2 * b + half))
                for i in range(4):
                    k = half * 4 + i
                    ins = nc.tensor.transpose(bank[6][:, i * P:(i + 1) * P], ao[b % 2][:, k * P:(k + 1) * P], core.ident)
                ins.then_inc(aot.sem, 1)
            t.wait_ge(aoc.sem, aoc.at(g, 2 * b + 2))
            t.wait_ge(nmc.sem, nmc.at(g, min(b + 2, GB)))
            t.wait_ge(xd.sem, xd.at(g, b))
            for k in range(TILES):
                ins = nc.tensor.matmul(bank[7][:, 2 * P:3 * P], aoT[:, k * P:(k + 1) * P], wo[:, k * P:(k + 1) * P],
                                       start=k == 0, stop=k == TILES - 1)
            ins.then_inc(yd.sem, 1)

        with t.Fori(0, G) as g:
            t.wait_ge(mx.sem, mx.at(g, 0))
            t.wait_ge(ex.sem, ex.at(g, 0))
            for k in range(TILES):
                if k >= 4:
                    t.wait_ge(qd.sem, qd.at(g, k - 3))
                nc.tensor.matmul(bank[k % 4], wq[:, k * P:(k + 1) * P], xnT[:, ds(g * GT, GT)], start=True, stop=True) \
                    .then_inc(pj.sem, 1)
            for k in range(TILES):
                if k < 4:
                    t.wait_ge(qd.sem, qd.at(g, TILES - 3 + k))
                else:
                    t.wait_ge(kvc.sem, kvc.at(g, k - 3))
                nc.tensor.matmul(bank[k % 4], wk[:, k * P:(k + 1) * P], cnT[:, ds(g * GT, GT)], start=True, stop=True) \
                    .then_inc(pj.sem, 1)
            for b in range(GB):
                t.wait_ge(ct.sem, ct.at(g, b + 1))
                for half in range(2):
                    k = b * 2 + half
                    t.wait_ge(kvc.sem, kvc.at(g, TILES + k - 3))
                    nc.tensor.matmul(bank[k % 4], cT[:, b * P:(b + 1) * P], wv[:, half * GT:(half + 1) * GT],
                                     start=True, stop=True).then_inc(pj.sem, 1)
            t.wait_ge(kvc.sem, kvc.at(g, 2 * TILES))
            natural(g, 0)
            turn_max(g, 0)
            for b in range(GB):
                if b + 1 < GB:
                    natural(g, b + 1)
                attend(g, b)
                if b + 1 < GB:
                    turn_max(g, b + 1)
                if b > 0:
                    project_out(g, b - 1)
            project_out(g, GB - 1)

    def act(a):
        for f in (ln_ctx, ln_xx):
            f["act"](a)
        a.wait_ge(set_, 3)

        def copy_max(g, b):
            a.wait_ge(nmt.sem, nmt.at(g, b + 1))
            a.wait_ge(st.sem, st.at(g, (b - 1) * QUADS))
            nc.scalar.activation(nmT[b % 2], bank[7][:, 0:P // 2].bitcast(BF16), ACT.Copy).then_inc(nmc.sem, 1)

        def exps(g, b):
            for q in range(QUADS):
                n = b * QUADS + q
                a.wait_ge(st.sem, st.at(g, n + 1))
                a.wait_ge(av.sem, av.at(g, n - 1))
                nc.scalar.activation(pT[q % 2], bank[2 + q % 2], ACT.Exp, scale=SCALE).then_inc(ex.sem, 1)

        def copy_ao(g, b):
            for half in range(2):
                a.wait_ge(aot.sem, aot.at(g, 2 * b + half + 1))
                a.wait_ge(yd.sem, yd.at(g, b))
                nc.scalar.activation(aoT[:, half * GT:(half + 1) * GT], bank[6], ACT.Copy).then_inc(aoc.sem, 1)

        with a.Fori(0, G) as g:
            a.wait_ge(st.sem, st.at(g, 0))
            for k in range(TILES):
                a.wait_ge(pj.sem, pj.at(g, TILES + k + 1))
                nc.scalar.activation(kT[:, k * GT:(k + 1) * GT], bank[k % 4], ACT.Copy).then_inc(kvc.sem, 1)
            a.wait_ge(av.sem, av.at(g, 0))
            for k in range(TILES):
                b, half = divmod(k, 2)
                a.wait_ge(pj.sem, pj.at(g, 2 * TILES + k + 1))
                nc.scalar.activation(vaug[:, b, half * H // 2:(half + 1) * H // 2, 0:DH],
                                     bank[k % 4].rearrange("p (h e) -> p h e", e=DH), ACT.Copy).then_inc(kvc.sem, 1)
            copy_max(g, 0)
            for b in range(GB):
                exps(g, b)
                if b + 1 < GB:
                    copy_max(g, b + 1)
                if b > 0:
                    copy_ao(g, b - 1)
            copy_ao(g, GB - 1)

    return dict(sp=sp, pool=pool, dve=dve, pe=pe, act=act), [(xd.sem, xd.at(G, 0))]


def stage_attention3(core, arena, start):
    nc, d, bank = core.nc, core.dram, core.bank
    x, xnT, ctxT = core.x, core.xnT, core.ctxT
    C1 = P + 1
    w, bqk = arena.take(2 * P), arena.take(2)
    ctxa = arena.take(B * C1)
    qT, kT, pT = arena.take(GT), arena.take(GT), arena.take(GT)
    nm, rsum = arena.take(GB), arena.take(GB)
    nm2, nmT = arena.take(GB * P, BF16), arena.take(GB * P, BF16)

    fns, ln_done = layernorm(core, x, start, dst_t=xnT)
    w_in, set_ = core.sem("a3_w_in"), core.sem("a3_set")
    pj = core.counter("a3_pj", 2)
    pc = core.counter("a3_pc", 2)
    nat = core.counter("a3_nat", 1)
    nms = core.counter("a3_nms", 1)
    nmt = core.counter("a3_nmt", 1)
    nmc = core.counter("a3_nmc", 1)
    st = core.counter("a3_st", 1)
    ex = core.counter("a3_ex", 1)
    av = core.counter("a3_av", 2)
    xd = core.counter("a3_xd", 2)
    chain = core.counter("a3_chain", 4)

    def sp(s):
        for sem, n in start:
            s.wait_ge(sem, n)
        s.dma_start(w, d["a3_w"]).then_inc(w_in, 16)
        s.dma_start(bqk, d["a3_bqk"]).then_inc(w_in, 16)
        s.dma_start(ctxa.rearrange("p (b e) -> p b e", e=C1)[:, :, 0:P], d["ctx"].rearrange("b p d -> p b d")) \
            .then_inc(w_in, 16)

    def pool(p):
        for sem, n in start:
            p.wait_ge(sem, n)
        nc.gpsimd.memset(ctxa.rearrange("p (b e) -> p b e", e=C1)[:, :, P:C1], 1.0).then_inc(set_, 1)
        nc.gpsimd.memset(nm2, 0.0).then_inc(set_, 1)
        fns["pool"](p)

    def pe(t):
        fns["pe"](t)
        t.wait_ge(w_in, 48)
        t.wait_ge(set_, 2)
        t.wait_ge(*ln_done)
        with t.Fori(0, G) as g:
            t.wait_ge(pc.sem, pc.at(g, 0))
            nc.tensor.matmul(bank[0], w[:, 0:P], xnT[:, ds(g * GT, GT)], start=True, stop=True).then_inc(pj.sem, 1)
            nc.tensor.matmul(bank[1], w[:, P:2 * P], ctxT[:, ds(g * GT, GT)], start=True, stop=True) \
                .then_inc(pj.sem, 1)
            t.wait_ge(pc.sem, pc.at(g, 2))
            t.wait_ge(nms.sem, nms.at(g, 0))
            for b in range(GB):
                cols = slice(b * P, (b + 1) * P)
                ins = nc.tensor.matmul(bank[2][:, cols], qT[:, cols], kT[:, cols], start=True, stop=True)
            ins.then_inc(nat.sem, 1)
            t.wait_ge(nms.sem, nms.at(g, 1))
            for b in range(GB):
                cols = slice(b * P, (b + 1) * P)
                ins = nc.tensor.transpose(bank[3].bitcast(BF16)[:, cols], nm2[:, cols], core.ident_b)
            ins.then_inc(nmt.sem, 1)
            t.wait_ge(nmc.sem, nmc.at(g, 1))
            for b in range(GB):
                cols = slice(b * P, (b + 1) * P)
                nc.tensor.matmul(bank[4][:, cols], kT[:, cols], qT[:, cols], start=True, stop=False)
                ins = nc.tensor.matmul(bank[4][:, cols], core.sel_head[:, 0:P], nmT[:, cols], start=False, stop=True)
            ins.then_inc(st.sem, 1)
            t.wait_ge(ex.sem, ex.at(g, 1))
            for pair in range(2):
                t.wait_ge(xd.sem, xd.at(g, pair - 1))
                for i in range(2):
                    b = pair * 2 + i
                    ins = nc.tensor.matmul(bank[5 + pair][:, i * C1:(i + 1) * C1], pT[:, b * P:(b + 1) * P],
                                           ctxa[:, ds((g * GB + b) * C1, C1)], start=True, stop=True)
                ins.then_inc(av.sem, 1)

    def act(a):
        fns["act"](a)
        a.wait_ge(w_in, 48)
        with a.Fori(0, G) as g:
            a.wait_ge(st.sem, st.at(g, 0))
            for i, dst in enumerate((qT, kT)):
                a.wait_ge(pj.sem, pj.at(g, i + 1))
                nc.scalar.activation(dst, bank[i], ACT.Identity, bias=bqk[:, i:i + 1]).then_inc(pc.sem, 1)
            a.wait_ge(nmt.sem, nmt.at(g, 1))
            nc.scalar.activation(nmT, bank[3].bitcast(BF16)[:, 0:GT], ACT.Copy).then_inc(nmc.sem, 1)
            a.wait_ge(st.sem, st.at(g, 1))
            a.wait_ge(av.sem, av.at(g, 0))
            nc.scalar.activation(pT, bank[4], ACT.Exp).then_inc(ex.sem, 1)

    def dve(v):
        fns["dve"](v)
        v.wait_ge(set_, 2)
        n3 = nm2.rearrange("p (b r) -> p b r", b=GB)
        with v.Fori(0, G) as g:
            c = Chain(v, chain, g)
            v.wait_ge(nat.sem, nat.at(g, 1))
            c.link(nc.vector.tensor_reduce(nm, bank[2].rearrange("p (b k) -> p b k", b=GB), X, ALU.max, negate=True))
            c.link(nc.vector.tensor_copy(n3[:, :, 0], nm))
            nc.vector.tensor_tensor(n3[:, :, H], nm, n3[:, :, 0], ALU.subtract).then_inc(nms.sem, 1)
            for pair in range(2):
                v.wait_ge(av.sem, av.at(g, pair + 1))
                o = bank[5 + pair][:, 0:2 * C1].rearrange("p (b e) -> p b e", b=2)
                c.link(nc.vector.reciprocal(rsum[:, pair * 2:pair * 2 + 2], o[:, :, P]))
                for i in range(2):
                    b = pair * 2 + i
                    xs = x[:, ds((g * GB + b) * P, P)]
                    ins = nc.vector.scalar_tensor_tensor(xs, o[:, i, 0:P], rsum[:, b:b + 1], xs, ALU.mult, ALU.add)
                ins.then_inc(xd.sem, 1)
            c.close()

    return dict(sp=sp, pool=pool, dve=dve, pe=pe, act=act), [(xd.sem, xd.at(G, 0))]


class Router:

    def __init__(self, core, arena, tag, experts, links, steps):
        self.core, self.e, self.steps = core, experts, steps
        n = GB * experts
        self.scratch = arena.take(7 * n)
        self.logit, self.gt, self.eq, self.cum, self.comb, self.val, self.tmp = (
            self.scratch[:, i * n:(i + 1) * n] for i in range(7))
        self.top = arena.take(GB * 8 * 8)
        self.small = arena.take(GB * 8 * 4)
        self.reset = arena.take(n)
        self.pad = arena.take(1)
        self.mask = self.val
        self.asked = core.counter(f"{tag}_asked", steps)
        self.answered = core.counter(f"{tag}_answered", steps)
        self.chain = core.counter(f"{tag}_chain", links)

    def hold(self):
        self.core.nc.vector.memset(self.pad, 0.0)

    def largest(self, c, sel, values, threshold, k, e):
        nc = self.core.nc
        v3 = lambda a: a[:, 0:GB * e].rearrange("p (b e) -> p b e", e=e)
        thr = threshold.unsqueeze(2).to_broadcast([P, GB, e])
        left = self.small[:, 0:GB]
        nc.vector.tensor_tensor(v3(self.eq), values, thr, ALU.is_equal)
        c.link(nc.vector.tensor_tensor(v3(self.gt), values, thr, ALU.is_gt))
        nc.vector.tensor_tensor_scan(self.cum[:, 0:GB * e], self.reset8 if e == 8 else self.reset,
                                     self.eq[:, 0:GB * e], 0.0, ALU.mult, ALU.add)
        c.link(nc.vector.tensor_reduce(left, v3(self.gt), X, ALU.add))
        c.link(nc.vector.tensor_scalar(left, left, -1.0, float(k), ALU.mult, ALU.add))
        c.link(nc.vector.tensor_tensor(v3(self.cum), v3(self.cum), left.unsqueeze(2).to_broadcast([P, GB, e]),
                                       ALU.is_le))
        c.link(nc.vector.tensor_tensor(self.cum[:, 0:GB * e], self.cum[:, 0:GB * e], self.eq[:, 0:GB * e], ALU.mult))
        c.link(nc.vector.tensor_tensor(sel, v3(self.cum), v3(self.gt), ALU.add))


class Top2Softmax(Router):

    def __init__(self, core, arena, tag):
        super().__init__(core, arena, tag, 8, 13, 1)
        self.reset8 = self.reset

    def dve(self, v, g, psum):
        nc, c = self.core.nc, Chain(v, self.chain, g)
        v3 = lambda a: a.rearrange("p (b e) -> p b e", e=8)
        top, w = v3(self.top[:, 0:GB * 8]), self.small[:, GB:3 * GB]
        c.link(nc.vector.tensor_copy(self.logit, psum))
        self.hold()
        for b in range(GB):
            ins = nc.vector.max(top[:, b, :], v3(self.logit)[:, b, :])
        c.link(ins)
        nc.vector.tensor_tensor(self.small[:, 3 * GB:4 * GB], top[:, :, 0], top[:, :, 1], ALU.subtract) \
            .then_inc(self.asked.sem, 1)
        self.largest(c, v3(self.val), v3(self.logit), top[:, :, 1], 2, 8)
        v.wait_ge(self.answered.sem, self.answered.at(g, 1))
        w1, w2 = w[:, 0:GB], w[:, GB:2 * GB]
        bc = lambda a: a.unsqueeze(2).to_broadcast([P, GB, 8])
        c.link(nc.vector.tensor_tensor(w1, w1, w2, ALU.subtract))
        c.link(nc.vector.tensor_tensor(v3(self.tmp), v3(self.logit), bc(top[:, :, 0]), ALU.is_equal))
        c.link(nc.vector.tensor_tensor(v3(self.tmp), v3(self.tmp), bc(w1), ALU.mult))
        c.link(nc.vector.tensor_tensor(v3(self.tmp), v3(self.tmp), bc(w2), ALU.add))
        c.link(nc.vector.tensor_tensor(self.comb, self.tmp, self.val, ALU.mult))
        c.close()

    def act(self, a, g):
        nc, w = self.core.nc, self.small[:, GB:3 * GB]
        dm = self.small[:, 3 * GB:4 * GB]
        a.wait_ge(self.asked.sem, self.asked.at(g, 1))
        nc.scalar.activation(w[:, 0:GB], dm, ACT.Sigmoid)
        nc.scalar.activation(w[:, GB:2 * GB], dm, ACT.Sigmoid, scale=-1.0).then_inc(self.answered.sem, 1)


class Top1Softmax(Router):

    def __init__(self, core, arena, tag):
        super().__init__(core, arena, tag, 8, 12, 1)
        self.reset8 = self.reset

    def dve(self, v, g, psum):
        nc, c = self.core.nc, Chain(v, self.chain, g)
        v3 = lambda a: a.rearrange("p (b e) -> p b e", e=8)
        top, total = v3(self.top[:, 0:GB * 8]), self.small[:, GB:2 * GB]
        bc = lambda a: a.unsqueeze(2).to_broadcast([P, GB, 8])
        c.link(nc.vector.tensor_copy(self.logit, psum))
        self.hold()
        for b in range(GB):
            ins = nc.vector.max(top[:, b, :], v3(self.logit)[:, b, :])
        c.link(ins)
        nc.vector.tensor_tensor(v3(self.tmp), v3(self.logit), bc(top[:, :, 0]), ALU.subtract) \
            .then_inc(self.asked.sem, 1)
        self.largest(c, v3(self.val), v3(self.logit), top[:, :, 0], 1, 8)
        v.wait_ge(self.answered.sem, self.answered.at(g, 1))
        c.link(nc.vector.tensor_reduce(total, v3(self.tmp), X, ALU.add))
        c.link(nc.vector.reciprocal(total, total))
        c.link(nc.vector.tensor_tensor(v3(self.comb), v3(self.val), bc(total), ALU.mult))
        c.link(nc.vector.tensor_copy(total, total))
        c.close()

    def act(self, a, g):
        a.wait_ge(self.asked.sem, self.asked.at(g, 1))
        self.core.nc.scalar.activation(self.tmp, self.tmp, ACT.Exp).then_inc(self.answered.sem, 1)


class GroupedTop8(Router):

    def __init__(self, core, arena, tag):
        super().__init__(core, arena, tag, 64, 24, 1)
        self.bias, self.reset8 = arena.take(64), arena.take(GB * 8)
        self.groups = arena.take(GB * 8 * 2)
        self.mask = self.eq

    def dve(self, v, g, psum):
        nc, c = self.core.nc, Chain(v, self.chain, g)
        score, choice, masked, sel = self.logit, self.val, self.tmp, self.comb
        v3 = lambda a: a.rearrange("p (b e) -> p b e", e=64)
        v8 = lambda a: a.rearrange("p (g e) -> p g e", e=8)
        b8 = lambda a: a.rearrange("p (b g) -> p b g", g=8)
        v.wait_ge(self.answered.sem, self.answered.at(g, 1))
        c.link(nc.vector.tensor_tensor(v3(choice), v3(score), self.bias.unsqueeze(1).to_broadcast([P, GB, 64]),
                                       ALU.add))
        top, gs, gsel = v8(self.top), self.groups[:, 0:GB * 8], self.groups[:, GB * 8:]
        self.hold()
        for i in range(GB * 8):
            ins = nc.vector.max(top[:, i, :], v8(choice)[:, i, :])
        c.link(ins)
        c.link(nc.vector.tensor_tensor(gs, top[:, :, 0], top[:, :, 1], ALU.add))
        self.hold()
        for b in range(GB):
            ins = nc.vector.max(top[:, b, :], b8(gs)[:, b, :])
        c.link(ins)
        self.largest(c, b8(gsel), b8(gs), top[:, 0:GB, 3], 4, 8)
        c.link(nc.vector.tensor_tensor(v8(masked), v8(choice), gsel.unsqueeze(2).to_broadcast([P, GB * 8, 8]),
                                       ALU.mult))
        self.hold()
        for b in range(GB):
            ins = nc.vector.max(top[:, b, :], v3(masked)[:, b, :])
        c.link(ins)
        self.largest(c, v3(self.mask), v3(masked), top[:, 0:GB, 7], 8, 64)
        c.link(nc.vector.tensor_tensor(sel, self.mask, score, ALU.mult))
        total = self.small[:, GB:2 * GB]
        c.link(nc.vector.tensor_reduce(total, v3(sel), X, ALU.add))
        c.link(nc.vector.tensor_scalar(total, total, 1e-20, None, ALU.add))
        c.link(nc.vector.reciprocal(total, total))
        c.link(nc.vector.tensor_scalar(total, total, 2.5, None, ALU.mult))
        c.link(nc.vector.tensor_tensor(v3(sel), v3(sel), total.unsqueeze(2).to_broadcast([P, GB, 64]), ALU.mult))
        c.close()

    def act(self, a, g, psum, ready, free):
        nc = self.core.nc
        a.wait_ge(*ready)
        a.wait_ge(*free)
        nc.scalar.activation(self.logit, psum, ACT.Sigmoid).then_inc(self.answered.sem, 1)


def stage_experts(tag, make_router, experts, top_k, shared, width, rows, quads, router_bias=None):
    TILES = -(-(B * P * top_k + experts * (P - 1)) // P)
    TILES = -(-TILES // (4 * quads)) * 4 * quads
    tiles = width // rows
    PER = 4 // tiles
    S = 4 // PER
    UNITS = S * quads
    COLS = -(-TILES // P)
    AHEAD = 2 if S == 1 else 1

    def stage(core, arena, start):
        nc, d, bank = core.nc, core.dram, core.bank
        x, xnT = core.x, core.xnT
        E = experts + shared
        N = GB * experts
        up = arena.take(E * 2 * width)
        down = arena.take(E * tiles * P)
        gate_w = arena.take(experts)
        natural = arena.take(B * P)
        gates, key = arena.take(B * experts), arena.take(B * experts)
        chosen_w = arena.take(max(B * experts // 2, 3 * B * 8))
        chosen = chosen_w[:, 0:B * experts // 2].bitcast(BF16)
        best = chosen_w[:, 0:B * 8]
        place = chosen_w[:, B * 8:B * 8 + B * top_k].bitcast(U32)
        weight = chosen_w[:, 2 * B * 8:2 * B * 8 + B * top_k]
        n_bufs = 3 + 2 * tiles if shared else 4
        scratch = arena.take(n_bufs * GT)
        bufs = [scratch[:, i * GT:(i + 1) * GT] for i in range(n_bufs)]
        xT, sg, h = bufs[0], bufs[1:3], bufs[3:]
        index = [arena.take(2 * top_k).bitcast(U32) for _ in range(2)]
        total, first, n_tiles, ends, base = (arena.take(experts) for _ in range(5))
        owner = arena.take(COLS)
        table = arena.take(COLS * P)[0:1].bitcast(I32)
        tile_id = arena.take(3)
        pad = arena.take(1)
        router = make_router(core, arena, tag)
        own_scores = isinstance(router, GroupedTop8)
        U = shared * tiles
        sorted_x = core.sorted_x
        sorted_y = nc.dram_tensor(f"{tag}_sorted_y", (TILES * P, P), F32, kind="Internal").ap()
        x_tiles = sorted_x.rearrange("(t p) d -> p t d", p=P)
        y_tiles = sorted_y.rearrange("(t p) d -> p t d", p=P)

        fns, ln_done = layernorm(core, x, start, dst_t=xnT, keep=natural)
        LOOPS = TILES // (4 * quads)
        CHUNK = min(512, B * experts)
        CHUNKS = B * experts // CHUNK
        K2 = 2 * top_k
        over = core.shared_counter
        w_in = core.sem(f"{tag}_w_in")
        ct = over("ct", GB, G)
        lg = over("lg", 1, G)
        rt = over("rt", 1, G)
        if shared:
            ud = over("ud", 2 * U, G)
            sd = over("sd", U, G)
            hd = over("hd", U, G)
            yd = over("yd", shared, G)
            xd = over("xd", shared, G)
        routed = over("routed", 1, 1, 0)
        counted = over("counted", 2 * CHUNKS, 1, 0)
        steps = over("steps", 17 + 2 * COLS + 3 * top_k, 1, 0)
        owned = over("owned", 1, 1, 0)
        owner_row = over("owner_row", 1, 1, 0)
        tabled = over("tabled", 1, 1, 0)
        placed = over("placed", 1, 1, 0)
        weighed = over("weighed", 1, 1, 0)
        ic = over("ic", 4, G)
        sc = [over(f"sc{i}", K2 * 16, G, 0) for i in range(2)]
        freed = over("freed", 2, G)
        ld = [over(f"ld{i}", 8 * quads, LOOPS) for i in range(2)]
        xt = over("xt", quads, LOOPS)
        xc = over("xc", quads, LOOPS)
        gu = over("gu", UNITS, LOOPS)
        si = over("si", UNITS, LOOPS)
        hn = over("hn", UNITS, LOOPS)
        ht = over("ht", UNITS, LOOPS)
        hc = over("hc", UNITS, LOOPS)
        dn = over("dn", UNITS, LOOPS)
        yc = over("yc", quads, LOOPS)
        stored = [over(f"y_stored{i}", 8 * quads, LOOPS) for i in range(2)]
        gic = over("gic", 2, G)
        ga = [over(f"ga{i}", K2 * 16, G, 0) for i in range(2)]
        mixed = over("mixed", 2, G)
        mixing = over("mixing", K2, G)

        xs, xTs, sgs, hs = ([xnT[:, (2 * i + j) * GT:(2 * i + j + 1) * GT] for j in range(2)] for i in range(4))
        hTs, ys = bufs[0:2], bufs[2:4]
        staged = [core.ln_xn[:, 0:2 * P], core.ln_xn[:, 2 * P:4 * P]]
        gathered = [natural[:, i * K2 * P:(i + 1) * K2 * P] for i in range(2)]
        before = scratch[:, 0:B * experts]
        count = router.scratch[:, 0:B * experts // 2].bitcast(BF16)
        taken = before

        def run(eng, step):
            step(0, 0, first=True)
            with eng.Fori(0, LOOPS - 1) as g:
                for u in range(1, UNITS + 1):
                    step(g, u)
            for u in range(1, UNITS):
                step(LOOPS - 1, u, last=True)

        def sp(s):
            for sem, n in start:
                s.wait_ge(sem, n)
            s.dma_start(gate_w, d[f"{tag}_gate"]).then_inc(w_in, 16)
            s.dma_start(router.reset, d["reset"][:, 0:GB * 8] if experts == 8 else d["reset64"]).then_inc(w_in, 16)
            s.dma_start(tile_id, d["tile_id"]).then_inc(w_in, 16)
            if own_scores:
                s.dma_start(router.bias, d[f"{tag}_bias"]).then_inc(w_in, 16)
                s.dma_start(router.reset8, d["reset"][:, 0:GB * 8]).then_inc(w_in, 16)
            s.dma_start(up, d[f"{tag}_up"]).then_inc(w_in, 16)
            s.dma_start(down[0:rows], d[f"{tag}_down"]).then_inc(w_in, 16)
            with s.Fori(0, G) as g:
                for i in range(2):
                    s.wait_ge(sc[i].sem, sc[i].at(g, K2 * 16))
                    s.sem_inc(freed.sem, 1)
            s.wait_ge(weighed.sem, weighed.at(0, 1))
            with s.Fori(0, LOOPS) as g:
                for q in range(quads):
                    s.wait_ge(xt.sem, xt.at(g, q - 1))
                    s.dma_start(xs[q % 2].rearrange("p (t d) -> p t d", d=P),
                                x_tiles[:, ds((g * quads + q) * 4, 4), :]).then_inc(ld[q % 2].sem, 16)

        loads = 16 * (7 if own_scores else 5)
        logits = bank[6][:, 0:N]

        def pool(p):
            fns["pool"](p)
            p.wait_ge(*ln_done)
            with p.Fori(0, G) as g:
                for b in range(GB):
                    p.wait_ge(lg.sem, lg.at(g, 0))
                    nc.gpsimd.tensor_copy(xT[:, b * P:(b + 1) * P], xnT[:, ds((g * GB + b) * P, P)]) \
                        .then_inc(ct.sem, 1)

            def hold():
                nc.gpsimd.tensor_tensor(pad, core.neg_half[:, 0:1], core.neg_half[:, 0:1], ALU.add)

            p.wait_ge(placed.sem, placed.at(0, 1))
            with p.Fori(0, G) as g:
                for i in range(2):
                    p.wait_ge(freed.sem, freed.at(g, i - 1))
                    nc.gpsimd.tensor_copy(index[i], place[:, ds((2 * g + i) * K2, K2)]).then_inc(ic.sem, 1)
                    nc.gpsimd.tensor_copy(staged[i], natural[:, ds((2 * g + i) * 2 * P, 2 * P)]).then_inc(ic.sem, 1)
                    p.wait_ge(ic.sem, ic.at(g, 2 * i + 2))
                    hold()
                    for b in range(2):
                        for k in range(top_k):
                            at = index[i][:, b * top_k + k:b * top_k + k + 1]
                            nc.gpsimd.indirect_dma_start(
                                out=sorted_x, out_offset=bass.IndirectOffsetOnAxis(ap=at, axis=0),
                                in_=staged[i][:, b * P:(b + 1) * P], in_offset=None).then_inc(sc[i].sem, 16)
            for i in range(2):
                p.wait_ge(stored[i].sem, stored[i].at(LOOPS, 0))
            with p.Fori(0, G) as g:
                for i in range(2):
                    p.wait_ge(mixed.sem, mixed.at(g, i - 1))
                    nc.gpsimd.tensor_copy(index[i], place[:, ds((2 * g + i) * K2, K2)]).then_inc(gic.sem, 1)
                    p.wait_ge(gic.sem, gic.at(g, i + 1))
                    hold()
                    for k in range(K2):
                        at = index[i][:, k:k + 1]
                        nc.gpsimd.indirect_dma_start(
                            out=gathered[i][:, k * P:(k + 1) * P], out_offset=None, in_=sorted_y,
                            in_offset=bass.IndirectOffsetOnAxis(ap=at, axis=0)).then_inc(ga[i].sem, 16)

        def pe(t):
            fns["pe"](t)
            t.wait_ge(w_in, loads)
            t.wait_ge(*ln_done)

            def shared_part(g, u):
                for k in range(2):
                    if k == 0:
                        t.wait_ge(hd.sem, hd.at(g, u - 1))
                    col = ((experts + u // tiles) * 2 * tiles + k * tiles + u % tiles) * rows
                    nc.tensor.matmul(bank[u % 2 * 2 + k][0:rows, :], up[:, col:col + rows],
                                     xnT[:, ds(g * GT, GT)], start=True, stop=True).then_inc(ud.sem, 1)

            def shared_output(g, e):
                t.wait_ge(hd.sem, hd.at(g, (e + 1) * tiles))
                t.wait_ge(xd.sem, xd.at(g, e - 1))
                for b in range(GB):
                    for k in range(tiles):
                        hk = h[e % 2 * tiles + k]
                        part = (experts + e) * tiles + k
                        ins = nc.tensor.matmul(bank[4 + e % 2][:, b * P:(b + 1) * P], hk[0:rows, b * P:(b + 1) * P],
                                               down[0:rows, part * P:(part + 1) * P],
                                               start=k == 0, stop=k == tiles - 1)
                ins.then_inc(yd.sem, 1)

            with t.Fori(0, G) as g:
                t.wait_ge(rt.sem, rt.at(g, 0))
                for b in range(GB):
                    t.wait_ge(ct.sem, ct.at(g, b + 1))
                    out = logits[:, b * experts:(b + 1) * experts]
                    ins = nc.tensor.matmul(out, xT[:, b * P:(b + 1) * P], gate_w, start=True, stop=router_bias is None)
                    if router_bias:
                        ins = nc.tensor.matmul(out, core.ones_row, core.bias[router_bias], start=False, stop=True)
                ins.then_inc(lg.sem, 1)
            t.wait_ge(routed.sem, routed.at(0, 1))
            for c in range(CHUNKS):
                rhs = chosen[:, c * CHUNK:(c + 1) * CHUNK]
                nc.tensor.matmul(bank[c][:, 0:CHUNK], core.earlier_b, rhs, start=True, stop=True).then_inc(counted.sem, 1)
                nc.tensor.matmul(bank[4 + c][:, 0:CHUNK], core.ones_b, rhs, start=True, stop=True).then_inc(counted.sem, 1)
            t.wait_ge(owned.sem, owned.at(0, 1))
            for c in range(COLS):
                ins = nc.tensor.matmul(bank[7][0:1, c * P:(c + 1) * P], owner[:, c:c + 1], core.ident,
                                       start=True, stop=True)
            ins.then_inc(owner_row.sem, 1)
            t.wait_ge(tabled.sem, tabled.at(0, 1))
            if shared:
                with t.Fori(0, G) as g:
                    shared_part(g, 0)
                    for u in range(U):
                        if u + 1 < U:
                            shared_part(g, u + 1)
                        if u % tiles == tiles - 1:
                            shared_output(g, u // tiles)

            def turn_x(g, q):
                t.wait_ge(ld[q % 2].sem, ld[q % 2].at(g, 16 * (q // 2 + 1)))
                t.wait_ge(xc.sem, xc.at(g, q))
                for i in range(4):
                    ins = nc.tensor.transpose(bank[0][:, i * P:(i + 1) * P], xs[q % 2][:, i * P:(i + 1) * P],
                                              core.ident)
                ins.then_inc(xt.sem, 1)

            def expert(g, q, i):
                return t.value_load(table[0:1, ds((g * quads + q) * 4 + i, 1)], min_val=0, max_val=experts - 1)

            def up_products(g, u):
                q, s = divmod(u, S)
                owners = [expert(g, q, s * PER + i) for i in range(PER)]
                t.wait_ge(xc.sem, xc.at(g, q + 1))
                t.wait_ge(hn.sem, hn.at(g, u - 1))
                for i, e in enumerate(owners):
                    lhs = xTs[q % 2][:, (s * PER + i) * P:(s * PER + i + 1) * P]
                    if 2 * width > 512:
                        for k in range(2):
                            ins = nc.tensor.matmul(bank[2 + u % 2 * 2 + k][:, 0:width], lhs,
                                                   up[:, ds(e * (2 * width) + k * width, width)],
                                                   start=True, stop=True)
                    else:
                        n = PER // 2
                        out = bank[2 + u % 2 * 2 + i // n][:, i % n * 2 * width:(i % n + 1) * 2 * width]
                        ins = nc.tensor.matmul(out, lhs, up[:, ds(e * (2 * width), 2 * width)], start=True, stop=True)
                ins.then_inc(gu.sem, 1)

            def turn_hidden(g, u):
                t.wait_ge(hn.sem, hn.at(g, u + 1))
                t.wait_ge(hc.sem, hc.at(g, u - 1))
                for j in range(4):
                    ins = nc.tensor.transpose(bank[6 + u % 2][0:rows, j * P:(j + 1) * P],
                                              hs[u % 2][:, j * rows:(j + 1) * rows], core.ident)
                ins.then_inc(ht.sem, 1)

            def down_products(g, u):
                q, s = divmod(u, S)
                owners = [expert(g, q, s * PER + i) for i in range(PER)]
                if s == 0:
                    t.wait_ge(yc.sem, yc.at(g, q))
                t.wait_ge(hc.sem, hc.at(g, u + 1))
                for i, e in enumerate(owners):
                    for k in range(tiles):
                        j = i * tiles + k
                        ins = nc.tensor.matmul(bank[1][:, (s * PER + i) * P:(s * PER + i + 1) * P],
                                               hTs[u % 2][0:rows, j * P:(j + 1) * P],
                                               down[0:rows, ds(e * (tiles * P) + k * P, P)],
                                               start=k == 0, stop=k == tiles - 1)
                ins.then_inc(dn.sem, 1)

            def step(g, u, first=False, last=False):
                if not (last and u == UNITS - 1):
                    up_products(g, u + 1)
                if u % S == 0 and not (last and u // S + AHEAD >= quads):
                    turn_x(g, u // S + AHEAD)
                turn_hidden(g, u)
                if not first:
                    down_products(g, u - 1)

            for q in range(AHEAD):
                turn_x(0, q)
            up_products(0, 0)
            run(t, step)
            down_products(LOOPS - 1, UNITS - 1)

        def act(a):
            fns["act"](a)
            with a.Fori(0, G) as g:
                if own_scores:
                    router.act(a, g, logits, (lg.sem, lg.at(g, 1)), (rt.sem, rt.at(g, 0)))
                else:
                    router.act(a, g)
            if shared:
                with a.Fori(0, G) as g:
                    for u in range(U):
                        a.wait_ge(ud.sem, ud.at(g, 2 * u + 1))
                        a.wait_ge(hd.sem, hd.at(g, u - 1))
                        nc.scalar.activation(sg[u % 2][0:rows], bank[u % 2 * 2][0:rows, :], ACT.Silu) \
                            .then_inc(sd.sem, 1)

            def copy_x(g, q):
                a.wait_ge(xt.sem, xt.at(g, q + 1))
                a.wait_ge(gu.sem, gu.at(g, (q - 1) * S))
                nc.scalar.activation(xTs[q % 2], bank[0], ACT.Copy).then_inc(xc.sem, 1)

            def silu(g, u):
                a.wait_ge(gu.sem, gu.at(g, u + 1))
                a.wait_ge(hn.sem, hn.at(g, u - 1))
                gate, _, out = unit_views(u, sgs[u % 2])
                nc.scalar.activation(out, gate, ACT.Silu).then_inc(si.sem, 1)

            def copy_y(g, q):
                a.wait_ge(dn.sem, dn.at(g, (q + 1) * S))
                a.wait_ge(stored[q % 2].sem, stored[q % 2].at(g, 16 * (q // 2)))
                nc.scalar.activation(ys[q % 2], bank[1], ACT.Copy).then_inc(yc.sem, 1)
                a.wait_ge(yc.sem, yc.at(g, q + 1))
                a.dma_start(y_tiles[:, ds((g * quads + q) * 4, 4), :],
                            ys[q % 2].rearrange("p (t d) -> p t d", d=P)).then_inc(stored[q % 2].sem, 16)

            def step(g, u, first=False, last=False):
                if not (last and u == UNITS - 1):
                    silu(g, u + 1)
                if u % S == 0 and not (last and u // S + AHEAD >= quads):
                    copy_x(g, u // S + AHEAD)
                if not first and u % S == 0:
                    copy_y(g, u // S - 1)

            for q in range(AHEAD):
                copy_x(0, q)
            silu(0, 0)
            run(a, step)
            copy_y(LOOPS - 1, quads - 1)

        def unit_views(u, out):
            if 2 * width > 512:
                return bank[2 + u % 2 * 2], bank[3 + u % 2 * 2], out
            n = PER // 2
            both = core.psum[:, (2 + u % 2 * 2) * 512:(4 + u % 2 * 2) * 512].rearrange("p (k w) -> p k w", k=2)
            both = both[:, :, 0:n * 2 * width].rearrange("p k (n f) -> p k n f", n=n)
            out = out[:, 0:PER * width].rearrange("p (k n f) -> p k n f", k=2, n=n)
            if n == 1:
                both, out = both[:, :, 0, :], out[:, :, 0, :]
                return both[:, :, 0:width], both[:, :, width:], out
            return both[:, :, :, 0:width], both[:, :, :, width:], out

        def dve(v):
            fns["dve"](v)
            v.wait_ge(w_in, loads)

            def shared_hidden(g, u):
                e, k = divmod(u, tiles)
                v.wait_ge(ud.sem, ud.at(g, 2 * u + 2))
                v.wait_ge(sd.sem, sd.at(g, u + 1))
                v.wait_ge(yd.sem, yd.at(g, e - 1))
                nc.vector.tensor_tensor(h[e % 2 * tiles + k][0:rows], sg[u % 2][0:rows],
                                        bank[u % 2 * 2 + 1][0:rows, :], ALU.mult).then_inc(hd.sem, 1)

            def add_shared(g, e):
                v.wait_ge(yd.sem, yd.at(g, e + 1))
                v.wait_ge(xd.sem, xd.at(g, e))
                xs_ = x[:, ds(g * GT, GT)]
                nc.vector.tensor_tensor(xs_, xs_, bank[4 + e % 2], ALU.add).then_inc(xd.sem, 1)

            with v.Fori(0, G) as g:
                v.wait_ge(lg.sem, lg.at(g, 1))
                router.dve(v, g, logits)
                nc.vector.tensor_copy(gates[:, ds(g * N, N)], router.comb)
                nc.vector.tensor_copy(chosen[:, ds(g * N, N)], router.mask).then_inc(rt.sem, 1)
                v.wait_ge(rt.sem, rt.at(g, 1))
            nc.vector.memset(router.pad, 0.0).then_inc(routed.sem, 1)
            v.wait_ge(routed.sem, routed.at(0, 1))

            BC = CHUNK // experts
            order = Steps(v, steps)
            link = order.link
            eb = lambda a_: a_.rearrange("p (e b) -> p e b", b=B)
            v.wait_ge(counted.sem, counted.at(0, 2 * CHUNKS))
            for c in range(CHUNKS):
                ins = nc.vector.tensor_copy(
                    count.rearrange("p (e b) -> p b e", b=B)[:, c * BC:(c + 1) * BC, :],
                    bank[4 + c][:, 0:CHUNK].rearrange("p (b e) -> p b e", e=experts))
            link(ins)
            link(nc.vector.tensor_tensor_scan(before, count, count, 0.0, ALU.add, ALU.max))
            link(nc.vector.tensor_copy(total, eb(before)[:, :, B - 1]))
            link(nc.vector.tensor_tensor(before, before, count, ALU.subtract))
            link(nc.vector.tensor_copy(first, eb(before)[:, :, 0]))
            link(nc.vector.tensor_tensor(total, total, first, ALU.subtract))
            link(nc.vector.tensor_scalar(n_tiles, total, 1.0 / P, 0.5 - 0.5 / P, ALU.mult, ALU.add))
            link(nc.vector.tensor_scalar(n_tiles, n_tiles, MAGIC, None, ALU.add))
            link(nc.vector.tensor_scalar(n_tiles, n_tiles, MAGIC, None, ALU.subtract))
            link(nc.vector.tensor_tensor_scan(ends, n_tiles, n_tiles, 0.0, ALU.add, ALU.max))
            link(nc.vector.tensor_tensor(base, ends, n_tiles, ALU.subtract))
            link(nc.vector.tensor_scalar(base, base, float(P), 1.0, ALU.mult, ALU.add))
            link(nc.vector.tensor_tensor(base, base, first, ALU.subtract))
            link(nc.vector.tensor_tensor(eb(before), eb(before), base.unsqueeze(2).to_broadcast([P, experts, B]),
                                         ALU.add))
            for c in range(CHUNKS):
                ins = nc.vector.tensor_tensor(
                    key[:, c * CHUNK:(c + 1) * CHUNK].rearrange("p (b e) -> p b e", e=experts),
                    bank[c][:, 0:CHUNK].rearrange("p (b e) -> p b e", e=experts),
                    before.rearrange("p (e b) -> p b e", b=B)[:, c * BC:(c + 1) * BC, :], ALU.add)
            link(ins)
            link(nc.vector.tensor_tensor(key, key, chosen, ALU.mult))
            for b in range(B):
                ins = nc.vector.max(best[:, b * 8:(b + 1) * 8], key[:, b * experts:(b + 1) * experts])
            link(ins)
            best3 = best.rearrange("p (b k) -> p b k", k=8)[:, :, 0:top_k]
            nc.vector.tensor_scalar(place.rearrange("p (b k) -> p b k", k=top_k), best3, 1.0, None, ALU.subtract) \
                .then_inc(placed.sem, 1)
            for c in range(COLS):
                link(nc.vector.tensor_scalar(total, ends, tile_id[:, c:c + 1], None, ALU.is_le))
                link(nc.vector.tensor_reduce(owner[:, c:c + 1], total, X, ALU.add))
            nc.vector.tensor_scalar(owner, owner, experts - 1.0, None, ALU.min).then_inc(owned.sem, 1)
            v.wait_ge(owner_row.sem, owner_row.at(0, 1))
            nc.vector.tensor_copy(table, bank[7][0:1, 0:COLS * P]).then_inc(tabled.sem, 1)
            if shared:
                with v.Fori(0, G) as g:
                    for u in range(U):
                        shared_hidden(g, u)
                        if u % tiles == tiles - 1 and u >= tiles:
                            add_shared(g, u // tiles - 1)
                    add_shared(g, shared - 1)
                v.wait_ge(xd.sem, xd.at(G, 0))
            for k in range(top_k):
                bc = best3[:, :, k:k + 1].to_broadcast([P, B, experts])
                k3 = lambda a_: a_.rearrange("p (b e) -> p b e", e=experts)
                link(nc.vector.tensor_tensor(k3(taken), k3(key), bc, ALU.is_equal))
                link(nc.vector.tensor_tensor(taken, taken, gates, ALU.mult))
                link(nc.vector.tensor_reduce(weight.rearrange("p (b k) -> p b k", k=top_k)[:, :, k], k3(taken),
                                             X, ALU.add))
            order.close()
            nc.vector.memset(router.pad, 0.0).then_inc(weighed.sem, 1)

            def hidden(g, u):
                v.wait_ge(gu.sem, gu.at(g, u + 1))
                v.wait_ge(si.sem, si.at(g, u + 1))
                v.wait_ge(ht.sem, ht.at(g, u - 1))
                _, upper, sg_ = unit_views(u, sgs[u % 2])
                _, _, out = unit_views(u, hs[u % 2])
                nc.vector.tensor_tensor(out, sg_, upper, ALU.mult).then_inc(hn.sem, 1)

            def step(g, u, first=False, last=False):
                v.wait_ge(ht.sem, ht.at(g, u + 1))
                v.wait_ge(dn.sem, dn.at(g, u - 1))
                nc.vector.tensor_copy(hTs[u % 2][0:rows], bank[6 + u % 2][0:rows, :]).then_inc(hc.sem, 1)
                if not (last and u == UNITS - 1):
                    hidden(g, u + 1)

            hidden(0, 0)
            run(v, step)

            with v.Fori(0, G) as g:
                c = Chain(v, mixing, g)
                for i in range(2):
                    v.wait_ge(ga[i].sem, ga[i].at(g, K2 * 16))
                    for k in range(top_k):
                        for b in range(2):
                            seq = g * GB + 2 * i + b
                            xs_ = x[:, ds(seq * P, P)]
                            n = b * top_k + k
                            ins = nc.vector.scalar_tensor_tensor(xs_, gathered[i][:, n * P:(n + 1) * P],
                                                                 weight[:, ds(seq * top_k + k, 1)], xs_,
                                                                 ALU.mult, ALU.add)
                        c.link(ins)
                    nc.vector.memset(router.pad, 0.0).then_inc(mixed.sem, 1)
                c.close()

        return dict(sp=sp, pool=pool, dve=dve, pe=pe, act=act), [(mixed.sem, mixed.at(G, 0))]

    return stage


BIAS_ROWS = {"a0_v": P, "a0_out": P, "ffn0": P, "a1_kv": 2 * P, "a1_off": 80, "a1_out": P, "router2": 8}
CONSTS = {"ident": P, "ones_row": P, "ones_row_cut": P, "head_mask": H, "neg_half": B,
          "dft_cos": P, "dft_sin": P, "dft_msin": P}


def build(nc, d, out, last_stage):
    with ExitStack() as ctx:
        core = Core(nc, ctx, d)
        core.x = core.sb("x", B * P)
        core.ctxT = core.sb("ctxT", B * P)
        core.xnT = core.sb("xnT", B * P)
        core.ln_stat, core.ln_moments = core.sb("ln_stat", 6 * B)[:, :], core.sb("ln_moments", 4 * B)
        core.ln_rstd, core.ln_xn = core.sb("ln_rstd", B)[:, :], core.sb("ln_xn", GT)
        consts = core.sb("consts", sum(CONSTS.values()))
        at = 0
        for name, n in CONSTS.items():
            core.const[name] = consts[:, at:at + n]
            at += n
        core.ident, core.ones_row = core.const["ident"], core.const["ones_row"]
        core.head_mask, core.neg_half = core.const["head_mask"], core.const["neg_half"]
        bias = core.sb("bias_rows", sum(BIAS_ROWS.values()))
        core.bias, at = {}, 0
        for name, n in BIAS_ROWS.items():
            core.bias[name] = bias[:, at:at + n]
            at += n
        cb = core.sb("consts_bf16", 3 * P + H * P, BF16)
        core.ident_b, core.sel_head = cb[:, 0:P], cb[:, P:P + H * P]
        core.earlier_b, core.ones_b = cb[:, P + H * P:2 * P + H * P], cb[:, 2 * P + H * P:3 * P + H * P]
        core.sorted_x = nc.dram_tensor("sorted_x", (SORTED_TILES * P, P), F32, kind="Internal").ap()

        WORDS = 35 * 1024
        area = core.sb("scratch", WORDS)

        loaded, stored = core.sem("loaded"), core.sem("stored")
        FILL = 16 * P
        zeros, zeroed, filled = area[:, WORDS - FILL:WORDS], core.sem("zeroed"), core.sem("filled")
        FILLS = SORTED_TILES * P // FILL
        start = [(loaded, 5 * 16)]
        stages = []
        for make in STAGES[:last_stage]:
            programs, start = make(core, Arena(area, WORDS if stages else WORDS - FILL), start)
            if not stages:
                start = start + [(filled, FILLS * 16)]
            stages.append(programs)

        block = ctx.enter_context(nc.Block())

        @block.sync
        def _(s):
            for sig in core.credits:
                s.sem_inc(sig.sem, sig.credit)
            s.dma_start(core.x[:, :].rearrange("p (b d) -> p b d", d=P), d["x"].rearrange("b p d -> p b d")) \
                .then_inc(loaded, 16)
            s.dma_start(consts[:, :], d["consts"]).then_inc(loaded, 16)
            s.dma_start(bias[:, :], d["bias_rows"]).then_inc(loaded, 16)
            s.dma_start(cb[:, :].bitcast(U16), d["consts_bf16"]).then_inc(loaded, 16)
            s.dma_start(core.ctxT[:, :].rearrange("p (b t) -> p b t", t=P), d["ctxT"].rearrange("b d t -> d b t")) \
                .then_inc(loaded, 16)
            for i, st in enumerate(stages):
                if "sp" in st:
                    st["sp"](s)
                if i == 0:
                    s.wait_ge(zeroed, 1)
                    with s.Fori(0, FILLS) as f:
                        s.dma_start(core.sorted_x.rearrange("(f p r) d -> f p (r d)", p=P, r=FILL // P)
                                    [ds(f, 1)].rearrange("o p w -> (o p) w"), zeros).then_inc(filled, 16)
            for sem, n in start:
                s.wait_ge(sem, n)
            s.dma_start(out.rearrange("b p d -> p b d"), core.x[:, :].rearrange("p (b d) -> p b d", d=P)) \
                .then_inc(stored, 16)
            s.wait_ge(stored, 16)

        @block.tensor
        def _(t):
            for st in stages:
                st["pe"](t)

        @block.scalar
        def _(a):
            for st in stages:
                st["act"](a)

        @block.vector
        def _(v):
            for st in stages:
                st["dve"](v)

        @block.gpsimd
        def _(p):
            nc.gpsimd.memset(zeros, 0.0).then_inc(zeroed, 1)
            for st in stages:
                st["pool"](p)


def bf16_bits(a):
    return (np.ascontiguousarray(a, np.float32).view(np.uint32) >> 16).astype(np.uint16)


def shape_constants():
    k = np.arange(P)
    row0 = np.zeros((P, P), np.float32)
    row0[0] = 1.0
    cut = row0.copy()
    cut[0, P - 1] = 0.0
    angle = 2.0 * np.pi * ((k[:, None] * k[None, :]) % P) / P
    tables = {
        "ident": np.eye(P), "ones_row": row0, "ones_row_cut": cut,
        "head_mask": k[:, None] // (P // H) == np.arange(H)[None, :],
        "neg_half": np.full((P, B), -0.5),
        "dft_cos": np.cos(angle), "dft_sin": np.sin(angle), "dft_msin": -np.sin(angle),
    }
    f32 = np.concatenate([np.asarray(tables[n], np.float32) for n in CONSTS], axis=1)
    sel = np.zeros((P, H, P), np.float32)
    for h in range(H):
        sel[h, h] = sel[H + h, h] = 1.0
    earlier = (k[:, None] < k[None, :]).astype(np.float32)
    return f32, bf16_bits(np.concatenate([np.eye(P, dtype=np.float32), sel.reshape(P, H * P), earlier,
                                          np.ones((P, P), np.float32)], axis=1))


def place_selectors(pairs=40):
    row = np.arange(P, dtype=np.float32)
    sel = np.zeros((P, pairs, P), np.float32)
    for r in range(pairs):
        sel[r, r] = 2.0 * row
        sel[pairs + r, r] = sel[2 * pairs + r, r] = -1.0
    high = ((1.0 - row * row).view(np.uint32) & 0xFFFF0000).view(np.float32)
    sel[3 * pairs], sel[3 * pairs + 1] = high, 1.0 - row * row - high
    return bf16_bits(sel.reshape(P, pairs * P))


def lay_out(a):
    rows = np.zeros((P, sum(BIAS_ROWS.values())), np.float32)
    parts = {"a0_v": [a["L0_xattn_b_v"]], "a0_out": [a["L0_xattn_b_out"]], "ffn0": [a["L0_ffn_bias"]],
             "a1_kv": [a["L1_xattn_bk"], a["L1_xattn_bv"]], "a1_off": [a["L1_xattn_boff"]],
             "a1_out": [a["L1_xattn_bo"]], "router2": [a["L2_ffn_router_b"]]}
    rows[0] = np.concatenate([v for n in BIAS_ROWS for v in parts[n]])
    f32, bf = shape_constants()
    out = {"x": a["x"], "ctx": a["ctx_1024"], "ctxT": a["ctx_1024"].transpose(0, 2, 1),
           "consts": f32, "consts_bf16": bf, "bias_rows": rows}
    out["a0_w"] = np.concatenate([a["L0_xattn_" + n].T for n in ("w_q", "w_k", "w_v", "w_out")], axis=1)
    out["a0_bqk"] = np.stack([a["L0_xattn_b_q"], a["L0_xattn_b_k"]], axis=1)
    out["f0_w"] = np.concatenate([a["L0_ffn_w_freq_real"], a["L0_ffn_w_freq_imag"]], axis=1)
    out["a1_w"] = np.concatenate([a["L1_xattn_" + n].T for n in ("Wq", "Woff", "Wk", "Wv", "Wo")], axis=1)
    out["a1_vecs"] = np.concatenate([a["L1_xattn_bq"][:, None], np.arange(P, dtype=np.float32)[:, None],
                                     np.tile(np.arange(-3, 2, dtype=np.float32), (P, H))], axis=1)
    out["a1_sel"] = place_selectors()
    out["a1_maskT"] = a["mask_BxS2_if0"].astype(np.int32).T
    out["a2_w"] = np.concatenate([a["L2_xattn_Wq"], a["L2_xattn_Wkv"],
                                  a["L2_xattn_Wout"].reshape(8, P, P).transpose(1, 0, 2).reshape(P, 8 * P)], axis=1)
    out["a2_ln"] = np.stack([a["L2_xattn_" + n] for n in ("ln1_w", "ln1_b", "ln2_w", "ln2_b")], axis=1)
    side = a["fside_Bx16_0"].reshape(B, 8, 2, 1)
    out["a2_shift"] = np.broadcast_to(side, (B, 8, 2, 64)).transpose(2, 3, 0, 1).reshape(P, B * 8)
    out["a3_w"] = np.concatenate([a["L3_xattn_Wq"].T, a["L3_xattn_Wk"].T], axis=1)
    out["a3_bqk"] = np.stack([a["L3_xattn_bq"], a["L3_xattn_bk"]], axis=1)
    reset = np.ones((P, GB, 64), np.float32)
    reset[:, :, 0] = 0.0
    out["reset64"] = reset.reshape(P, GB * 64)
    out["tile_id"] = (np.arange(3)[None, :] * P + np.arange(P)[:, None]).astype(np.float32)
    out["reset"] = np.tile(reset[:, 0, 0:8], (1, GB))
    w_up = np.concatenate([a["L1_ffn_w_up"], np.concatenate([a["L1_ffn_sg_gate"], a["L1_ffn_sg_up"]])[None]])
    w_down = np.concatenate([a["L1_ffn_w_down"], a["L1_ffn_sg_down"][None]])
    out["m1_up"] = w_up.transpose(2, 0, 1).reshape(P, -1)
    out["m1_down"] = w_down.transpose(2, 0, 1).reshape(2, 96, 9, P).transpose(1, 2, 0, 3).reshape(96, -1)
    out["m1_gate"] = a["L1_ffn_gate_w"].T
    out["m2_up"] = a["L2_ffn_w1"].transpose(1, 0, 2).reshape(P, -1)
    out["m2_down"] = a["L2_ffn_w2"].reshape(8, 4, P, P).transpose(2, 0, 1, 3).reshape(P, -1)
    out["m2_gate"] = a["L2_ffn_router_w"]
    gu = np.stack([np.concatenate([a["L3_ffn_Wg"], a["L3_ffn_Sg"].reshape(2, 88, P)]),
                   np.concatenate([a["L3_ffn_Wu"], a["L3_ffn_Su"].reshape(2, 88, P)])], axis=1)
    out["m3_up"] = gu.transpose(3, 0, 1, 2).reshape(P, -1)
    dn = np.concatenate([a["L3_ffn_Wd"], a["L3_ffn_Sd"].reshape(P, 2, 88).transpose(1, 0, 2)])
    out["m3_down"] = dn.transpose(2, 0, 1).reshape(88, -1)
    out["m3_gate"] = a["L3_ffn_gate_w"].T
    out["m3_bias"] = np.broadcast_to(a["L3_ffn_gate_bias"], (P, 64))
    return out


SORTED_TILES = 320

STAGES = [stage_attention0, stage_fourier_ffn, stage_attention1,
          stage_experts("m1", Top2Softmax, 8, 2, 1, 192, 96, 2), stage_attention2,
          stage_experts("m2", Top1Softmax, 8, 1, 0, 512, P, 2, "router2"), stage_attention3,
          stage_experts("m3", GroupedTop8, 64, 8, 2, 88, 88, 4)]


def kernel(**inputs):
    import numpy as _np
    import concourse.bacc as _bacc
    from concourse import mybir as _mybir
    from concourse.bass_utils import run_bass_kernel_spmd as _run

    nc = _bacc.Bacc("TRN2", target_bir_lowering=False, num_devices=1)
    arrays, aps = {}, {}
    for name, a in lay_out({k: _np.asarray(v) for k, v in inputs.items()}).items():
        arrays[f"in_{name}"] = _np.ascontiguousarray(a)
        aps[name] = nc.dram_tensor(f"in_{name}", a.shape, _mybir.dt.from_np(a.dtype), kind="ExternalInput").ap()
    out = nc.dram_tensor("out_0", (B, P, P), F32, kind="ExternalOutput").ap()
    build(nc, aps, out, LAST_STAGE)
    return _run(nc, [arrays], core_ids=[0]).results[0]["out_0"]
LAST_STAGE = 8
```

```python
from contextlib import ExitStack

import numpy as np

import concourse.bass as bass
from concourse import mybir

F32 = mybir.dt.float32
BF16 = mybir.dt.bfloat16
I32 = mybir.dt.int32
U16 = mybir.dt.uint16
U32 = mybir.dt.uint32
ALU = mybir.AluOpType
ACT = mybir.ActivationFunctionType
X = mybir.AxisListType.X
ds = bass.ds

P = 128
B = 32
GB = 4
G = B // GB
GT = GB * P
EPS = 1e-5
MAGIC = 1.5 * 2.0 ** 23
CREDIT = 129
H = 16


class Counter:

    def __init__(self, sem, per, earlier=0):
        self.sem, self.per, self.credit = sem, per, per + 1 + earlier

    def at(self, g, n):
        return g * self.per + (self.credit + n)


class Chain:

    def __init__(self, eng, sig, g, n=0):
        self.eng, self.sig, self.g, self.n = eng, sig, g, n

    def link(self, ins):
        self.n += 1
        ins.then_inc(self.sig.sem, 1)
        self.eng.wait_ge(self.sig.sem, self.sig.at(self.g, self.n))

    def close(self):
        assert self.n == self.sig.per, (self.n, self.sig.per)


def run_sequences(eng, step, chain=None, links=0):
    c = lambda g: (Chain(eng, chain, g, links),) if chain else ()
    with eng.Fori(0, G - 1) as g:
        cs = c(g)
        for b in range(1, GB + 1):
            step(g, b, *cs)
    cs = c(G - 1)
    for b in range(1, GB):
        step(G - 1, b, *cs)


def more(g, b):
    return not isinstance(g, int) or g * GB + b < B


class Steps:

    def __init__(self, eng, sig):
        self.eng, self.sig, self.n = eng, sig, 0

    def link(self, ins):
        self.n += 1
        ins.then_inc(self.sig.sem, 1)
        self.eng.wait_ge(self.sig.sem, self.sig.at(0, self.n))

    def close(self):
        assert self.n == self.sig.per, (self.n, self.sig.per)


class Arena:

    def __init__(self, tensor, words, from_end):
        self.tensor, self.words, self.used, self.from_end = tensor, words, 0, from_end

    def take(self, n, dt=F32):
        words = n if dt == F32 else (n + 1) // 2
        assert self.used + words <= self.words, (self.used, words, self.words)
        at = self.words - self.used - words if self.from_end else self.used
        v = self.tensor[:, at:at + words]
        self.used += words
        return v if dt == F32 else v.bitcast(dt)


class Core:

    def __init__(self, nc, ctx, dram):
        self.nc, self.ctx, self.dram = nc, ctx, dram
        self.credits, self.const, self.shared_sems = [], {}, {}
        self.psum = ctx.enter_context(nc.psum_tensor("psum", [P, 8 * 512], F32))
        self.bank = [self.psum[:, i * 512:(i + 1) * 512] for i in range(8)]
        self.ln_passes = self.ln_turns = 0
        self.ln_sems = [self.sem(f"ln_{n}") for n in ("stats", "var", "rstd", "chain")]
        self.ln_xn_done = self.counter("ln_xn", GB)
        self.ln_turned = self.counter("ln_turned", 2)
        self.ln_copied = self.counter("ln_copied", 2)
        self.ln_ring = self.counter("ln_ring", GB)
        self.ln_rings = 0

    def sb(self, name, n, dt=F32):
        return self.ctx.enter_context(self.nc.sbuf_tensor(name, [P, n], dt))

    def sem(self, name):
        return self.ctx.enter_context(self.nc.semaphore(name))

    def counter(self, name, per):
        s = Counter(self.sem(name), per)
        self.credits.append(s)
        return s

    def shared_counter(self, name, per, loops, credit=CREDIT):
        if name not in self.shared_sems:
            self.shared_sems[name] = [self.sem(name), 0]
            if credit:
                self.credits.append(Counter(self.shared_sems[name][0], credit - 1))
        entry = self.shared_sems[name]
        c = Counter(entry[0], per)
        c.credit = credit + entry[1]
        entry[1] += per * loops
        return c


def layernorm(core, src, start, dst_natural=None, dst_t=None, t_scale=None, t_bias=None, keep=None):
    nc = core.nc
    stat, moments, rstd, xn = core.ln_stat, core.ln_moments, core.ln_rstd, core.ln_xn
    n = core.ln_passes
    core.ln_passes += 1
    stats_done, var_done, rstd_done, chain = core.ln_sems
    xn_done = Counter(core.ln_xn_done.sem, GB, n * B)
    turned = Counter(core.ln_turned.sem, 2, core.ln_turns * 2 * G)
    copied = Counter(core.ln_copied.sem, 2, core.ln_turns * 2 * G)
    ring = Counter(core.ln_ring.sem, GB, core.ln_rings * B)
    core.ln_turns += dst_natural is None
    core.ln_rings += keep is not None
    st = stat.rearrange("p (b s) -> p b s", s=6)

    def dve(v):
        for s, value in start:
            v.wait_ge(s, value)
        with v.Fori(0, G) as g:
            for b in range(GB):
                nc.vector.bn_stats(stat[:, ds((g * GB + b) * 6, 6)], src[:, ds((g * GB + b) * P, P)]) \
                    .then_inc(stats_done, 1)
        v.wait_ge(stats_done, (n + 1) * B)
        mean, delta, dev, var = (moments[:, i * B:(i + 1) * B] for i in range(4))
        nc.vector.tensor_tensor(mean, st[:, :, 1], st[:, :, 4], ALU.add).then_inc(chain, 1)
        nc.vector.tensor_tensor(delta, st[:, :, 1], st[:, :, 4], ALU.subtract).then_inc(chain, 1)
        nc.vector.tensor_tensor(dev, st[:, :, 2], st[:, :, 5], ALU.add).then_inc(chain, 1)
        v.wait_ge(chain, 6 * n + 3)
        nc.vector.tensor_scalar(mean, mean, 0.5, None, ALU.mult).then_inc(chain, 1)
        nc.vector.scalar_tensor_tensor(delta, delta, 0.25, delta, ALU.mult, ALU.mult).then_inc(chain, 1)
        nc.vector.tensor_scalar(dev, dev, 1.0 / P, EPS, ALU.mult, ALU.add).then_inc(chain, 1)
        v.wait_ge(chain, 6 * n + 6)
        nc.vector.tensor_tensor(var, dev, delta, ALU.add).then_inc(var_done, 1)
        v.wait_ge(rstd_done, n + 1)
        with v.Fori(0, G) as g:
            for b in range(GB):
                if keep is not None:
                    out = keep[:, ds((g * GB + b) * P, P)]
                elif dst_natural is None:
                    v.wait_ge(turned.sem, turned.at(g, b // 2 - 1))
                    out = xn[:, b * P:(b + 1) * P]
                else:
                    out = dst_natural[:, ds((g * GB + b) * P, P)]
                nc.vector.tensor_scalar(out, src[:, ds((g * GB + b) * P, P)], mean[:, ds(g * GB + b, 1)],
                                        rstd[:, ds(g * GB + b, 1)], ALU.subtract, ALU.mult) \
                    .then_inc(xn_done.sem, 1)

    def pool(p):
        p.wait_ge(var_done, n + 1)
        nc.gpsimd.tensor_tensor(rstd, moments[:, 3 * B:4 * B], core.neg_half, ALU.pow).then_inc(rstd_done, 1)
        if keep is None:
            return
        with p.Fori(0, G) as g:
            for b in range(GB):
                p.wait_ge(xn_done.sem, xn_done.at(g, b + 1))
                p.wait_ge(turned.sem, turned.at(g, b // 2 - 1))
                nc.gpsimd.tensor_copy(xn[:, b * P:(b + 1) * P], keep[:, ds((g * GB + b) * P, P)]) \
                    .then_inc(ring.sem, 1)

    def pe(t):
        for s, value in start:
            t.wait_ge(s, value)
        with t.Fori(0, G) as g:
            for half in range(2):
                t.wait_ge(copied.sem, copied.at(g, half - 1))
                for b in (2 * half, 2 * half + 1):
                    xn_here = xn_done if keep is None else ring
                    t.wait_ge(xn_here.sem, xn_here.at(g, b + 1))
                    ins = nc.tensor.transpose(core.bank[half][:, b % 2 * P:(b % 2 + 1) * P],
                                              xn[:, b * P:(b + 1) * P], core.ident)
                ins.then_inc(turned.sem, 1)

    def act(a):
        with a.Fori(0, G) as g:
            for half in range(2):
                a.wait_ge(turned.sem, turned.at(g, half + 1))
                out = dst_t[:, ds(g * GT + half * 2 * P, 2 * P)]
                if t_scale is None:
                    ins = nc.scalar.activation(out, core.bank[half][:, 0:2 * P], ACT.Copy)
                else:
                    ins = nc.scalar.activation(out, core.bank[half][:, 0:2 * P], ACT.Identity,
                                               bias=t_bias, scale=t_scale)
                ins.then_inc(copied.sem, 1)

    if dst_natural is not None:
        return dict(dve=dve, pool=pool), (xn_done.sem, xn_done.at(G, 0))
    return dict(dve=dve, pool=pool, pe=pe, act=act), (copied.sem, copied.at(G, 0))


def stage_attention0(core, arena, start):
    nc, d, bank = core.nc, core.dram, core.bank
    DH, QUADS = P // H, H // GB
    SCALE = 1.0 / DH ** 0.5
    xnT, ctxT, x = core.xnT, core.ctxT, core.x
    w = arena.take(4 * P)
    wq, wk, wv, wo = (w[:, i * P:(i + 1) * P] for i in range(4))
    bqk = arena.take(2)
    qT, kT = arena.take(GT), arena.take(GT)
    qm = [arena.take(H * P) for _ in range(GB)]
    cT = arena.take(GB * P)
    vaug = arena.take(GB * H * (DH + 1)).rearrange("p (b h e) -> p b h e", b=GB, h=H)
    nm = arena.take(2 * H)
    nm2 = [arena.take(P, BF16) for _ in range(2)]
    nmT = [arena.take(P, BF16) for _ in range(2)]
    pT = [arena.take(GT) for _ in range(2)]
    rsum = arena.take(2 * H)
    ao, aoT = arena.take(2 * P), arena.take(2 * P)

    w_in = core.sem("a0_w_in")
    ones_set = core.sem("a0_ones_set")
    fns, (ln_sem, ln_n) = layernorm(core, x, start, dst_t=xnT)
    proj = core.shared_counter("att_proj", GB, G)
    qkv = core.shared_counter("att_qkv", 3 * GB, G)
    ct = core.shared_counter("att_ct", GB, G)
    qm_v = core.shared_counter("att_qm_v", GB, G)
    qm_p = core.shared_counter("att_qm_p", GB, G)
    nat = core.shared_counter("att_nat", GB * QUADS, G)
    mx = core.shared_counter("att_mx", GB * QUADS, G)
    nms = core.shared_counter("att_nms", GB, G)
    nmt = core.shared_counter("att_nmt", GB, G)
    nmc = core.shared_counter("att_nmc", GB, G)
    st = core.shared_counter("att_st", GB * QUADS, G)
    ex = core.shared_counter("att_ex", GB * QUADS, G)
    av = core.shared_counter("att_av", GB * QUADS, G)
    aon = core.shared_counter("att_aon", GB, G)
    aot = core.shared_counter("att_aot", GB, G)
    aoc = core.shared_counter("att_aoc", GB, G)
    yd = core.shared_counter("att_yd", GB, G)
    xd = core.shared_counter("att_xd", GB, G)
    chain = core.shared_counter("att_chain", 2 * GB, G)

    def load(s):
        s.dma_start(w, d["a0_w"]).then_inc(w_in, 16)
        s.dma_start(bqk, d["a0_bqk"]).then_inc(w_in, 16)
        s.dma_start(core.bias_all, d["bias_rows"]).then_inc(w_in, 16)
        s.dma_start(core.bf16_all.bitcast(U16), d["consts_bf16"]).then_inc(w_in, 16)
        s.dma_start(ctxT[:, :], d["ctxT"]).then_inc(w_in, 16)

    def pool(p):
        nc.gpsimd.memset(vaug[:, :, :, DH:DH + 1], 1.0).then_inc(ones_set, 1)
        for t in nm2:
            nc.gpsimd.memset(t, 0.0).then_inc(ones_set, 1)
        fns["pool"](p)
        p.wait_ge(w_in, 80)

        def prepare(g, b):
            if not more(g, b):
                return
            p.wait_ge(proj.sem, proj.at(g, b - GB + 1))
            nc.gpsimd.tensor_copy(cT[:, b % GB * P:(b % GB + 1) * P], ctxT[:, ds((g * GB + b) * P, P)]) \
                .then_inc(ct.sem, 1)
            p.wait_ge(qkv.sem, qkv.at(g, 3 * b + 1))
            p.wait_ge(st.sem, st.at(g, (b - GB + 1) * QUADS))
            half = H // 2
            nc.gpsimd.tensor_tensor(
                qm[b % GB][:, half * P:].rearrange("p (h q) -> p h q", h=half),
                qT[:, b % GB * P:(b % GB + 1) * P].unsqueeze(1).to_broadcast([P, half, P]),
                core.head_mask[:, half:H].unsqueeze(2).to_broadcast([P, half, P]), ALU.mult) \
                .then_inc(qm_p.sem, 1)

        with p.Fori(0, G) as g:
            for b in range(GB):
                prepare(g, b)

    def dve(v):
        fns["dve"](v)
        v.wait_ge(ones_set, 3)

        def mask_q(g, b):
            v.wait_ge(qkv.sem, qkv.at(g, 3 * b + 1))
            v.wait_ge(st.sem, st.at(g, (b - GB + 1) * QUADS))
            half = H // 2
            nc.vector.tensor_tensor(
                qm[b % GB][:, 0:half * P].rearrange("p (h q) -> p h q", h=half),
                qT[:, b % GB * P:(b % GB + 1) * P].unsqueeze(1).to_broadcast([P, half, P]),
                core.head_mask[:, 0:half].unsqueeze(2).to_broadcast([P, half, P]), ALU.mult) \
                .then_inc(qm_v.sem, 1)

        def row_max(g, b, c):
            n = nm[:, b % 2 * H:b % 2 * H + H]
            for t in range(QUADS):
                v.wait_ge(nat.sem, nat.at(g, b * QUADS + t + 1))
                nc.vector.tensor_reduce(n[:, t * 4:t * 4 + 4], bank[t % 2][:, :].rearrange("p (h k) -> p h k", h=4),
                                        X, ALU.max, negate=True).then_inc(mx.sem, 1)
            v.wait_ge(nmt.sem, nmt.at(g, b - 1))
            v.wait_ge(mx.sem, mx.at(g, (b + 1) * QUADS))
            c.link(nc.vector.tensor_copy(nm2[b % 2][:, 0:H], n))
            nc.vector.tensor_tensor(nm2[b % 2][:, H:2 * H], n, nm2[b % 2][:, 0:H], ALU.subtract) \
                .then_inc(nms.sem, 1)

        def normalise(g, b, c):
            v.wait_ge(av.sem, av.at(g, (b + 1) * QUADS))
            o = bank[4 + b % 2][:, 0:H * (DH + 1)].rearrange("p (h e) -> p h e", h=H)
            r = rsum[:, b % 2 * H:b % 2 * H + H]
            c.link(nc.vector.reciprocal(r, o[:, :, DH]))
            v.wait_ge(aot.sem, aot.at(g, b - 1))
            nc.vector.tensor_tensor(ao[:, b % 2 * P:(b % 2 + 1) * P].rearrange("p (h e) -> p h e", h=H),
                                    o[:, :, 0:DH], r.unsqueeze(2).to_broadcast([P, H, DH]), ALU.mult) \
                .then_inc(aon.sem, 1)

        def update(g, b):
            v.wait_ge(yd.sem, yd.at(g, b + 1))
            xs = x[:, ds((g * GB + b) * P, P)]
            nc.vector.tensor_tensor(xs, xs, bank[6][:, P:2 * P], ALU.add).then_inc(xd.sem, 1)

        def step(g, b, c):
            if more(g, b + 1):
                row_max(g, b + 1, c)
            if more(g, b + 2):
                mask_q(g, b + 2)
            if b:
                update(g, b - 1)
            normalise(g, b, c)

        c = Chain(v, chain, 0)
        mask_q(0, 0)
        mask_q(0, 1)
        row_max(0, 0, c)
        step(0, 0, c)
        run_sequences(v, step, chain, c.n)
        update(G - 1, GB - 1)

    def pe(t):
        fns["pe"](t)
        t.wait_ge(w_in, 80)
        t.wait_ge(ln_sem, ln_n)

        def natural(g, b, quads=range(QUADS)):
            t.wait_ge(qm_v.sem, qm_v.at(g, b + 1))
            t.wait_ge(qm_p.sem, qm_p.at(g, b + 1))
            if 0 in quads:
                t.wait_ge(qkv.sem, qkv.at(g, 3 * b + 3))
            for q in quads:
                t.wait_ge(mx.sem, mx.at(g, b * QUADS + q - 1))
                for i in range(4):
                    h = q * 4 + i
                    ins = nc.tensor.matmul(bank[q % 2][:, i * P:(i + 1) * P], qm[b % GB][:, h * P:(h + 1) * P],
                                           kT[:, b % GB * P:(b % GB + 1) * P], start=True, stop=True)
                ins.then_inc(nat.sem, 1)

        def turn_max(g, b):
            t.wait_ge(nms.sem, nms.at(g, b + 1))
            t.wait_ge(nmc.sem, nmc.at(g, b))
            if more(g, b + 1):
                t.wait_ge(qkv.sem, qkv.at(g, 3 * (b + 2)))
            nc.tensor.transpose(bank[7][:, 0:P // 2].bitcast(BF16), nm2[b % 2], core.ident_b).then_inc(nmt.sem, 1)

        def attend(g, b):
            def av_quad(q):
                n = b * QUADS + q
                t.wait_ge(ex.sem, ex.at(g, n + 1))
                if q == 0:
                    t.wait_ge(aon.sem, aon.at(g, b - 1))
                for i in range(4):
                    h = q * 4 + i
                    ins = nc.tensor.matmul(bank[4 + b % 2][:, h * (DH + 1):(h + 1) * (DH + 1)],
                                           pT[q % 2][:, i * P:(i + 1) * P], vaug[:, b % GB, h, :], start=True, stop=True)
                ins.then_inc(av.sem, 1)

            t.wait_ge(nmc.sem, nmc.at(g, b + 1))
            for q in range(QUADS):
                n = b * QUADS + q
                t.wait_ge(ex.sem, ex.at(g, n - 1))
                nc.tensor.matmul(bank[2 + q % 2][:, :], kT[:, b % GB * P:(b % GB + 1) * P],
                                 qm[b % GB][:, q * 4 * P:(q * 4 + 4) * P], start=True, stop=False)
                for i in range(4):
                    h = q * 4 + i
                    ins = nc.tensor.matmul(bank[2 + q % 2][:, i * P:(i + 1) * P], core.sel_head[:, h * P:(h + 1) * P],
                                           nmT[b % 2], start=False, stop=i == 3)
                ins.then_inc(st.sem, 1)
                if more(g, b + 1):
                    natural(g, b + 1, [q])
                if q:
                    av_quad(q - 1)
                if b and q == 1:
                    turn_out(g, b - 1)
                if b and q == 3:
                    project_out(g, b - 1)
            av_quad(QUADS - 1)

        def turn_out(g, b):
            t.wait_ge(aon.sem, aon.at(g, b + 1))
            t.wait_ge(xd.sem, xd.at(g, b))
            nc.tensor.transpose(bank[6][:, 0:P], ao[:, b % 2 * P:(b % 2 + 1) * P], core.ident).then_inc(aot.sem, 1)

        def project_out(g, b):
            t.wait_ge(aoc.sem, aoc.at(g, b + 1))
            nc.tensor.matmul(bank[6][:, P:2 * P], aoT[:, b % 2 * P:(b % 2 + 1) * P], wo, start=True, stop=False)
            nc.tensor.matmul(bank[6][:, P:2 * P], core.ones_row, core.bias["a0_out"], start=False, stop=True) \
                .then_inc(yd.sem, 1)

        def project(g, b):
            t.wait_ge(nmc.sem, nmc.at(g, b - 1))
            t.wait_ge(qkv.sem, qkv.at(g, 3 * b))
            at = ds((g * GB + b) * P, P)
            nc.tensor.matmul(bank[7][:, P:2 * P], wq, xnT[:, at], start=True, stop=True)
            nc.tensor.matmul(bank[7][:, 2 * P:3 * P], wk, ctxT[:, at], start=True, stop=True)
            t.wait_ge(ct.sem, ct.at(g, b + 1))
            nc.tensor.matmul(bank[7][:, 3 * P:4 * P], cT[:, b % GB * P:(b % GB + 1) * P], wv, start=True, stop=False)
            nc.tensor.matmul(bank[7][:, 3 * P:4 * P], core.ones_row, core.bias["a0_v"], start=False, stop=True) \
                .then_inc(proj.sem, 1)

        def step(g, b):
            if more(g, b + 2):
                project(g, b + 2)
            attend(g, b)
            if more(g, b + 1):
                turn_max(g, b + 1)

        project(0, 0)
        project(0, 1)
        natural(0, 0)
        turn_max(0, 0)
        step(0, 0)
        run_sequences(t, step)
        turn_out(G - 1, GB - 1)
        project_out(G - 1, GB - 1)

    def act(a):
        fns["act"](a)
        a.wait_ge(w_in, 80)
        a.wait_ge(ones_set, 3)

        def copy_max(g, b):
            a.wait_ge(nmt.sem, nmt.at(g, b + 1))
            a.wait_ge(st.sem, st.at(g, (b - 1) * QUADS))
            nc.scalar.activation(nmT[b % 2], bank[7][:, 0:P // 2].bitcast(BF16), ACT.Copy).then_inc(nmc.sem, 1)

        def exps(g, b):
            for q in range(QUADS):
                n = b * QUADS + q
                a.wait_ge(st.sem, st.at(g, n + 1))
                a.wait_ge(av.sem, av.at(g, n - 1))
                nc.scalar.activation(pT[q % 2], bank[2 + q % 2][:, :], ACT.Exp, scale=SCALE).then_inc(ex.sem, 1)
                if b and q == 1:
                    copy_ao(g, b - 1)

        def copy_ao(g, b):
            a.wait_ge(aot.sem, aot.at(g, b + 1))
            a.wait_ge(yd.sem, yd.at(g, b - 1))
            nc.scalar.activation(aoT[:, b % 2 * P:(b % 2 + 1) * P], bank[6][:, 0:P], ACT.Copy).then_inc(aoc.sem, 1)

        def copy_qkv(g, b):
            if not more(g, b):
                return
            a.wait_ge(proj.sem, proj.at(g, b + 1))
            a.wait_ge(qm_v.sem, qm_v.at(g, b - GB + 1))
            a.wait_ge(qm_p.sem, qm_p.at(g, b - GB + 1))
            slot = slice(b % GB * P, (b % GB + 1) * P)
            nc.scalar.activation(qT[:, slot], bank[7][:, P:2 * P], ACT.Identity, bias=bqk[:, 0:1]).then_inc(qkv.sem, 1)
            nc.scalar.activation(kT[:, slot], bank[7][:, 2 * P:3 * P], ACT.Identity, bias=bqk[:, 1:2]) \
                .then_inc(qkv.sem, 1)
            nc.scalar.activation(vaug[:, b % GB, :, 0:DH], bank[7][:, 3 * P:4 * P].rearrange("p (h e) -> p h e", h=H),
                                 ACT.Copy).then_inc(qkv.sem, 1)

        def step(g, b):
            copy_qkv(g, b + 2)
            exps(g, b)
            if more(g, b + 1):
                copy_max(g, b + 1)

        copy_qkv(0, 0)
        copy_qkv(0, 1)
        copy_max(0, 0)
        step(0, 0)
        run_sequences(a, step)
        copy_ao(G - 1, GB - 1)

    return dict(load=load, pool=pool, dve=dve, pe=pe, act=act), [(xd.sem, xd.at(G, 0))]


def stage_fourier_ffn(core, arena, start):
    nc, d, bank = core.nc, core.dram, core.bank
    x, xnT = core.x, core.xnT
    cos, sin, msin = (core.const[n] for n in ("dft_cos", "dft_sin", "dft_msin"))
    w = arena.take(2 * P)
    wr, wi = w[:, 0:P], w[:, P:2 * P]
    ab, m = arena.take(2 * P), arena.take(P)
    xT = arena.take(GT)

    fns, ln_done = layernorm(core, x, start, dst_t=xnT)
    w_in = core.sem("f0_w_in")
    pre, prec = core.sem("f0_pre"), core.sem("f0_prec")
    ct = core.counter("f0_ct", 2)
    yd = core.counter("f0_yd", 2)
    xd = core.counter("f0_xd", 2)

    def load(s):
        s.dma_start(w, d["f0_w"]).then_inc(w_in, 16)

    def pool(p):
        fns["pool"](p)
        p.wait_ge(*ln_done)
        with p.Fori(0, G) as g:
            for half in range(2):
                p.wait_ge(yd.sem, yd.at(g, half - 1))
                nc.gpsimd.tensor_copy(xT[:, half * 2 * P:(half + 1) * 2 * P],
                                      xnT[:, ds(g * GT + half * 2 * P, 2 * P)]).then_inc(ct.sem, 1)

    def pe(t):
        fns["pe"](t)
        t.wait_ge(w_in, 16)
        nc.tensor.matmul(bank[4][:, 0:P], wr, cos, start=True, stop=False)
        nc.tensor.matmul(bank[4][:, 0:P], wi, sin, start=False, stop=True)
        nc.tensor.matmul(bank[4][:, P:2 * P], wi, cos, start=True, stop=False)
        nc.tensor.matmul(bank[4][:, P:2 * P], wr, msin, start=False, stop=True).then_inc(pre, 1)
        t.wait_ge(prec, 1)
        nc.tensor.matmul(bank[5][:, 0:P], ab[:, 0:P], cos, start=True, stop=False)
        nc.tensor.matmul(bank[5][:, 0:P], ab[:, P:2 * P], msin, start=False, stop=True).then_inc(pre, 1)
        t.wait_ge(prec, 2)
        with t.Fori(0, G) as g:
            for half in range(2):
                t.wait_ge(ct.sem, ct.at(g, half + 1))
                t.wait_ge(xd.sem, xd.at(g, half - 1))
                for b in range(2):
                    out = bank[2 + half][:, b * P:(b + 1) * P]
                    nc.tensor.matmul(out, xT[:, (half * 2 + b) * P:(half * 2 + b + 1) * P], m, start=True, stop=False)
                    ins = nc.tensor.matmul(out, core.ones_row, core.bias["ffn0"], start=False, stop=True)
                ins.then_inc(yd.sem, 1)

    def act(a):
        fns["act"](a)
        a.wait_ge(pre, 1)
        nc.scalar.activation(ab, bank[4][:, 0:2 * P], ACT.Copy).then_inc(prec, 1)
        a.wait_ge(pre, 2)
        nc.scalar.activation(m, bank[5][:, 0:P], ACT.Copy, scale=1.0 / P).then_inc(prec, 1)

    def dve(v):
        fns["dve"](v)
        with v.Fori(0, G) as g:
            for half in range(2):
                v.wait_ge(yd.sem, yd.at(g, half + 1))
                xs = x[:, ds(g * GT + half * 2 * P, 2 * P)]
                nc.vector.tensor_tensor(xs, xs, bank[2 + half][:, 0:2 * P], ALU.add).then_inc(xd.sem, 1)

    return dict(load=load, pool=pool, dve=dve, pe=pe, act=act), [(xd.sem, xd.at(G, 0))]


def stage_attention1(core, arena, start):
    nc, d, bank = core.nc, core.dram, core.bank
    x, xnT, ctxT = core.x, core.xnT, core.ctxT
    NK, DH = 5, P // H
    R = H * NK
    HR = R // 2
    QUADS, CH = R // 4, 4
    QC = QUADS // CH
    NQ = GB * QUADS
    SCALE = 0.5 / DH ** 0.5
    CW = P + 2

    w = arena.take(P + R + 2 * P + P)
    wq, woff, wkv, wo = w[:, 0:P], w[:, P:P + R], w[:, P + R:3 * P + R], w[:, 3 * P + R:4 * P + R]
    vecs = arena.take(2 + R)
    bq, token, ref = vecs[:, 0:1], vecs[:, 1:2], vecs[:, 2:2 + R]
    sel = arena.take(HR * P, BF16)
    mask_i = arena.take(B)
    om, ones, slen, rslen = arena.take(B), arena.take(P), arena.take(B), arena.take(B)
    qpT, qn = arena.take(GT), arena.take(GT)
    cT = arena.take(GB * CW)
    t_, n_, m_, ix, i0, dx = (arena.take(GB * R) for _ in range(6))
    w01 = arena.take(GB * R * 2)
    rows = arena.take(GB * 2 * P, BF16)
    rT = arena.take(GB * 2 * P, BF16)
    kvs = [arena.take(3 * GT, BF16) for _ in range(2)]
    kvr = arena.take(GT)
    oh = [arena.take(GT, BF16) for _ in range(4)]
    prod = arena.take(QC * 4 * 2 * DH)
    sp_, s2, sc, ee, pw, aw = (arena.take(n) for n in (2 * 2 * R, 2 * R, R, R, R, 2 * R))
    mxs, sm = arena.take(H), arena.take(H)
    gv = [arena.take(2 * R * DH) for _ in range(2)]
    pv = arena.take(2 * R * DH)
    cx, cxT = arena.take(P), arena.take(P)
    G2 = [core.psum[:, 3 * 512:3 * 512 + QC * 128], core.psum[:, 5 * 512:5 * 512 + QC * 128]]

    w_in, set_, pre = core.sem("a1_w_in"), core.sem("a1_set"), core.sem("a1_pre")
    lens = core.sem("a1_lens")
    fns, ln_done = layernorm(core, x, start, dst_t=xnT)
    pj = core.counter("a1_pj", 4)
    pc = core.counter("a1_pc", 3)
    idx = core.counter("a1_idx", 1)
    ct = core.counter("a1_ct", GB)
    kvp = core.counter("a1_kvp", GB)
    kvh = core.counter("a1_kvh", GB)
    kvd = core.counter("a1_kvd", GB)
    kvl = core.counter("a1_kvl", 2 * GB)
    bc = core.counter("a1_bc", NQ)
    rla = core.counter("a1_rla", NQ * 3 // 4)
    rlv = core.counter("a1_rlv", NQ // 4)
    gat = core.counter("a1_gat", NQ)
    kp = core.counter("a1_kp", GB * CH)
    gc = core.counter("a1_gc", GB * CH)
    scd = core.counter("a1_scd", GB)
    exd = core.counter("a1_exd", GB)
    awd = core.counter("a1_awd", GB)
    vpd = core.counter("a1_vpd", GB)
    cxd = core.counter("a1_cxd", GB)
    cxt = core.counter("a1_cxt", GB)
    cxc = core.counter("a1_cxc", GB)
    yd = core.counter("a1_yd", GB)
    xd = core.counter("a1_xd", GB)
    chain = core.counter("a1_chain", 20 + GB * (CH + 3 + 3))

    def on_dve(n):
        return n % 4 == 3

    def wait_onehot(eng, g, n):
        if on_dve(n):
            eng.wait_ge(rlv.sem, rlv.at(g, n // 4 + 1))
        else:
            eng.wait_ge(rla.sem, rla.at(g, n + 1 - (n + 1) // 4))

    def load(s):
        s.dma_start(w, d["a1_w"]).then_inc(w_in, 16)
        s.dma_start(vecs, d["a1_vecs"]).then_inc(w_in, 16)
        s.dma_start(sel.bitcast(U16), d["a1_sel"]).then_inc(w_in, 16)
        s.dma_start(mask_i.bitcast(I32), d["a1_maskT"]).then_inc(w_in, 16)

    def pool(p):
        for sem, n in start:
            p.wait_ge(sem, n)
        nc.gpsimd.memset(ones, 1.0).then_inc(set_, 1)
        rv = rows.rearrange("p (c r) -> p c r", r=P)
        nc.gpsimd.memset(rv[:, :, 3 * HR:3 * HR + 2], 1.0).then_inc(set_, 1)
        nc.gpsimd.memset(rv[:, :, 3 * HR + 2:P], 0.0).then_inc(set_, 1)
        nc.gpsimd.memset(cT.rearrange("p (b c) -> p b c", c=CW)[:, :, P:CW], 0.0).then_inc(set_, 1)
        fns["pool"](p)

        def split_kv(g, b):
            p.wait_ge(kvd.sem, kvd.at(g, b + 1))
            k3 = kvs[b % 2].rearrange("p (s n) -> p s n", s=3)
            nc.gpsimd.tensor_tensor(k3[:, 1, :], kvr, ones[:, 0:1].to_broadcast([P, GT]), ALU.mult).then_inc(kvl.sem, 1)
            p.wait_ge(kvl.sem, kvl.at(g, 2 * b + 1))
            nc.gpsimd.tensor_tensor(k3[:, 2, :], kvr, k3[:, 1, :], ALU.subtract).then_inc(kvl.sem, 1)

        def weigh_values(g, b):
            p.wait_ge(awd.sem, awd.at(g, b + 1))
            p.wait_ge(gc.sem, gc.at(g, (b + 1) * CH))
            p.wait_ge(cxd.sem, cxd.at(g, b))
            nc.gpsimd.tensor_tensor(pv.rearrange("p (r e) -> p r e", e=DH),
                                    gv[b % 2].rearrange("p (r e) -> p r e", e=DH),
                                    aw.unsqueeze(2).to_broadcast([P, 2 * R, DH]), ALU.mult).then_inc(vpd.sem, 1)

        with p.Fori(0, G) as g:
            for b in range(GB):
                p.wait_ge(kvp.sem, kvp.at(g, b - GB + 1))
                nc.gpsimd.tensor_copy(cT[:, b * CW:b * CW + P], ctxT[:, ds((g * GB + b) * P, P)]).then_inc(ct.sem, 1)
            split_kv(g, 0)
            for b in range(GB):
                if b > 0:
                    weigh_values(g, b - 1)
                if b + 1 < GB:
                    split_kv(g, b + 1)
            weigh_values(g, GB - 1)

    def pe(t):
        fns["pe"](t)
        t.wait_ge(w_in, 64)
        t.wait_ge(set_, 4)
        t.wait_ge(pre, 1)
        nc.tensor.matmul(bank[7][:, 0:B], ones, om, start=True, stop=True).then_inc(lens, 1)
        t.wait_ge(lens, 2)
        t.wait_ge(*ln_done)

        def project_kv(g, b):
            dst = bank[2] if b == 0 else bank[7]
            t.wait_ge(ct.sem, ct.at(g, b + 1))
            for shift in range(2):
                out = dst[:, shift * 2 * P:(shift + 1) * 2 * P]
                nc.tensor.matmul(out, cT[:, b * CW + shift:b * CW + shift + P], wkv, start=True, stop=False)
                ins = nc.tensor.matmul(out, (core.ones_row, core.const["ones_row_cut"])[shift], core.bias["a1_kv"],
                                       start=False, stop=True)
            ins.then_inc(kvp.sem, 1)

        def places(g, n):
            b, m = divmod(n, QUADS)
            if n < 3:
                t.wait_ge(pc.sem, pc.at(g, 3))
                t.wait_ge(kvd.sem, kvd.at(g, 1))
            else:
                wait_onehot(t, g, n - 3)
            for j in range(4):
                r = m * 4 + j
                ins = nc.tensor.matmul(bank[n % 3][:, j * P:(j + 1) * P], sel[:, r % HR * P:(r % HR + 1) * P],
                                       rT[:, (b * 2 + r // HR) * P:(b * 2 + r // HR + 1) * P], start=True, stop=True)
            ins.then_inc(bc.sem, 1)

        def sample(g, n):
            b, m = divmod(n, QUADS)
            c = m // QC
            if m == 0:
                t.wait_ge(kvl.sem, kvl.at(g, 2 * (b + 1)))
            if m % QC == 0:
                t.wait_ge(gc.sem, gc.at(g, b * CH + c - 1))
            wait_onehot(t, g, n)
            k5 = kvs[b % 2].rearrange("p (s i k e) -> p s i k e", s=3, i=2, k=2)
            for j in range(4):
                r = m * 4 + j
                h = r // NK
                col = (r - c * QC * 4) * 4 * DH
                for s in range(3):
                    ins = nc.tensor.matmul(G2[c % 2][:, col:col + 4 * DH], oh[n % 4][:, j * P:(j + 1) * P],
                                           k5[:, s, :, :, h * DH:(h + 1) * DH], start=s == 0, stop=s == 2)
            ins.then_inc(gat.sem, 1)

        def turn_ctx(g, b):
            t.wait_ge(cxd.sem, cxd.at(g, b + 1))
            if b + 2 < GB:
                t.wait_ge(kvd.sem, kvd.at(g, b + 3))
            t.wait_ge(xd.sem, xd.at(g, b))
            nc.tensor.transpose(bank[7][:, 0:P], cx, core.ident).then_inc(cxt.sem, 1)

        def project_out(g, b):
            t.wait_ge(cxc.sem, cxc.at(g, b + 1))
            nc.tensor.matmul(bank[7][:, P:2 * P], cxT, wo, start=True, stop=False)
            nc.tensor.matmul(bank[7][:, P:2 * P], core.ones_row, core.bias["a1_out"], start=False, stop=True) \
                .then_inc(yd.sem, 1)

        with t.Fori(0, G) as g:
            t.wait_ge(rla.sem, rla.at(g, 0))
            t.wait_ge(rlv.sem, rlv.at(g, 0))
            nc.tensor.matmul(bank[0], wq, xnT[:, ds(g * GT, GT)], start=True, stop=True).then_inc(pj.sem, 1)
            project_kv(g, 0)
            t.wait_ge(pc.sem, pc.at(g, 1))
            for b in range(GB):
                ins = nc.tensor.transpose(bank[1][:, b * P:(b + 1) * P], qpT[:, b * P:(b + 1) * P], core.ident)
            ins.then_inc(pj.sem, 1)
            t.wait_ge(xd.sem, xd.at(g, 0))
            for b in range(GB):
                out = bank[7][:, b * R:(b + 1) * R]
                nc.tensor.matmul(out, qpT[:, b * P:(b + 1) * P], woff, start=True, stop=False)
                ins = nc.tensor.matmul(out, core.ones_row, core.bias["a1_off"], start=False, stop=True)
            ins.then_inc(pj.sem, 1)
            t.wait_ge(idx.sem, idx.at(g, 1))
            for c in range(2 * GB):
                ins = nc.tensor.transpose(bank[0].bitcast(BF16)[:, c * P:(c + 1) * P], rows[:, c * P:(c + 1) * P],
                                          core.ident_b)
            ins.then_inc(pj.sem, 1)
            places(g, 0)
            places(g, 1)
            for s in range(GB + 2):
                if s < GB:
                    for m in range(QUADS):
                        n = s * QUADS + m
                        if n + 2 < NQ:
                            places(g, n + 2)
                        sample(g, n)
                        if m == 2 and s >= 2:
                            project_out(g, s - 2)
                        if m == 7 and s + 1 < GB:
                            t.wait_ge(xd.sem, xd.at(g, max(s - 1, 0)))
                            t.wait_ge(cxc.sem, cxc.at(g, max(s - 1, 0)))
                            t.wait_ge(idx.sem, idx.at(g, 1))
                            project_kv(g, s + 1)
                elif s - 2 >= 0:
                    project_out(g, s - 2)
                if 1 <= s <= GB:
                    turn_ctx(g, s - 1)

    def act(a):
        fns["act"](a)
        a.wait_ge(w_in, 64)

        def high_part(g, b):
            a.wait_ge(kvp.sem, kvp.at(g, b + 1))
            a.wait_ge(gat.sem, gat.at(g, (b - 1) * QUADS))
            nc.scalar.activation(kvs[b % 2][:, 0:GT], bank[2] if b == 0 else bank[7], ACT.Copy).then_inc(kvh.sem, 1)

        def onehot(g, n):
            a.wait_ge(bc.sem, bc.at(g, n + 1))
            a.wait_ge(gat.sem, gat.at(g, n - 3))
            nc.scalar.activation(oh[n % 4], bank[n % 3], ACT.Relu).then_inc(rla.sem, 1)

        def copy_values(g, b, c):
            a.wait_ge(kp.sem, kp.at(g, b * CH + c + 1))
            a.wait_ge(vpd.sem, vpd.at(g, b - 1))
            n = QC * 4 * 2
            nc.scalar.activation(gv[b % 2].rearrange("p (c r e) -> p c r e", c=CH, e=DH)[:, c],
                                 G2[c % 2].rearrange("p (r e) -> p r e", r=n)[:, :, DH:2 * DH], ACT.Copy) \
                .then_inc(gc.sem, 1)

        def exps(g, b):
            a.wait_ge(scd.sem, scd.at(g, b + 1))
            nc.scalar.activation(ee, sc, ACT.Exp, scale=SCALE).then_inc(exd.sem, 1)

        def copy_ctx(g, b):
            a.wait_ge(cxt.sem, cxt.at(g, b + 1))
            a.wait_ge(yd.sem, yd.at(g, b))
            nc.scalar.activation(cxT, bank[7][:, 0:P], ACT.Copy).then_inc(cxc.sem, 1)

        with a.Fori(0, G) as g:
            a.wait_ge(pj.sem, pj.at(g, 1))
            nc.scalar.activation(qpT, bank[0], ACT.Identity, bias=bq).then_inc(pc.sem, 1)
            high_part(g, 0)
            a.wait_ge(pj.sem, pj.at(g, 2))
            a.wait_ge(kp.sem, kp.at(g, 0))
            nc.scalar.activation(qn, bank[1], ACT.Copy).then_inc(pc.sem, 1)
            a.wait_ge(pj.sem, pj.at(g, 4))
            nc.scalar.activation(rT, bank[0].bitcast(BF16), ACT.Copy).then_inc(pc.sem, 1)
            for s in range(GB + 2):
                if s < GB:
                    for m in range(QUADS):
                        n = s * QUADS + m
                        if not on_dve(n):
                            onehot(g, n)
                        if m == 1 and s >= 2:
                            copy_ctx(g, s - 2)
                        if m == 2 and s >= 1:
                            copy_values(g, s - 1, CH - 1)
                        if m == 6 and s >= 1:
                            exps(g, s - 1)
                        if m == 9 and s + 1 < GB:
                            high_part(g, s + 1)
                        if m in (8, 12, 17):
                            copy_values(g, s, (8, 12, 17).index(m))
                else:
                    copy_ctx(g, s - 2)
                    if s == GB:
                        copy_values(g, s - 1, CH - 1)
                        exps(g, s - 1)

    def dve(v):
        fns["dve"](v)
        v.wait_ge(w_in, 64)
        v.wait_ge(set_, 4)
        nc.vector.tensor_scalar(om, mask_i.bitcast(I32), -1.0, 1.0, ALU.mult, ALU.add).then_inc(pre, 1)
        v.wait_ge(lens, 1)
        nc.vector.tensor_scalar(slen, bank[7][:, 0:B], -1.0, None, ALU.add).then_inc(lens, 1)
        v.wait_ge(lens, 2)
        nc.vector.reciprocal(rslen, slen).then_inc(lens, 1)
        v.wait_ge(lens, 3)
        v3 = lambda a: a.rearrange("p (b r) -> p b r", b=GB)

        def find_places(g, c):
            v.wait_ge(pj.sem, pj.at(g, 3))
            sl = slen[:, ds(g * GB, GB)].unsqueeze(2).to_broadcast([P, GB, R])
            rs = rslen[:, ds(g * GB, GB)].unsqueeze(2).to_broadcast([P, GB, R])
            link = c.link
            link(nc.vector.tensor_tensor(v3(t_), v3(bank[7][:, 0:GB * R]),
                                         ref.unsqueeze(1).to_broadcast([P, GB, R]), ALU.add))
            link(nc.vector.tensor_scalar(t_, t_, token, None, ALU.add))
            link(nc.vector.tensor_tensor(v3(n_), v3(t_), rs, ALU.mult))
            link(nc.vector.tensor_scalar(n_, n_, -0.5, MAGIC, ALU.add, ALU.add))
            link(nc.vector.scalar_tensor_tensor(v3(n_), v3(n_), MAGIC, sl, ALU.subtract, ALU.mult))
            link(nc.vector.tensor_tensor(t_, t_, n_, ALU.subtract))
            link(nc.vector.scalar_tensor_tensor(v3(m_), v3(t_), 0.0, sl, ALU.is_lt, ALU.mult))
            link(nc.vector.tensor_tensor(t_, t_, m_, ALU.add))
            link(nc.vector.tensor_tensor(v3(m_), v3(t_), sl, ALU.is_ge))
            link(nc.vector.tensor_tensor(v3(m_), v3(m_), sl, ALU.mult))
            link(nc.vector.tensor_tensor(t_, t_, m_, ALU.subtract))
            link(nc.vector.tensor_scalar(ix, t_, P / (P - 1.0), -0.5, ALU.mult, ALU.add))
            link(nc.vector.tensor_scalar(i0, ix, -0.5, MAGIC, ALU.add, ALU.add))
            link(nc.vector.tensor_scalar(i0, i0, MAGIC, None, ALU.subtract))
            link(nc.vector.tensor_tensor(dx, ix, i0, ALU.subtract))
            rv = rows.rearrange("p (c r) -> p c r", r=P)
            i8 = i0.rearrange("p (c r) -> p c r", r=HR)
            w2 = w01.rearrange("p (r i) -> p r i", i=2)
            nc.vector.tensor_scalar(rv[:, :, 0:HR], i8, 0.0, None, ALU.max)
            nc.vector.scalar_tensor_tensor(w2[:, :, 1], i0, 0.0, dx, ALU.is_ge, ALU.mult)
            nc.vector.tensor_scalar(t_, dx, -2.0, 1.0, ALU.mult, ALU.add)
            link(nc.vector.scalar_tensor_tensor(m_, i0, 0.0, i0, ALU.max, ALU.mult))
            link(nc.vector.tensor_copy(rv[:, :, HR:2 * HR], m_.rearrange("p (c r) -> p c r", r=HR)))
            link(nc.vector.scalar_tensor_tensor(n_, i0, 0.0, t_, ALU.is_ge, ALU.mult))
            link(nc.vector.tensor_tensor(w2[:, :, 0], n_, dx, ALU.add))
            nc.vector.tensor_tensor(rv[:, :, 2 * HR:3 * HR], m_.rearrange("p (c r) -> p c r", r=HR),
                                    rv[:, :, HR:2 * HR], ALU.subtract).then_inc(idx.sem, 1)
            link(nc.vector.tensor_copy(mxs, i0[:, 0:H]))

        def rest_part(g, b):
            v.wait_ge(kvh.sem, kvh.at(g, b + 1))
            v.wait_ge(kvl.sem, kvl.at(g, 2 * b))
            nc.vector.tensor_tensor(kvr, bank[2] if b == 0 else bank[7], kvs[b % 2][:, 0:GT], ALU.subtract) \
                .then_inc(kvd.sem, 1)

        def onehot(g, n):
            v.wait_ge(bc.sem, bc.at(g, n + 1))
            v.wait_ge(gat.sem, gat.at(g, n - 3))
            nc.vector.tensor_scalar(oh[n % 4], bank[n % 3], 0.0, None, ALU.max).then_inc(rlv.sem, 1)

        def key_products(g, b, c, ch):
            v.wait_ge(gat.sem, gat.at(g, b * QUADS + (c + 1) * QC))
            v.wait_ge(pc.sem, pc.at(g, 2))
            g4 = G2[c % 2].rearrange("p (h r e) -> p h r e", h=4, e=2 * DH)[:, :, :, 0:DH]
            q4 = qn[:, b * P + c * 4 * DH:b * P + (c + 1) * 4 * DH].rearrange("p (h e) -> p h e", h=4)
            nc.vector.tensor_tensor(prod.rearrange("p (h r e) -> p h r e", h=4, e=DH), g4,
                                    q4.unsqueeze(2).to_broadcast([P, 4, 2 * NK, DH]), ALU.mult).then_inc(kp.sem, 1)
            v.wait_ge(kp.sem, kp.at(g, b * CH + c + 1))
            ch.link(nc.vector.tensor_reduce(sp_[:, b % 2 * 2 * R + c * 8 * NK:b % 2 * 2 * R + (c + 1) * 8 * NK],
                                            prod.rearrange("p (r e) -> p r e", e=DH), X, ALU.add))

        def scores(g, b, ch):
            ch.link(nc.vector.tensor_tensor(s2, sp_[:, b % 2 * 2 * R:(b % 2 + 1) * 2 * R],
                                            w01[:, b * 2 * R:(b + 1) * 2 * R], ALU.mult))
            ch.link(nc.vector.tensor_reduce(sc, s2.rearrange("p (r i) -> p r i", i=2), X, ALU.add))
            ch.link(nc.vector.tensor_reduce(mxs, sc.rearrange("p (h k) -> p h k", k=NK), X, ALU.max))
            s3 = sc.rearrange("p (h k) -> p h k", k=NK)
            nc.vector.tensor_tensor(s3, s3, mxs.unsqueeze(2).to_broadcast([P, H, NK]), ALU.subtract) \
                .then_inc(scd.sem, 1)

        def weights(g, b, ch):
            v.wait_ge(exd.sem, exd.at(g, b + 1))
            e3 = ee.rearrange("p (h k) -> p h k", k=NK)
            ch.link(nc.vector.tensor_reduce(sm, e3, X, ALU.add))
            ch.link(nc.vector.reciprocal(sm, sm))
            ch.link(nc.vector.tensor_tensor(pw.rearrange("p (h k) -> p h k", k=NK), e3,
                                            sm.unsqueeze(2).to_broadcast([P, H, NK]), ALU.mult))
            nc.vector.scalar_tensor_tensor(aw.rearrange("p (r i) -> p r i", i=2),
                                           w01[:, b * 2 * R:(b + 1) * 2 * R].rearrange("p (r i) -> p r i", i=2), 0.5,
                                           pw.unsqueeze(2).to_broadcast([P, R, 2]), ALU.mult, ALU.mult) \
                .then_inc(awd.sem, 1)

        def sum_values(g, b):
            v.wait_ge(vpd.sem, vpd.at(g, b + 1))
            v.wait_ge(cxt.sem, cxt.at(g, b))
            nc.vector.tensor_reduce(cx.rearrange("p (h e) -> p h e", h=H),
                                    pv.rearrange("p (h r e) -> p h e r", h=H, e=DH), X, ALU.add).then_inc(cxd.sem, 1)

        def update(g, b):
            v.wait_ge(yd.sem, yd.at(g, b + 1))
            xs = x[:, ds((g * GB + b) * P, P)]
            nc.vector.tensor_tensor(xs, xs, bank[7][:, P:2 * P], ALU.add).then_inc(xd.sem, 1)

        with v.Fori(0, G) as g:
            c = Chain(v, chain, g)
            rest_part(g, 0)
            find_places(g, c)
            for s in range(GB + 2):
                b = s
                if s < GB:
                    onehot(g, b * QUADS + 3)
                if 1 <= s <= GB:
                    scores(g, s - 1, c)
                if s < GB:
                    key_products(g, b, 0, c)
                    onehot(g, b * QUADS + 7)
                if s >= 2:
                    update(g, s - 2)
                if 1 <= s <= GB:
                    weights(g, s - 1, c)
                if s < GB:
                    key_products(g, b, 1, c)
                    onehot(g, b * QUADS + 11)
                    if s + 1 < GB:
                        rest_part(g, s + 1)
                    key_products(g, b, 2, c)
                    onehot(g, b * QUADS + 15)
                if 1 <= s <= GB:
                    sum_values(g, s - 1)
                if s < GB:
                    onehot(g, b * QUADS + 19)
                    key_products(g, b, 3, c)
            c.close()

    return dict(load=load, pool=pool, dve=dve, pe=pe, act=act), [(xd.sem, xd.at(G, 0))]


def stage_attention2(core, arena, start):
    nc, d, bank = core.nc, core.dram, core.bank
    x, xnT = core.x, core.xnT
    DH = 64
    TILES = H * DH // P
    QUADS = H // 4
    SCALE = DH ** -0.5
    E1 = DH + 1
    w = arena.take(4 * TILES * P)
    wq, wk, wv, wo = (w[:, i * TILES * P:(i + 1) * TILES * P] for i in range(4))
    lnp = arena.take(4)
    shift = arena.take(B * TILES)
    nat_buf, gain, cnT = arena.take(B * P), arena.take(B * TILES), arena.take(B * P)
    qT, kT = arena.take(TILES * GT), arena.take(TILES * GT)
    cT = arena.take(GT)
    vaug = arena.take(GB * H * E1).rearrange("p (b h e) -> p b h e", b=GB, h=H)
    nm = arena.take(2 * H)
    nm2 = [arena.take(P, BF16) for _ in range(2)]
    nmT = [arena.take(P, BF16) for _ in range(2)]
    pT = [arena.take(GT) for _ in range(2)]
    rsum = arena.take(2 * 4)
    ao, aoT = [arena.take(H * DH) for _ in range(2)], arena.take(H * DH)

    def head(q, i):
        return q // 2 * 8 + 2 * i + q % 2

    def rows_of(buf, h, b):
        part, b = slice(h % 2 * DH, h % 2 * DH + DH), b % GB
        return buf[part, h // 2 * GT + b * P:h // 2 * GT + (b + 1) * P]

    w_in, ctx_in, set_, gain_set = (core.sem(f"a2_{n}") for n in ("w_in", "ctx_in", "set", "gain_set"))
    ln_ctx, ctx_done = layernorm(core, nat_buf, [(ctx_in, 16), (w_in, 48)] + start, dst_t=cnT,
                                 t_scale=lnp[:, 0:1], t_bias=lnp[:, 1:2])
    ln_x, x_done = layernorm(core, x, [ctx_done], dst_natural=nat_buf)
    ln_xx, xx_done = layernorm(core, nat_buf, [x_done], dst_t=xnT, t_scale=lnp[:, 2:3], t_bias=lnp[:, 3:4])
    pj = core.shared_counter("att_pj", 6 * GB, G)
    qd = core.shared_counter("att_qd", 2 * GB, G)
    kvc = core.shared_counter("att_kvc", 4 * GB, G)
    ct = core.shared_counter("att_ct", GB, G)
    nat = core.shared_counter("att_nat", GB * QUADS, G)
    mx = core.shared_counter("att_mx", GB * QUADS, G)
    nms = core.shared_counter("att_nms", GB, G)
    nmt = core.shared_counter("att_nmt", GB, G)
    nmc = core.shared_counter("att_nmc", GB, G)
    st = core.shared_counter("att_st", GB * QUADS, G)
    ex = core.shared_counter("att_ex", GB * QUADS, G)
    av = core.shared_counter("att_av", GB * QUADS, G)
    aon = core.shared_counter("att_aon", GB * QUADS, G)
    aot = core.shared_counter("att_aot", GB * 2, G)
    aoc = core.shared_counter("att_aoc", GB * 2, G)
    yd = core.shared_counter("att_yd", GB, G)
    xd = core.shared_counter("att_xd", GB, G)
    chain = core.shared_counter("att_chain", GB * (1 + QUADS), G)

    def load(s):
        s.dma_start(w, d["a2_w"]).then_inc(w_in, 16)
        s.dma_start(lnp, d["a2_ln"]).then_inc(w_in, 16)
        s.dma_start(shift, d["a2_shift"]).then_inc(w_in, 16)
        s.dma_start(nat_buf, d["ctx"]).then_inc(ctx_in, 16)

    def pool(p):
        for sem, n in start:
            p.wait_ge(sem, n)
        nc.gpsimd.memset(vaug[:, :, :, DH:E1], 1.0).then_inc(set_, 1)
        for t in nm2:
            nc.gpsimd.memset(t, 0.0).then_inc(set_, 1)
        for f in (ln_ctx, ln_x, ln_xx):
            f["pool"](p)
        p.wait_ge(*ctx_done)
        with p.Fori(0, G) as g:
            for b in range(GB):
                p.wait_ge(pj.sem, pj.at(g, 6 * (b - GB + 1)))
                nc.gpsimd.tensor_copy(cT[:, b * P:(b + 1) * P], cnT[:, ds((g * GB + b) * P, P)]).then_inc(ct.sem, 1)

    def dve(v):
        for f in (ln_ctx, ln_x, ln_xx):
            f["dve"](v)
        v.wait_ge(set_, 3)
        nc.vector.tensor_scalar(gain, shift, 1.0, None, ALU.add).then_inc(gain_set, 1)
        v.wait_ge(gain_set, 1)

        def scale_q(g, b, half):
            v.wait_ge(pj.sem, pj.at(g, 6 * b + half + 1))
            for i in range(4):
                t = half * 4 + i
                col = (g * GB + b) * TILES + t
                at = t * GT + b % GB * P
                ins = nc.vector.tensor_scalar(qT[:, at:at + P], bank[6][:, i * P:(i + 1) * P], gain[:, ds(col, 1)],
                                              shift[:, ds(col, 1)], ALU.mult, ALU.add)
            ins.then_inc(qd.sem, 1)

        def row_max(g, b, q):
            n = nm[:, b % 2 * H:b % 2 * H + H]
            v.wait_ge(nat.sem, nat.at(g, b * QUADS + q + 1))
            nc.vector.tensor_reduce(n[:, q * 4:q * 4 + 4], bank[q % 2].rearrange("p (h k) -> p h k", h=4),
                                    X, ALU.max, negate=True).then_inc(mx.sem, 1)

        def split_max(g, b, c):
            n = nm[:, b % 2 * H:b % 2 * H + H]
            v.wait_ge(nmt.sem, nmt.at(g, b - 1))
            v.wait_ge(mx.sem, mx.at(g, (b + 1) * QUADS))
            c.link(nc.vector.tensor_copy(nm2[b % 2][:, 0:H], n))
            nc.vector.tensor_tensor(nm2[b % 2][:, H:2 * H], n, nm2[b % 2][:, 0:H], ALU.subtract) \
                .then_inc(nms.sem, 1)

        def normalise(g, b, q, c):
            n = b * QUADS + q
            v.wait_ge(av.sem, av.at(g, n + 1))
            o = bank[4 + q % 2][:, 0:4 * E1].rearrange("p (h e) -> p h e", h=4)
            r = rsum[:, q % 2 * 4:q % 2 * 4 + 4]
            c.link(nc.vector.reciprocal(r, o[:, :, DH]))
            if q == 0:
                v.wait_ge(aot.sem, aot.at(g, 2 * (b - 1)))
            out = ao[b % 2].rearrange("p (o i s e) -> p o i s e", o=2, i=4, s=2)[:, q // 2, :, q % 2, :]
            nc.vector.tensor_tensor(out, o[:, :, 0:DH], r.unsqueeze(2).to_broadcast([P, 4, DH]), ALU.mult) \
                .then_inc(aon.sem, 1)

        def update(g, b):
            v.wait_ge(yd.sem, yd.at(g, b + 1))
            xs = x[:, ds((g * GB + b) * P, P)]
            nc.vector.tensor_tensor(xs, xs, bank[7][:, 2 * P:3 * P], ALU.add).then_inc(xd.sem, 1)

        def step(g, b, c):
            for q in range(QUADS):
                if more(g, b + 2) and q < 2:
                    scale_q(g, b + 2, q)
                if more(g, b + 1):
                    row_max(g, b + 1, q)
                if more(g, b + 1) and q == 3:
                    split_max(g, b + 1, c)
                if q:
                    normalise(g, b, q - 1, c)
            if b:
                update(g, b - 1)
            normalise(g, b, QUADS - 1, c)

        c = Chain(v, chain, 0)
        for b in range(2):
            for half in range(2):
                scale_q(0, b, half)
        for q in range(QUADS):
            row_max(0, 0, q)
        split_max(0, 0, c)
        step(0, 0, c)
        run_sequences(v, step, chain, c.n)
        update(G - 1, GB - 1)

    def pe(t):
        for f in (ln_ctx, ln_xx):
            f["pe"](t)
        t.wait_ge(*xx_done)

        def natural(g, b, q):
            if q == 0:
                t.wait_ge(kvc.sem, kvc.at(g, 4 * b + 4))
            t.wait_ge(mx.sem, mx.at(g, b * QUADS + q - 1))
            for i in range(4):
                h = head(q, i)
                ins = nc.tensor.matmul(bank[q % 2][:, i * P:(i + 1) * P], rows_of(qT, h, b), rows_of(kT, h, b),
                                       start=True, stop=True)
            ins.then_inc(nat.sem, 1)

        def turn_max(g, b):
            t.wait_ge(nms.sem, nms.at(g, b + 1))
            t.wait_ge(nmc.sem, nmc.at(g, b))
            t.wait_ge(xd.sem, xd.at(g, b - 1))
            nc.tensor.transpose(bank[7][:, 0:P // 2].bitcast(BF16), nm2[b % 2], core.ident_b).then_inc(nmt.sem, 1)

        def project(g, b, k):
            if k == 0:
                t.wait_ge(aoc.sem, aoc.at(g, 2 * (b - 3)))
                t.wait_ge(kvc.sem, kvc.at(g, 4 * b))
            elif k < 3:
                t.wait_ge(qd.sem, qd.at(g, 2 * b + k))
            else:
                t.wait_ge(kvc.sem, kvc.at(g, 4 * b + k - 2))
            if k < 4:
                src, wt = (xnT, wq) if k < 2 else (cnT, wk)
                for i in range(4):
                    tile = k % 2 * 4 + i
                    ins = nc.tensor.matmul(bank[6][:, i * P:(i + 1) * P], wt[:, tile * P:(tile + 1) * P],
                                           src[:, ds((g * GB + b) * P, P)], start=True, stop=True)
            else:
                t.wait_ge(ct.sem, ct.at(g, b + 1))
                ins = nc.tensor.matmul(bank[6], cT[:, b % GB * P:(b % GB + 1) * P], wv[:, k % 2 * GT:(k % 2 + 1) * GT],
                                       start=True, stop=True)
            ins.then_inc(pj.sem, 1)

        def turn_out(g, b, half):
            if half == 0:
                t.wait_ge(aon.sem, aon.at(g, (b + 1) * QUADS))
                t.wait_ge(kvc.sem, kvc.at(g, 4 * (b + 4)) if more(g, b + 3) else kvc.at(G, 0))
            t.wait_ge(aoc.sem, aoc.at(g, 2 * b + half))
            for i in range(4):
                k = half * 4 + i
                ins = nc.tensor.transpose(bank[6][:, i * P:(i + 1) * P], ao[b % 2][:, k * P:(k + 1) * P], core.ident)
            ins.then_inc(aot.sem, 1)

        def project_out(g, b):
            t.wait_ge(aoc.sem, aoc.at(g, 2 * b + 2))
            t.wait_ge(nmc.sem, nmc.at(g, b + 2) if more(g, b + 1) else nmc.at(G, 0))
            t.wait_ge(xd.sem, xd.at(g, b))
            for k in range(TILES):
                ins = nc.tensor.matmul(bank[7][:, 2 * P:3 * P], aoT[:, k * P:(k + 1) * P], wo[:, k * P:(k + 1) * P],
                                       start=k == 0, stop=k == TILES - 1)
            ins.then_inc(yd.sem, 1)

        def av_quad(g, b, q):
            n = b * QUADS + q
            t.wait_ge(ex.sem, ex.at(g, n + 1))
            t.wait_ge(aon.sem, aon.at(g, n - 1))
            for i in range(4):
                ins = nc.tensor.matmul(bank[4 + q % 2][:, i * E1:(i + 1) * E1], pT[q % 2][:, i * P:(i + 1) * P],
                                       vaug[:, b % GB, head(q, i), :], start=True, stop=True)
            ins.then_inc(av.sem, 1)

        def step(g, b):
            t.wait_ge(nmc.sem, nmc.at(g, b + 1))
            for q in range(QUADS):
                n = b * QUADS + q
                t.wait_ge(ex.sem, ex.at(g, n - 1))
                for i in range(4):
                    h = head(q, i)
                    out = bank[2 + q % 2][:, i * P:(i + 1) * P]
                    nc.tensor.matmul(out, rows_of(kT, h, b), rows_of(qT, h, b), start=True, stop=False)
                    k = q * 4 + i
                    ins = nc.tensor.matmul(out, core.sel_head[:, k * P:(k + 1) * P], nmT[b % 2],
                                           start=False, stop=True)
                ins.then_inc(st.sem, 1)
                if more(g, b + 2) and q < 3:
                    project(g, b + 2, 2 * q)
                if b and q == 3:
                    turn_out(g, b - 1, 0)
                if more(g, b + 1):
                    natural(g, b + 1, q)
                if more(g, b + 2) and q < 3:
                    project(g, b + 2, 2 * q + 1)
                if b and q == 3:
                    turn_out(g, b - 1, 1)
                if q:
                    av_quad(g, b, q - 1)
                if b and q == 3:
                    project_out(g, b - 1)
            av_quad(g, b, QUADS - 1)
            if more(g, b + 1):
                turn_max(g, b + 1)

        for b in range(2):
            for k in range(6):
                project(0, b, k)
        for q in range(QUADS):
            natural(0, 0, q)
        turn_max(0, 0)
        step(0, 0)
        run_sequences(t, step)
        turn_out(G - 1, GB - 1, 0)
        turn_out(G - 1, GB - 1, 1)
        project_out(G - 1, GB - 1)

    def act(a):
        for f in (ln_ctx, ln_xx):
            f["act"](a)
        a.wait_ge(set_, 3)

        def copy_max(g, b):
            a.wait_ge(nmt.sem, nmt.at(g, b + 1))
            a.wait_ge(st.sem, st.at(g, (b - 1) * QUADS))
            nc.scalar.activation(nmT[b % 2], bank[7][:, 0:P // 2].bitcast(BF16), ACT.Copy).then_inc(nmc.sem, 1)

        def copy_k(g, b, half):
            a.wait_ge(pj.sem, pj.at(g, 6 * b + half + 3))
            out = kT.rearrange("p (t b k) -> p t b k", b=GB, k=P)[:, half * 4:half * 4 + 4, b % GB, :]
            nc.scalar.activation(out, bank[6].rearrange("p (t k) -> p t k", k=P), ACT.Copy).then_inc(kvc.sem, 1)

        def copy_v(g, b, half):
            a.wait_ge(pj.sem, pj.at(g, 6 * b + half + 5))
            nc.scalar.activation(vaug[:, b % GB, half * H // 2:(half + 1) * H // 2, 0:DH],
                                 bank[6].rearrange("p (h e) -> p h e", e=DH), ACT.Copy).then_inc(kvc.sem, 1)

        def copy_ao(g, b, half):
            a.wait_ge(aot.sem, aot.at(g, 2 * b + half + 1))
            a.wait_ge(yd.sem, yd.at(g, b))
            nc.scalar.activation(aoT[:, half * GT:(half + 1) * GT], bank[6], ACT.Copy).then_inc(aoc.sem, 1)

        def step(g, b):
            for q in range(QUADS):
                n = b * QUADS + q
                a.wait_ge(st.sem, st.at(g, n + 1))
                a.wait_ge(av.sem, av.at(g, n - 1))
                nc.scalar.activation(pT[q % 2], bank[2 + q % 2], ACT.Exp, scale=SCALE).then_inc(ex.sem, 1)
                for half in range(2):
                    if q == 1 and more(g, b + 2):
                        copy_k(g, b + 2, half)
                    if q == 2 and more(g, b + 2):
                        copy_v(g, b + 2, half)
                    if q == 3 and b:
                        copy_ao(g, b - 1, half)
            if more(g, b + 1):
                copy_max(g, b + 1)

        for b in range(2):
            for f in (copy_k, copy_v):
                for half in range(2):
                    f(0, b, half)
        copy_max(0, 0)
        step(0, 0)
        run_sequences(a, step)
        copy_ao(G - 1, GB - 1, 0)
        copy_ao(G - 1, GB - 1, 1)

    return dict(load=load, pool=pool, dve=dve, pe=pe, act=act), [(xd.sem, xd.at(G, 0))]


def stage_attention3(core, arena, start):
    nc, d, bank = core.nc, core.dram, core.bank
    x, xnT, ctxT = core.x, core.xnT, core.ctxT
    C1 = P + 1
    w, bqk = arena.take(2 * P), arena.take(2)
    ctxa = arena.take(B * C1)
    qT, kT, pT = arena.take(GT), arena.take(GT), arena.take(GT)
    nm, rsum = arena.take(GB), arena.take(GB)
    nm2, nmT = arena.take(GB * P, BF16), arena.take(GB * P, BF16)

    fns, ln_done = layernorm(core, x, start, dst_t=xnT)
    w_in, set_ = core.sem("a3_w_in"), core.sem("a3_set")
    pj = core.shared_counter("att_pj", 2, G)
    pc = core.shared_counter("att_pc", 2, G)
    nat = core.shared_counter("att_nat", 1, G)
    nms = core.shared_counter("att_nms", 1, G)
    nmt = core.shared_counter("att_nmt", 1, G)
    nmc = core.shared_counter("att_nmc", 1, G)
    st = core.shared_counter("att_st", 1, G)
    ex = core.shared_counter("att_ex", 1, G)
    av = core.shared_counter("att_av", 2, G)
    xd = core.shared_counter("att_xd", 2, G)
    chain = core.shared_counter("att_chain", 4, G)

    def load(s):
        s.dma_start(w, d["a3_w"]).then_inc(w_in, 16)
        s.dma_start(bqk, d["a3_bqk"]).then_inc(w_in, 16)
        s.dma_start(ctxa.rearrange("p (b e) -> p b e", e=C1)[:, :, 0:P], d["ctx"].rearrange("p (b d) -> p b d", d=P)) \
            .then_inc(w_in, 16)

    def pool(p):
        for sem, n in start:
            p.wait_ge(sem, n)
        nc.gpsimd.memset(ctxa.rearrange("p (b e) -> p b e", e=C1)[:, :, P:C1], 1.0).then_inc(set_, 1)
        nc.gpsimd.memset(nm2, 0.0).then_inc(set_, 1)
        fns["pool"](p)

    def pe(t):
        fns["pe"](t)
        t.wait_ge(w_in, 48)
        t.wait_ge(set_, 2)
        t.wait_ge(*ln_done)
        with t.Fori(0, G) as g:
            t.wait_ge(pc.sem, pc.at(g, 0))
            nc.tensor.matmul(bank[0], w[:, 0:P], xnT[:, ds(g * GT, GT)], start=True, stop=True).then_inc(pj.sem, 1)
            nc.tensor.matmul(bank[1], w[:, P:2 * P], ctxT[:, ds(g * GT, GT)], start=True, stop=True) \
                .then_inc(pj.sem, 1)
            t.wait_ge(pc.sem, pc.at(g, 2))
            t.wait_ge(nms.sem, nms.at(g, 0))
            for b in range(GB):
                cols = slice(b * P, (b + 1) * P)
                ins = nc.tensor.matmul(bank[2][:, cols], qT[:, cols], kT[:, cols], start=True, stop=True)
            ins.then_inc(nat.sem, 1)
            t.wait_ge(nms.sem, nms.at(g, 1))
            for b in range(GB):
                cols = slice(b * P, (b + 1) * P)
                ins = nc.tensor.transpose(bank[3].bitcast(BF16)[:, cols], nm2[:, cols], core.ident_b)
            ins.then_inc(nmt.sem, 1)
            t.wait_ge(nmc.sem, nmc.at(g, 1))
            for b in range(GB):
                cols = slice(b * P, (b + 1) * P)
                nc.tensor.matmul(bank[4][:, cols], kT[:, cols], qT[:, cols], start=True, stop=False)
                ins = nc.tensor.matmul(bank[4][:, cols], core.sel_head[:, 0:P], nmT[:, cols], start=False, stop=True)
            ins.then_inc(st.sem, 1)
            t.wait_ge(ex.sem, ex.at(g, 1))
            for pair in range(2):
                t.wait_ge(xd.sem, xd.at(g, pair - 1))
                for i in range(2):
                    b = pair * 2 + i
                    ins = nc.tensor.matmul(bank[5 + pair][:, i * C1:(i + 1) * C1], pT[:, b * P:(b + 1) * P],
                                           ctxa[:, ds((g * GB + b) * C1, C1)], start=True, stop=True)
                ins.then_inc(av.sem, 1)

    def act(a):
        fns["act"](a)
        a.wait_ge(w_in, 48)
        with a.Fori(0, G) as g:
            a.wait_ge(st.sem, st.at(g, 0))
            for i, dst in enumerate((qT, kT)):
                a.wait_ge(pj.sem, pj.at(g, i + 1))
                nc.scalar.activation(dst, bank[i], ACT.Identity, bias=bqk[:, i:i + 1]).then_inc(pc.sem, 1)
            a.wait_ge(nmt.sem, nmt.at(g, 1))
            nc.scalar.activation(nmT, bank[3].bitcast(BF16)[:, 0:GT], ACT.Copy).then_inc(nmc.sem, 1)
            a.wait_ge(st.sem, st.at(g, 1))
            a.wait_ge(av.sem, av.at(g, 0))
            nc.scalar.activation(pT, bank[4], ACT.Exp).then_inc(ex.sem, 1)

    def dve(v):
        fns["dve"](v)
        v.wait_ge(set_, 2)
        n3 = nm2.rearrange("p (b r) -> p b r", b=GB)
        with v.Fori(0, G) as g:
            c = Chain(v, chain, g)
            v.wait_ge(nat.sem, nat.at(g, 1))
            c.link(nc.vector.tensor_reduce(nm, bank[2].rearrange("p (b k) -> p b k", b=GB), X, ALU.max, negate=True))
            c.link(nc.vector.tensor_copy(n3[:, :, 0], nm))
            nc.vector.tensor_tensor(n3[:, :, H], nm, n3[:, :, 0], ALU.subtract).then_inc(nms.sem, 1)
            for pair in range(2):
                v.wait_ge(av.sem, av.at(g, pair + 1))
                o = bank[5 + pair][:, 0:2 * C1].rearrange("p (b e) -> p b e", b=2)
                c.link(nc.vector.reciprocal(rsum[:, pair * 2:pair * 2 + 2], o[:, :, P]))
                for i in range(2):
                    b = pair * 2 + i
                    xs = x[:, ds((g * GB + b) * P, P)]
                    ins = nc.vector.scalar_tensor_tensor(xs, o[:, i, 0:P], rsum[:, b:b + 1], xs, ALU.mult, ALU.add)
                ins.then_inc(xd.sem, 1)
            c.close()

    return dict(load=load, pool=pool, dve=dve, pe=pe, act=act), [(xd.sem, xd.at(G, 0))]


class Router:

    def __init__(self, core, arena, tag, experts, links, steps):
        self.core, self.e, self.steps = core, experts, steps
        n = GB * experts
        self.scratch = arena.take(7 * n)
        self.logit, self.gt, self.eq, self.cum, self.comb, self.val, self.tmp = (
            self.scratch[:, i * n:(i + 1) * n] for i in range(7))
        self.top = arena.take(GB * 8 * 8)
        self.small = arena.take(GB * 8 * 4)
        self.reset = arena.take(n)
        self.pad = arena.take(1)
        self.mask = self.val
        self.asked = core.counter(f"{tag}_asked", steps)
        self.answered = core.counter(f"{tag}_answered", steps)
        self.chain = core.counter(f"{tag}_chain", links)

    def hold(self):
        self.core.nc.vector.memset(self.pad, 0.0)

    def largest(self, c, sel, values, threshold, k, e):
        nc = self.core.nc
        v3 = lambda a: a[:, 0:GB * e].rearrange("p (b e) -> p b e", e=e)
        thr = threshold.unsqueeze(2).to_broadcast([P, GB, e])
        left = self.small[:, 0:GB]
        nc.vector.tensor_tensor(v3(self.eq), values, thr, ALU.is_equal)
        c.link(nc.vector.tensor_tensor(v3(self.gt), values, thr, ALU.is_gt))
        nc.vector.tensor_tensor_scan(self.cum[:, 0:GB * e], self.reset8 if e == 8 else self.reset,
                                     self.eq[:, 0:GB * e], 0.0, ALU.mult, ALU.add)
        c.link(nc.vector.tensor_reduce(left, v3(self.gt), X, ALU.add))
        c.link(nc.vector.tensor_scalar(left, left, -1.0, float(k), ALU.mult, ALU.add))
        c.link(nc.vector.tensor_tensor(v3(self.cum), v3(self.cum), left.unsqueeze(2).to_broadcast([P, GB, e]),
                                       ALU.is_le))
        c.link(nc.vector.tensor_tensor(self.cum[:, 0:GB * e], self.cum[:, 0:GB * e], self.eq[:, 0:GB * e], ALU.mult))
        c.link(nc.vector.tensor_tensor(sel, v3(self.cum), v3(self.gt), ALU.add))


class Top2Softmax(Router):

    def __init__(self, core, arena, tag):
        super().__init__(core, arena, tag, 8, 13, 1)
        self.reset8 = self.reset

    def dve(self, v, g, psum):
        nc, c = self.core.nc, Chain(v, self.chain, g)
        v3 = lambda a: a.rearrange("p (b e) -> p b e", e=8)
        top, w = v3(self.top[:, 0:GB * 8]), self.small[:, GB:3 * GB]
        c.link(nc.vector.tensor_copy(self.logit, psum))
        self.hold()
        for b in range(GB):
            ins = nc.vector.max(top[:, b, :], v3(self.logit)[:, b, :])
        c.link(ins)
        nc.vector.tensor_tensor(self.small[:, 3 * GB:4 * GB], top[:, :, 0], top[:, :, 1], ALU.subtract) \
            .then_inc(self.asked.sem, 1)
        self.largest(c, v3(self.val), v3(self.logit), top[:, :, 1], 2, 8)
        v.wait_ge(self.answered.sem, self.answered.at(g, 1))
        w1, w2 = w[:, 0:GB], w[:, GB:2 * GB]
        bc = lambda a: a.unsqueeze(2).to_broadcast([P, GB, 8])
        c.link(nc.vector.tensor_tensor(w1, w1, w2, ALU.subtract))
        c.link(nc.vector.tensor_tensor(v3(self.tmp), v3(self.logit), bc(top[:, :, 0]), ALU.is_equal))
        c.link(nc.vector.tensor_tensor(v3(self.tmp), v3(self.tmp), bc(w1), ALU.mult))
        c.link(nc.vector.tensor_tensor(v3(self.tmp), v3(self.tmp), bc(w2), ALU.add))
        c.link(nc.vector.tensor_tensor(self.comb, self.tmp, self.val, ALU.mult))
        c.close()

    def act(self, a, g):
        nc, w = self.core.nc, self.small[:, GB:3 * GB]
        dm = self.small[:, 3 * GB:4 * GB]
        a.wait_ge(self.asked.sem, self.asked.at(g, 1))
        nc.scalar.activation(w[:, 0:GB], dm, ACT.Sigmoid)
        nc.scalar.activation(w[:, GB:2 * GB], dm, ACT.Sigmoid, scale=-1.0).then_inc(self.answered.sem, 1)


class Top1Softmax(Router):

    def __init__(self, core, arena, tag):
        super().__init__(core, arena, tag, 8, 12, 1)
        self.reset8 = self.reset

    def dve(self, v, g, psum):
        nc, c = self.core.nc, Chain(v, self.chain, g)
        v3 = lambda a: a.rearrange("p (b e) -> p b e", e=8)
        top, total = v3(self.top[:, 0:GB * 8]), self.small[:, GB:2 * GB]
        bc = lambda a: a.unsqueeze(2).to_broadcast([P, GB, 8])
        c.link(nc.vector.tensor_copy(self.logit, psum))
        self.hold()
        for b in range(GB):
            ins = nc.vector.max(top[:, b, :], v3(self.logit)[:, b, :])
        c.link(ins)
        nc.vector.tensor_tensor(v3(self.tmp), v3(self.logit), bc(top[:, :, 0]), ALU.subtract) \
            .then_inc(self.asked.sem, 1)
        self.largest(c, v3(self.val), v3(self.logit), top[:, :, 0], 1, 8)
        v.wait_ge(self.answered.sem, self.answered.at(g, 1))
        c.link(nc.vector.tensor_reduce(total, v3(self.tmp), X, ALU.add))
        c.link(nc.vector.reciprocal(total, total))
        c.link(nc.vector.tensor_tensor(v3(self.comb), v3(self.val), bc(total), ALU.mult))
        c.link(nc.vector.tensor_copy(total, total))
        c.close()

    def act(self, a, g):
        a.wait_ge(self.asked.sem, self.asked.at(g, 1))
        self.core.nc.scalar.activation(self.tmp, self.tmp, ACT.Exp).then_inc(self.answered.sem, 1)


class GroupedTop8(Router):

    def __init__(self, core, arena, tag):
        super().__init__(core, arena, tag, 64, 24, 1)
        self.bias, self.reset8 = arena.take(64), arena.take(GB * 8)
        self.groups = arena.take(GB * 8 * 2)
        self.mask = self.eq

    def dve(self, v, g, psum):
        nc, c = self.core.nc, Chain(v, self.chain, g)
        score, choice, masked, sel = self.logit, self.val, self.tmp, self.comb
        v3 = lambda a: a.rearrange("p (b e) -> p b e", e=64)
        v8 = lambda a: a.rearrange("p (g e) -> p g e", e=8)
        b8 = lambda a: a.rearrange("p (b g) -> p b g", g=8)
        v.wait_ge(self.answered.sem, self.answered.at(g, 1))
        c.link(nc.vector.tensor_tensor(v3(choice), v3(score), self.bias.unsqueeze(1).to_broadcast([P, GB, 64]),
                                       ALU.add))
        top, gs, gsel = v8(self.top), self.groups[:, 0:GB * 8], self.groups[:, GB * 8:]
        self.hold()
        for i in range(GB * 8):
            ins = nc.vector.max(top[:, i, :], v8(choice)[:, i, :])
        c.link(ins)
        c.link(nc.vector.tensor_tensor(gs, top[:, :, 0], top[:, :, 1], ALU.add))
        self.hold()
        for b in range(GB):
            ins = nc.vector.max(top[:, b, :], b8(gs)[:, b, :])
        c.link(ins)
        self.largest(c, b8(gsel), b8(gs), top[:, 0:GB, 3], 4, 8)
        c.link(nc.vector.tensor_tensor(v8(masked), v8(choice), gsel.unsqueeze(2).to_broadcast([P, GB * 8, 8]),
                                       ALU.mult))
        self.hold()
        for b in range(GB):
            ins = nc.vector.max(top[:, b, :], v3(masked)[:, b, :])
        c.link(ins)
        self.largest(c, v3(self.mask), v3(masked), top[:, 0:GB, 7], 8, 64)
        c.link(nc.vector.tensor_tensor(sel, self.mask, score, ALU.mult))
        total = self.small[:, GB:2 * GB]
        c.link(nc.vector.tensor_reduce(total, v3(sel), X, ALU.add))
        c.link(nc.vector.tensor_scalar(total, total, 1e-20, None, ALU.add))
        c.link(nc.vector.reciprocal(total, total))
        c.link(nc.vector.tensor_scalar(total, total, 2.5, None, ALU.mult))
        c.link(nc.vector.tensor_tensor(v3(sel), v3(sel), total.unsqueeze(2).to_broadcast([P, GB, 64]), ALU.mult))
        c.close()

    def act(self, a, g, psum, ready, free):
        nc = self.core.nc
        a.wait_ge(*ready)
        a.wait_ge(*free)
        nc.scalar.activation(self.logit, psum, ACT.Sigmoid).then_inc(self.answered.sem, 1)


def stage_experts(tag, make_router, experts, top_k, shared, width, rows, quads, router_bias=None):
    TILES = -(-(B * P * top_k + experts * (P - 1)) // P)
    TILES = -(-TILES // (4 * quads)) * 4 * quads
    tiles = width // rows
    PER = 4 // tiles
    S = 4 // PER
    UNITS = S * quads
    COLS = -(-TILES // P)
    AHEAD = 2 if S == 1 else 1

    def stage(core, arena, start):
        nc, d, bank = core.nc, core.dram, core.bank
        x, xnT = core.x, core.xnT
        E = experts + shared
        N = GB * experts
        gate_w = arena.take(experts)
        tile_id = arena.take(3)
        router = make_router(core, arena, tag)
        own_scores = isinstance(router, GroupedTop8)
        up = arena.take(E * 2 * width)
        down = arena.take(E * tiles * P)
        natural = arena.take(B * P)
        gates, key = arena.take(B * experts), arena.take(B * experts)
        chosen_w = arena.take(max(B * experts // 2, 3 * B * 8))
        chosen = chosen_w[:, 0:B * experts // 2].bitcast(BF16)
        best = chosen_w[:, 0:B * 8]
        place = chosen_w[:, B * 8:B * 8 + B * top_k].bitcast(U32)
        weight = chosen_w[:, 2 * B * 8:2 * B * 8 + B * top_k]
        n_bufs = 3 + 2 * tiles if shared else 4
        scratch = arena.take(n_bufs * GT)
        bufs = [scratch[:, i * GT:(i + 1) * GT] for i in range(n_bufs)]
        xT, sg, h = bufs[0], bufs[1:3], bufs[3:]
        index = [arena.take(2 * top_k).bitcast(U32) for _ in range(2)]
        total, first, n_tiles, ends, base = (arena.take(experts) for _ in range(5))
        owner = arena.take(COLS)
        table = arena.take(COLS * P)[0:1].bitcast(I32)
        U = shared * tiles
        sorted_x = core.sorted_x
        sorted_y = nc.dram_tensor(f"{tag}_sorted_y", (TILES * P, P), F32, kind="Internal").ap()
        x_tiles = sorted_x.rearrange("(t p) d -> p t d", p=P)
        y_tiles = sorted_y.rearrange("(t p) d -> p t d", p=P)

        fns, ln_done = layernorm(core, x, start, dst_t=xnT, keep=natural)
        LOOPS = TILES // (4 * quads)
        CHUNK = min(512, B * experts)
        CHUNKS = B * experts // CHUNK
        K2 = 2 * top_k
        over = core.shared_counter
        w_in, experts_in = core.sem(f"{tag}_w_in"), core.sem(f"{tag}_experts_in")
        ct = over("ct", GB, G)
        lg = over("lg", 1, G)
        rt = over("rt", 1, G)
        if shared:
            ud = over("ud", 2 * U, G)
            sd = over("sd", U, G)
            hd = over("hd", U, G)
            yd = over("yd", shared, G)
            xd = over("xd", shared, G)
        routed = over("routed", 1, 1, 0)
        counted = over("counted", 2 * CHUNKS, 1, 0)
        steps = over("steps", 17 + 2 * COLS + 3 * top_k, 1, 0)
        owned = over("owned", 1, 1, 0)
        owner_row = over("owner_row", 1, 1, 0)
        tabled = over("tabled", 1, 1, 0)
        placed = over("placed", 1, 1, 0)
        weighed = over("weighed", 1, 1, 0)
        xl = [over(f"xl{i}", 32, G) for i in range(2)]
        sc = [over(f"sc{i}", K2 * 16, G, 0) for i in range(2)]
        ring = min(quads, 4)
        ld = [over(f"ld{i}", 16 * quads // ring, LOOPS) for i in range(ring)]
        xt = over("xt", quads, LOOPS)
        xc = over("xc", quads, LOOPS)
        gu = over("gu", UNITS, LOOPS)
        si = over("si", UNITS, LOOPS)
        hn = over("hn", UNITS, LOOPS)
        ht = over("ht", UNITS, LOOPS)
        hc = over("hc", UNITS, LOOPS)
        dn = over("dn", UNITS, LOOPS)
        yc = over("yc", quads, LOOPS)
        stored = [over(f"y_stored{i}", 8 * quads, LOOPS) for i in range(2)]
        il = [over(f"il{i}", 16, G) for i in range(2)]
        ga = [over(f"ga{i}", K2 * 16, G, 0) for i in range(2)]
        mixed = over("mixed", 2, G)
        mixing = over("mixing", K2, G)

        xs, xTs, sgs, hs = ([xnT[:, (2 * i + j) * GT:(2 * i + j + 1) * GT] for j in range(2)] for i in range(4))
        hTs, ys = bufs[0:2], bufs[2:4]
        if ring == 4:
            xs += [bufs[4], core.ln_xn[:, :]]
        staged = [core.ln_xn[:, 0:2 * P], core.ln_xn[:, 2 * P:4 * P]]
        gathered = [natural[:, i * K2 * P:(i + 1) * K2 * P] for i in range(2)]
        before = scratch[:, 0:B * experts]
        count = router.scratch[:, 0:B * experts // 2].bitcast(BF16)
        taken = before

        def run(eng, step):
            step(0, 0, first=True)
            with eng.Fori(0, LOOPS - 1) as g:
                for u in range(1, UNITS + 1):
                    step(g, u)
            for u in range(1, UNITS):
                step(LOOPS - 1, u, last=True)

        def load(s):
            s.dma_start(gate_w, d[f"{tag}_gate"]).then_inc(w_in, 16)
            s.dma_start(router.reset, d["reset"][:, 0:GB * 8] if experts == 8 else d["reset64"]).then_inc(w_in, 16)
            s.dma_start(tile_id, d["tile_id"]).then_inc(w_in, 16)
            if own_scores:
                s.dma_start(router.bias, d[f"{tag}_bias"]).then_inc(w_in, 16)
                s.dma_start(router.reset8, d["reset"][:, 0:GB * 8]).then_inc(w_in, 16)

        def sp(s):
            def places_to(g, i, sig):
                s.dma_start(index[i], place[:, ds((2 * g + i) * K2, K2)]).then_inc(sig[i].sem, 16)

            def stage_rows(g, i):
                places_to(g, i, xl)
                s.dma_start(staged[i], natural[:, ds((2 * g + i) * 2 * P, 2 * P)]).then_inc(xl[i].sem, 16)

            s.dma_start(up, d[f"{tag}_up"]).then_inc(experts_in, 16)
            s.dma_start(down[0:rows], d[f"{tag}_down"]).then_inc(experts_in, 16)
            s.wait_ge(placed.sem, placed.at(0, 1))
            for i in range(2):
                stage_rows(0, i)
            with s.Fori(0, G - 1) as g:
                for i in range(2):
                    s.wait_ge(sc[i].sem, sc[i].at(g, K2 * 16))
                    stage_rows(g + 1, i)
            for i in range(2):
                s.wait_ge(sc[i].sem, sc[i].at(G - 1, K2 * 16))
            s.wait_ge(weighed.sem, weighed.at(0, 1))
            with s.Fori(0, LOOPS) as g:
                for q in range(quads):
                    s.wait_ge(xt.sem, xt.at(g, q - ring + 1))
                    s.dma_start(xs[q % ring].rearrange("p (t d) -> p t d", d=P),
                                x_tiles[:, ds((g * quads + q) * 4, 4), :]).then_inc(ld[q % ring].sem, 16)
            for i in range(2):
                places_to(0, i, il)
            with s.Fori(0, G - 1) as g:
                for i in range(2):
                    s.wait_ge(ga[i].sem, ga[i].at(g, K2 * 16))
                    places_to(g + 1, i, il)

        loads = 16 * (5 if own_scores else 3)
        logits = bank[6][:, 0:N]

        def pool(p):
            fns["pool"](p)
            p.wait_ge(*ln_done)
            with p.Fori(0, G) as g:
                for b in range(GB):
                    p.wait_ge(lg.sem, lg.at(g, 0))
                    nc.gpsimd.tensor_copy(xT[:, b * P:(b + 1) * P], xnT[:, ds((g * GB + b) * P, P)]) \
                        .then_inc(ct.sem, 1)

            def hold():
                p.sem_inc(core.held, 1)

            p.wait_ge(placed.sem, placed.at(0, 1))
            with p.Fori(0, G) as g:
                for i in range(2):
                    p.wait_ge(xl[i].sem, xl[i].at(g, 32))
                    hold()
                    for b in range(2):
                        for k in range(top_k):
                            at = index[i][:, b * top_k + k:b * top_k + k + 1]
                            nc.gpsimd.indirect_dma_start(
                                out=sorted_x, out_offset=bass.IndirectOffsetOnAxis(ap=at, axis=0),
                                in_=staged[i][:, b * P:(b + 1) * P], in_offset=None).then_inc(sc[i].sem, 16)
            for i in range(2):
                p.wait_ge(stored[i].sem, stored[i].at(LOOPS, 0))
            with p.Fori(0, G) as g:
                for i in range(2):
                    p.wait_ge(mixed.sem, mixed.at(g, i - 1))
                    p.wait_ge(il[i].sem, il[i].at(g, 16))
                    hold()
                    for k in range(K2):
                        at = index[i][:, k:k + 1]
                        nc.gpsimd.indirect_dma_start(
                            out=gathered[i][:, k * P:(k + 1) * P], out_offset=None, in_=sorted_y,
                            in_offset=bass.IndirectOffsetOnAxis(ap=at, axis=0)).then_inc(ga[i].sem, 16)

        def pe(t):
            fns["pe"](t)
            t.wait_ge(w_in, loads)
            t.wait_ge(*ln_done)

            def shared_part(g, u):
                for k in range(2):
                    if k == 0:
                        t.wait_ge(hd.sem, hd.at(g, u - 1))
                    col = ((experts + u // tiles) * 2 * tiles + k * tiles + u % tiles) * rows
                    nc.tensor.matmul(bank[u % 2 * 2 + k][0:rows, :], up[:, col:col + rows],
                                     xnT[:, ds(g * GT, GT)], start=True, stop=True).then_inc(ud.sem, 1)

            def shared_output(g, e):
                t.wait_ge(hd.sem, hd.at(g, (e + 1) * tiles))
                t.wait_ge(xd.sem, xd.at(g, e - 1))
                for b in range(GB):
                    for k in range(tiles):
                        hk = h[e % 2 * tiles + k]
                        part = (experts + e) * tiles + k
                        ins = nc.tensor.matmul(bank[4 + e % 2][:, b * P:(b + 1) * P], hk[0:rows, b * P:(b + 1) * P],
                                               down[0:rows, part * P:(part + 1) * P],
                                               start=k == 0, stop=k == tiles - 1)
                ins.then_inc(yd.sem, 1)

            with t.Fori(0, G) as g:
                t.wait_ge(rt.sem, rt.at(g, 0))
                for b in range(GB):
                    t.wait_ge(ct.sem, ct.at(g, b + 1))
                    out = logits[:, b * experts:(b + 1) * experts]
                    ins = nc.tensor.matmul(out, xT[:, b * P:(b + 1) * P], gate_w, start=True, stop=router_bias is None)
                    if router_bias:
                        ins = nc.tensor.matmul(out, core.ones_row, core.bias[router_bias], start=False, stop=True)
                ins.then_inc(lg.sem, 1)
            t.wait_ge(experts_in, 32)
            t.wait_ge(routed.sem, routed.at(0, 1))
            for c in range(CHUNKS):
                rhs = chosen[:, c * CHUNK:(c + 1) * CHUNK]
                nc.tensor.matmul(bank[c][:, 0:CHUNK], core.earlier_b, rhs, start=True, stop=True).then_inc(counted.sem, 1)
                nc.tensor.matmul(bank[4 + c][:, 0:CHUNK], core.ones_b, rhs, start=True, stop=True).then_inc(counted.sem, 1)
            t.wait_ge(owned.sem, owned.at(0, 1))
            for c in range(COLS):
                ins = nc.tensor.matmul(bank[7][0:1, c * P:(c + 1) * P], owner[:, c:c + 1], core.ident,
                                       start=True, stop=True)
            ins.then_inc(owner_row.sem, 1)
            t.wait_ge(tabled.sem, tabled.at(0, 1))
            if shared:
                with t.Fori(0, G) as g:
                    shared_part(g, 0)
                    for u in range(U):
                        if u + 1 < U:
                            shared_part(g, u + 1)
                        if u % tiles == tiles - 1:
                            shared_output(g, u // tiles)

            def turn_x(g, q):
                t.wait_ge(ld[q % ring].sem, ld[q % ring].at(g, 16 * (q // ring + 1)))
                t.wait_ge(xc.sem, xc.at(g, q))
                for i in range(4):
                    ins = nc.tensor.transpose(bank[0][:, i * P:(i + 1) * P], xs[q % ring][:, i * P:(i + 1) * P],
                                              core.ident)
                ins.then_inc(xt.sem, 1)

            def expert(g, q, i):
                return nc.values_load(table[0:1, ds((g * quads + q) * 4 + i, 1)], engines=[mybir.EngineType.PE],
                                    min_val=0, max_val=experts - 1,
                                    skip_runtime_bounds_check_because="the table is clamped to the experts")

            owners_of = {}

            def up_products(g, u):
                q, s = divmod(u, S)
                owners = owners_of[id(g), u] = [expert(g, q, s * PER + i) for i in range(PER)]
                t.wait_ge(xc.sem, xc.at(g, q + 1))
                t.wait_ge(hn.sem, hn.at(g, u - 1))
                for i, e in enumerate(owners):
                    lhs = xTs[q % 2][:, (s * PER + i) * P:(s * PER + i + 1) * P]
                    if 2 * width > 512:
                        for k in range(2):
                            ins = nc.tensor.matmul(bank[2 + u % 2 * 2 + k][:, 0:width], lhs,
                                                   up[:, ds(e * (2 * width) + k * width, width)],
                                                   start=True, stop=True)
                    else:
                        n = PER // 2
                        out = bank[2 + u % 2 * 2 + i // n][:, i % n * 2 * width:(i % n + 1) * 2 * width]
                        ins = nc.tensor.matmul(out, lhs, up[:, ds(e * (2 * width), 2 * width)], start=True, stop=True)
                ins.then_inc(gu.sem, 1)

            def turn_hidden(g, u):
                t.wait_ge(hn.sem, hn.at(g, u + 1))
                t.wait_ge(hc.sem, hc.at(g, u - 1))
                for j in range(4):
                    ins = nc.tensor.transpose(bank[6 + u % 2][0:rows, j * P:(j + 1) * P],
                                              hs[u % 2][:, j * rows:(j + 1) * rows], core.ident)
                ins.then_inc(ht.sem, 1)

            def down_products(g, u):
                q, s = divmod(u, S)
                owners = owners_of.pop((id(g), u), None) or [expert(g, q, s * PER + i) for i in range(PER)]
                if s == 0:
                    t.wait_ge(yc.sem, yc.at(g, q))
                t.wait_ge(hc.sem, hc.at(g, u + 1))
                for i, e in enumerate(owners):
                    for k in range(tiles):
                        j = i * tiles + k
                        ins = nc.tensor.matmul(bank[1][:, (s * PER + i) * P:(s * PER + i + 1) * P],
                                               hTs[u % 2][0:rows, j * P:(j + 1) * P],
                                               down[0:rows, ds(e * (tiles * P) + k * P, P)],
                                               start=k == 0, stop=k == tiles - 1)
                ins.then_inc(dn.sem, 1)

            def step(g, u, first=False, last=False):
                if not (last and u == UNITS - 1):
                    up_products(g, u + 1)
                if u % S == 0 and not (last and u // S + AHEAD >= quads):
                    turn_x(g, u // S + AHEAD)
                turn_hidden(g, u)
                if not first:
                    down_products(g, u - 1)

            for q in range(AHEAD):
                turn_x(0, q)
            up_products(0, 0)
            run(t, step)
            down_products(LOOPS - 1, UNITS - 1)

        def act(a):
            fns["act"](a)
            with a.Fori(0, G) as g:
                if own_scores:
                    router.act(a, g, logits, (lg.sem, lg.at(g, 1)), (rt.sem, rt.at(g, 0)))
                else:
                    router.act(a, g)
            if shared:
                with a.Fori(0, G) as g:
                    for u in range(U):
                        a.wait_ge(ud.sem, ud.at(g, 2 * u + 1))
                        a.wait_ge(hd.sem, hd.at(g, u - 1))
                        nc.scalar.activation(sg[u % 2][0:rows], bank[u % 2 * 2][0:rows, :], ACT.Silu) \
                            .then_inc(sd.sem, 1)

            def copy_x(g, q):
                a.wait_ge(xt.sem, xt.at(g, q + 1))
                a.wait_ge(gu.sem, gu.at(g, (q - 1) * S))
                nc.scalar.activation(xTs[q % 2], bank[0], ACT.Copy).then_inc(xc.sem, 1)

            def silu(g, u):
                a.wait_ge(gu.sem, gu.at(g, u + 1))
                a.wait_ge(hn.sem, hn.at(g, u - 1))
                gate, _, out = unit_views(u, sgs[u % 2])
                nc.scalar.activation(out, gate, ACT.Silu).then_inc(si.sem, 1)

            def copy_y(g, q):
                a.wait_ge(dn.sem, dn.at(g, (q + 1) * S))
                a.wait_ge(stored[q % 2].sem, stored[q % 2].at(g, 16 * (q // 2)))
                nc.scalar.activation(ys[q % 2], bank[1], ACT.Copy).then_inc(yc.sem, 1)
                a.wait_ge(yc.sem, yc.at(g, q + 1))
                a.dma_start(y_tiles[:, ds((g * quads + q) * 4, 4), :],
                            ys[q % 2].rearrange("p (t d) -> p t d", d=P)).then_inc(stored[q % 2].sem, 16)

            def step(g, u, first=False, last=False):
                if not (last and u == UNITS - 1):
                    silu(g, u + 1)
                if u % S == 0 and not (last and u // S + AHEAD >= quads):
                    copy_x(g, u // S + AHEAD)
                if not first and u % S == 0:
                    copy_y(g, u // S - 1)

            for q in range(AHEAD):
                copy_x(0, q)
            silu(0, 0)
            run(a, step)
            copy_y(LOOPS - 1, quads - 1)

        def unit_views(u, out):
            if 2 * width > 512:
                return bank[2 + u % 2 * 2], bank[3 + u % 2 * 2], out
            n = PER // 2
            both = core.psum[:, (2 + u % 2 * 2) * 512:(4 + u % 2 * 2) * 512].rearrange("p (k w) -> p k w", k=2)
            both = both[:, :, 0:n * 2 * width].rearrange("p k (n f) -> p k n f", n=n)
            out = out[:, 0:PER * width].rearrange("p (k n f) -> p k n f", k=2, n=n)
            if n == 1:
                both, out = both[:, :, 0, :], out[:, :, 0, :]
                return both[:, :, 0:width], both[:, :, width:], out
            return both[:, :, :, 0:width], both[:, :, :, width:], out

        def dve(v):
            fns["dve"](v)
            v.wait_ge(w_in, loads)

            def shared_hidden(g, u):
                e, k = divmod(u, tiles)
                v.wait_ge(ud.sem, ud.at(g, 2 * u + 2))
                v.wait_ge(sd.sem, sd.at(g, u + 1))
                v.wait_ge(yd.sem, yd.at(g, e - 1))
                nc.vector.tensor_tensor(h[e % 2 * tiles + k][0:rows], sg[u % 2][0:rows],
                                        bank[u % 2 * 2 + 1][0:rows, :], ALU.mult).then_inc(hd.sem, 1)

            def add_shared(g, e):
                v.wait_ge(yd.sem, yd.at(g, e + 1))
                v.wait_ge(xd.sem, xd.at(g, e))
                xs_ = x[:, ds(g * GT, GT)]
                nc.vector.tensor_tensor(xs_, xs_, bank[4 + e % 2], ALU.add).then_inc(xd.sem, 1)

            with v.Fori(0, G) as g:
                v.wait_ge(lg.sem, lg.at(g, 1))
                router.dve(v, g, logits)
                nc.vector.tensor_copy(gates[:, ds(g * N, N)], router.comb)
                nc.vector.tensor_copy(chosen[:, ds(g * N, N)], router.mask).then_inc(rt.sem, 1)
                v.wait_ge(rt.sem, rt.at(g, 1))
            nc.vector.memset(router.pad, 0.0).then_inc(routed.sem, 1)
            v.wait_ge(routed.sem, routed.at(0, 1))

            BC = CHUNK // experts
            order = Steps(v, steps)
            link = order.link
            eb = lambda a_: a_.rearrange("p (e b) -> p e b", b=B)
            v.wait_ge(counted.sem, counted.at(0, 2 * CHUNKS))
            for c in range(CHUNKS):
                ins = nc.vector.tensor_copy(
                    count.rearrange("p (e b) -> p b e", b=B)[:, c * BC:(c + 1) * BC, :],
                    bank[4 + c][:, 0:CHUNK].rearrange("p (b e) -> p b e", e=experts))
            link(ins)
            link(nc.vector.tensor_tensor_scan(before, count, count, 0.0, ALU.add, ALU.max))
            link(nc.vector.tensor_copy(total, eb(before)[:, :, B - 1]))
            link(nc.vector.tensor_tensor(before, before, count, ALU.subtract))
            link(nc.vector.tensor_copy(first, eb(before)[:, :, 0]))
            link(nc.vector.tensor_tensor(total, total, first, ALU.subtract))
            link(nc.vector.tensor_scalar(n_tiles, total, 1.0 / P, 0.5 - 0.5 / P, ALU.mult, ALU.add))
            link(nc.vector.tensor_scalar(n_tiles, n_tiles, MAGIC, None, ALU.add))
            link(nc.vector.tensor_scalar(n_tiles, n_tiles, MAGIC, None, ALU.subtract))
            link(nc.vector.tensor_tensor_scan(ends, n_tiles, n_tiles, 0.0, ALU.add, ALU.max))
            link(nc.vector.tensor_tensor(base, ends, n_tiles, ALU.subtract))
            link(nc.vector.tensor_scalar(base, base, float(P), 1.0, ALU.mult, ALU.add))
            link(nc.vector.tensor_tensor(base, base, first, ALU.subtract))
            link(nc.vector.tensor_tensor(eb(before), eb(before), base.unsqueeze(2).to_broadcast([P, experts, B]),
                                         ALU.add))
            for c in range(CHUNKS):
                ins = nc.vector.tensor_tensor(
                    key[:, c * CHUNK:(c + 1) * CHUNK].rearrange("p (b e) -> p b e", e=experts),
                    bank[c][:, 0:CHUNK].rearrange("p (b e) -> p b e", e=experts),
                    before.rearrange("p (e b) -> p b e", b=B)[:, c * BC:(c + 1) * BC, :], ALU.add)
            link(ins)
            link(nc.vector.tensor_tensor(key, key, chosen, ALU.mult))
            for b in range(B):
                ins = nc.vector.max(best[:, b * 8:(b + 1) * 8], key[:, b * experts:(b + 1) * experts])
            link(ins)
            best3 = best.rearrange("p (b k) -> p b k", k=8)[:, :, 0:top_k]
            nc.vector.tensor_scalar(place.rearrange("p (b k) -> p b k", k=top_k), best3, 1.0, None, ALU.subtract) \
                .then_inc(placed.sem, 1)
            for c in range(COLS):
                link(nc.vector.tensor_scalar(total, ends, tile_id[:, c:c + 1], None, ALU.is_le))
                link(nc.vector.tensor_reduce(owner[:, c:c + 1], total, X, ALU.add))
            nc.vector.tensor_scalar(owner, owner, experts - 1.0, None, ALU.min).then_inc(owned.sem, 1)
            v.wait_ge(owner_row.sem, owner_row.at(0, 1))
            nc.vector.tensor_copy(table, bank[7][0:1, 0:COLS * P]).then_inc(tabled.sem, 1)
            if shared:
                with v.Fori(0, G) as g:
                    for u in range(U):
                        shared_hidden(g, u)
                        if u % tiles == tiles - 1 and u >= tiles:
                            add_shared(g, u // tiles - 1)
                    add_shared(g, shared - 1)
                v.wait_ge(xd.sem, xd.at(G, 0))
            for k in range(top_k):
                bc = best3[:, :, k:k + 1].to_broadcast([P, B, experts])
                k3 = lambda a_: a_.rearrange("p (b e) -> p b e", e=experts)
                link(nc.vector.tensor_tensor(k3(taken), k3(key), bc, ALU.is_equal))
                link(nc.vector.tensor_tensor(taken, taken, gates, ALU.mult))
                link(nc.vector.tensor_reduce(weight.rearrange("p (b k) -> p b k", k=top_k)[:, :, k], k3(taken),
                                             X, ALU.add))
            order.close()
            nc.vector.memset(router.pad, 0.0).then_inc(weighed.sem, 1)

            def hidden(g, u):
                v.wait_ge(gu.sem, gu.at(g, u + 1))
                v.wait_ge(si.sem, si.at(g, u + 1))
                v.wait_ge(ht.sem, ht.at(g, u - 1))
                _, upper, sg_ = unit_views(u, sgs[u % 2])
                _, _, out = unit_views(u, hs[u % 2])
                nc.vector.tensor_tensor(out, sg_, upper, ALU.mult).then_inc(hn.sem, 1)

            def step(g, u, first=False, last=False):
                v.wait_ge(ht.sem, ht.at(g, u + 1))
                v.wait_ge(dn.sem, dn.at(g, u - 1))
                nc.vector.tensor_copy(hTs[u % 2][0:rows], bank[6 + u % 2][0:rows, :]).then_inc(hc.sem, 1)
                if not (last and u == UNITS - 1):
                    hidden(g, u + 1)

            hidden(0, 0)
            run(v, step)

            with v.Fori(0, G) as g:
                c = Chain(v, mixing, g)
                for i in range(2):
                    v.wait_ge(ga[i].sem, ga[i].at(g, K2 * 16))
                    for k in range(top_k):
                        for b in range(2):
                            seq = g * GB + 2 * i + b
                            xs_ = x[:, ds(seq * P, P)]
                            n = b * top_k + k
                            ins = nc.vector.scalar_tensor_tensor(xs_, gathered[i][:, n * P:(n + 1) * P],
                                                                 weight[:, ds(seq * top_k + k, 1)], xs_,
                                                                 ALU.mult, ALU.add)
                        c.link(ins)
                    nc.vector.memset(router.pad, 0.0).then_inc(mixed.sem, 1)
                c.close()

        return dict(load=load, sp=sp, pool=pool, dve=dve, pe=pe, act=act), [(mixed.sem, mixed.at(G, 0))]

    return stage


BIAS_ROWS = {"a0_v": P, "a0_out": P, "ffn0": P, "a1_kv": 2 * P, "a1_off": 80, "a1_out": P, "router2": 8}
CONSTS = {"ident": P, "ones_row": P, "ones_row_cut": P, "head_mask": H, "neg_half": B,
          "dft_cos": P, "dft_sin": P, "dft_msin": P}


def build(nc, d, out, last_stage):
    with ExitStack() as ctx:
        core = Core(nc, ctx, d)
        core.x = core.sb("x", B * P)
        core.ctxT = core.sb("ctxT", B * P)
        core.xnT = core.sb("xnT", B * P)
        core.ln_stat, core.ln_moments = core.sb("ln_stat", 6 * B)[:, :], core.sb("ln_moments", 4 * B)
        core.ln_rstd, core.ln_xn = core.sb("ln_rstd", B)[:, :], core.sb("ln_xn", GT)
        consts = core.sb("consts", sum(CONSTS.values()))
        at = 0
        for name, n in CONSTS.items():
            core.const[name] = consts[:, at:at + n]
            at += n
        core.held = core.sem("held")
        core.ident, core.ones_row = core.const["ident"], core.const["ones_row"]
        core.head_mask, core.neg_half = core.const["head_mask"], core.const["neg_half"]
        bias = core.sb("bias_rows", sum(BIAS_ROWS.values()))
        core.bias, at = {}, 0
        for name, n in BIAS_ROWS.items():
            core.bias[name] = bias[:, at:at + n]
            at += n
        cb = core.sb("consts_bf16", 3 * P + H * P, BF16)
        core.bias_all, core.bf16_all = bias[:, :], cb[:, :]
        core.ident_b, core.sel_head = cb[:, 0:P], cb[:, P:P + H * P]
        core.earlier_b, core.ones_b = cb[:, P + H * P:2 * P + H * P], cb[:, 2 * P + H * P:3 * P + H * P]
        core.sorted_x = nc.dram_tensor("sorted_x", (SORTED_TILES * P, P), F32, kind="Internal").ap()

        WORDS = 35 * 1024
        area = core.sb("scratch", WORDS)

        loaded, stored = core.sem("loaded"), core.sem("stored")
        FILL = 16 * P
        zeros, zeroed, filled = area[:, WORDS - 2 * FILL:WORDS - FILL], core.sem("zeroed"), core.sem("filled")
        FILLS = SORTED_TILES * P // FILL
        start = [(loaded, 2 * 16)]
        stages, starts = [], []
        for make in STAGES[:last_stage]:
            starts.append(start)
            programs, start = make(core, Arena(area, WORDS, len(stages) % 2), start)
            if len(stages) == 1:
                start = start + [(filled, FILLS * 16)]
            stages.append(programs)

        block = ctx.enter_context(nc.Block())

        @block.sync
        def _(s):
            for sig in core.credits:
                s.sem_inc(sig.sem, sig.credit)
            s.dma_start(core.x[:, :], d["x"]).then_inc(loaded, 16)
            s.dma_start(consts[:, :], d["consts"]).then_inc(loaded, 16)
            stages[0]["load"](s)
            s.wait_ge(zeroed, 1)
            with s.Fori(0, FILLS) as f:
                s.dma_start(core.sorted_x.rearrange("(f p r) d -> f p (r d)", p=P, r=FILL // P)
                            [ds(f, 1)].rearrange("o p w -> (o p) w"), zeros).then_inc(filled, 16)
            for i, st in enumerate(stages):
                if i + 1 < len(stages):
                    for sem, n in starts[i]:
                        s.wait_ge(sem, n)
                    stages[i + 1]["load"](s)
                if "sp" in st:
                    st["sp"](s)
            for sem, n in start:
                s.wait_ge(sem, n)
            s.dma_start(out, core.x[:, :]).then_inc(stored, 16)
            s.wait_ge(stored, 16)

        @block.tensor
        def _(t):
            for st in stages:
                st["pe"](t)

        @block.scalar
        def _(a):
            for st in stages:
                st["act"](a)

        @block.vector
        def _(v):
            for st in stages:
                st["dve"](v)

        @block.gpsimd
        def _(p):
            nc.gpsimd.memset(zeros, 0.0).then_inc(zeroed, 1)
            for st in stages:
                st["pool"](p)


def bf16_bits(a):
    return (np.ascontiguousarray(a, np.float32).view(np.uint32) >> 16).astype(np.uint16)


def shape_constants():
    k = np.arange(P)
    row0 = np.zeros((P, P), np.float32)
    row0[0] = 1.0
    cut = row0.copy()
    cut[0, P - 1] = 0.0
    angle = 2.0 * np.pi * ((k[:, None] * k[None, :]) % P) / P
    tables = {
        "ident": np.eye(P), "ones_row": row0, "ones_row_cut": cut,
        "head_mask": k[:, None] // (P // H) == np.arange(H)[None, :],
        "neg_half": np.full((P, B), -0.5),
        "dft_cos": np.cos(angle), "dft_sin": np.sin(angle), "dft_msin": -np.sin(angle),
    }
    f32 = np.concatenate([np.asarray(tables[n], np.float32) for n in CONSTS], axis=1)
    sel = np.zeros((P, H, P), np.float32)
    for h in range(H):
        sel[h, h] = sel[H + h, h] = 1.0
    earlier = (k[:, None] < k[None, :]).astype(np.float32)
    return f32, bf16_bits(np.concatenate([np.eye(P, dtype=np.float32), sel.reshape(P, H * P), earlier,
                                          np.ones((P, P), np.float32)], axis=1))


def place_selectors(pairs=40):
    row = np.arange(P, dtype=np.float32)
    sel = np.zeros((P, pairs, P), np.float32)
    for r in range(pairs):
        sel[r, r] = 2.0 * row
        sel[pairs + r, r] = sel[2 * pairs + r, r] = -1.0
    high = ((1.0 - row * row).view(np.uint32) & 0xFFFF0000).view(np.float32)
    sel[3 * pairs], sel[3 * pairs + 1] = high, 1.0 - row * row - high
    return bf16_bits(sel.reshape(P, pairs * P))


def lay_out(a):
    rows = np.zeros((P, sum(BIAS_ROWS.values())), np.float32)
    parts = {"a0_v": [a["L0_xattn_b_v"]], "a0_out": [a["L0_xattn_b_out"]], "ffn0": [a["L0_ffn_bias"]],
             "a1_kv": [a["L1_xattn_bk"], a["L1_xattn_bv"]], "a1_off": [a["L1_xattn_boff"]],
             "a1_out": [a["L1_xattn_bo"]], "router2": [a["L2_ffn_router_b"]]}
    rows[0] = np.concatenate([v for n in BIAS_ROWS for v in parts[n]])
    f32, bf = shape_constants()
    out = {"x": a["x"].transpose(1, 0, 2).reshape(P, -1), "ctx": a["ctx_1024"].transpose(1, 0, 2).reshape(P, -1),
           "ctxT": a["ctx_1024"].transpose(2, 0, 1).reshape(P, -1),
           "consts": f32, "consts_bf16": bf, "bias_rows": rows}
    out["a0_w"] = np.concatenate([a["L0_xattn_" + n].T for n in ("w_q", "w_k", "w_v", "w_out")], axis=1)
    out["a0_bqk"] = np.stack([a["L0_xattn_b_q"], a["L0_xattn_b_k"]], axis=1)
    out["f0_w"] = np.concatenate([a["L0_ffn_w_freq_real"], a["L0_ffn_w_freq_imag"]], axis=1)
    out["a1_w"] = np.concatenate([a["L1_xattn_" + n].T for n in ("Wq", "Woff", "Wk", "Wv", "Wo")], axis=1)
    out["a1_vecs"] = np.concatenate([a["L1_xattn_bq"][:, None], np.arange(P, dtype=np.float32)[:, None],
                                     np.tile(np.arange(-3, 2, dtype=np.float32), (P, H))], axis=1)
    out["a1_sel"] = place_selectors()
    out["a1_maskT"] = a["mask_BxS2_if0"].astype(np.int32).T
    out["a2_w"] = np.concatenate([a["L2_xattn_Wq"], a["L2_xattn_Wkv"],
                                  a["L2_xattn_Wout"].reshape(8, P, P).transpose(1, 0, 2).reshape(P, 8 * P)], axis=1)
    out["a2_ln"] = np.stack([a["L2_xattn_" + n] for n in ("ln1_w", "ln1_b", "ln2_w", "ln2_b")], axis=1)
    side = a["fside_Bx16_0"].reshape(B, 8, 2, 1)
    out["a2_shift"] = np.broadcast_to(side, (B, 8, 2, 64)).transpose(2, 3, 0, 1).reshape(P, B * 8)
    out["a3_w"] = np.concatenate([a["L3_xattn_Wq"].T, a["L3_xattn_Wk"].T], axis=1)
    out["a3_bqk"] = np.stack([a["L3_xattn_bq"], a["L3_xattn_bk"]], axis=1)
    reset = np.ones((P, GB, 64), np.float32)
    reset[:, :, 0] = 0.0
    out["reset64"] = reset.reshape(P, GB * 64)
    out["tile_id"] = (np.arange(3)[None, :] * P + np.arange(P)[:, None]).astype(np.float32)
    out["reset"] = np.tile(reset[:, 0, 0:8], (1, GB))
    w_up = np.concatenate([a["L1_ffn_w_up"], np.concatenate([a["L1_ffn_sg_gate"], a["L1_ffn_sg_up"]])[None]])
    w_down = np.concatenate([a["L1_ffn_w_down"], a["L1_ffn_sg_down"][None]])
    out["m1_up"] = w_up.transpose(2, 0, 1).reshape(P, -1)
    out["m1_down"] = w_down.transpose(2, 0, 1).reshape(2, 96, 9, P).transpose(1, 2, 0, 3).reshape(96, -1)
    out["m1_gate"] = a["L1_ffn_gate_w"].T
    out["m2_up"] = a["L2_ffn_w1"].transpose(1, 0, 2).reshape(P, -1)
    out["m2_down"] = a["L2_ffn_w2"].reshape(8, 4, P, P).transpose(2, 0, 1, 3).reshape(P, -1)
    out["m2_gate"] = a["L2_ffn_router_w"]
    gu = np.stack([np.concatenate([a["L3_ffn_Wg"], a["L3_ffn_Sg"].reshape(2, 88, P)]),
                   np.concatenate([a["L3_ffn_Wu"], a["L3_ffn_Su"].reshape(2, 88, P)])], axis=1)
    out["m3_up"] = gu.transpose(3, 0, 1, 2).reshape(P, -1)
    dn = np.concatenate([a["L3_ffn_Wd"], a["L3_ffn_Sd"].reshape(P, 2, 88).transpose(1, 0, 2)])
    out["m3_down"] = dn.transpose(2, 0, 1).reshape(88, -1)
    out["m3_gate"] = a["L3_ffn_gate_w"].T
    out["m3_bias"] = np.broadcast_to(a["L3_ffn_gate_bias"], (P, 64))
    return out


SORTED_TILES = 320

STAGES = [stage_attention0, stage_fourier_ffn, stage_attention1,
          stage_experts("m1", Top2Softmax, 8, 2, 1, 192, 96, 2), stage_attention2,
          stage_experts("m2", Top1Softmax, 8, 1, 0, 512, P, 2, "router2"), stage_attention3,
          stage_experts("m3", GroupedTop8, 64, 8, 2, 88, 88, 8)]


def kernel(**inputs):
    import numpy as _np
    import concourse.bacc as _bacc
    from concourse import mybir as _mybir
    from concourse.bass_utils import run_bass_kernel_spmd as _run

    nc = _bacc.Bacc("TRN2", target_bir_lowering=False, num_devices=1)
    arrays, aps = {}, {}
    for name, a in lay_out({k: _np.asarray(v) for k, v in inputs.items()}).items():
        arrays[f"in_{name}"] = _np.ascontiguousarray(a)
        aps[name] = nc.dram_tensor(f"in_{name}", a.shape, _mybir.dt.from_np(a.dtype), kind="ExternalInput").ap()
    out = nc.dram_tensor("out_0", (P, B * P), F32, kind="ExternalOutput").ap()
    build(nc, aps, out, LAST_STAGE)
    x = _run(nc, [arrays], core_ids=[0]).results[0]["out_0"]
    return _np.ascontiguousarray(x.reshape(P, B, P).transpose(1, 0, 2))
LAST_STAGE = 8
```
